# Optimizing a Trainium2 kernel written in Bass

```python
import numpy as np
import jax
import jax.numpy as jnp

def _softmax(x, axis=-1):
    return jax.nn.softmax(x, axis=axis)

def _gelu(x):
    return jax.nn.gelu(x, approximate=True)

def _silu(x):
    return jax.nn.silu(x)

def _sigmoid(x):
    return jax.nn.sigmoid(x)

def _layernorm(x, axis=-1, eps=1e-05):
    m = jnp.mean(x, axis=axis, keepdims=True)
    v = jnp.var(x, axis=axis, keepdims=True)
    return (x - m) / jnp.sqrt(v + eps)

def _scatter_add(tgt, idx, src, axis=0):
    return tgt.at[idx].add(src)

def _segment_sum(src, seg, n):
    return jax.ops.segment_sum(src, seg, n)
kernel_name = 'mk_decoder_postln_d1_seqx_r4_ef8fb2'

def setup_inputs(seed: int=0):
    np.random.seed(seed)
    _w = jnp.asarray

    def _rec_inputs():
        import jax
        import jax.numpy as jnp
        _rk = jax.random.key(seed)
        x = 0.002226 + 0.9996 * jax.random.normal(jax.random.fold_in(_rk, 1), (16, 256, 256), jnp.float32)
        _lenS = 256 - jax.random.randint(jax.random.fold_in(_rk, 7), (16,), 0, max(1, 256 // 4) + 1, jnp.int32)
        _lenS2 = 77 - jax.random.randint(jax.random.fold_in(_rk, 8), (16,), 0, max(1, 77 // 4) + 1, jnp.int32)
        _ctx_1024P = jax.random.normal(jax.random.fold_in(_rk, 11), (16, 16, 256), jnp.float32)
        _ctx_1024c = jax.random.dirichlet(jax.random.fold_in(_rk, 511), 0.3 * jnp.ones((16,), jnp.float32), (16, 77))
        _ctx_1024t = jnp.einsum('bsk,bkd->bsd', _ctx_1024c, _ctx_1024P)
        _ctx_1024t = _ctx_1024t * jax.lax.rsqrt(jnp.mean(jnp.square(_ctx_1024t)) + 1e-12) * 0.953939
        ctx_1024 = -0.000125008 + 0.999885 * (_ctx_1024t + 0.3 * jax.random.normal(jax.random.fold_in(_rk, 611), (16, 77, 256), jnp.float32))
        return (x, ctx_1024)
    x, ctx_1024 = _rec_inputs()

    def _L0_attn_setup():
        import jax, jax.numpy as jnp
        import numpy as np
        D_STATE = 16
        D_CONV = 4

        def silu(x):
            return x * jax.nn.sigmoid(x)

        def _reference_tuple_inner(x, in_w, in_b, conv_w, conv_b, xp_w, xp_b, out_w, out_b):
            B, S, D = x.shape
            h = x @ in_w.T + in_b
            hc = jax.lax.conv_general_dilated(h.transpose(0, 2, 1), conv_w, window_strides=(1,), padding=[(D_CONV - 1, 0)], feature_group_count=conv_w.shape[0], dimension_numbers=('NCH', 'OIH', 'NCH')) + conv_b[None, :, None]
            h = silu(hc.transpose(0, 2, 1))
            xp = h @ xp_w.T + xp_b
            a = jnp.exp(-jnp.exp(xp[..., :D_STATE]))
            b = silu(xp[..., D_STATE:]) * jnp.sum(h, axis=-1, keepdims=True)

            def step(state, ab):
                a_t, b_t = ab
                state = state * a_t + b_t
                return (state, state)
            init = jnp.zeros((B, D_STATE), x.dtype)
            final_state, ys = jax.lax.scan(step, init, (a.transpose(1, 0, 2), b.transpose(1, 0, 2)))
            out = ys.transpose(1, 0, 2) @ out_w.T + out_b
            return (out, final_state)
        key = jax.random.key(seed)
        ks = jax.random.split(key, 9)
        B, S, D = (8, 1024, 256)
        DI = 2 * D

        def w(k, shape, fan_in):
            bound = 1.0 / np.sqrt(fan_in)
            return jax.random.uniform(k, shape, jnp.float32, -bound, bound)
        return {'x': jax.random.normal(ks[0], (B, S, D), jnp.float32), 'in_w': w(ks[1], (DI, D), D), 'in_b': w(ks[2], (DI,), D), 'conv_w': w(ks[3], (DI, 1, D_CONV), D_CONV), 'conv_b': w(ks[4], (DI,), D_CONV), 'xp_w': w(ks[5], (2 * D_STATE, DI), DI), 'xp_b': w(ks[6], (2 * D_STATE,), DI), 'out_w': w(ks[7], (D, D_STATE), D_STATE), 'out_b': w(ks[8], (D,), D_STATE)}
    _L0_attn_all = _L0_attn_setup()
    _L0_attn_in = {k: v for k, v in _L0_attn_all.items() if k in ('in_w', 'in_b', 'conv_w', 'conv_b', 'xp_w', 'xp_b', 'out_w', 'out_b')}
    del _L0_attn_all

    def _L0_xattn_setup():
        import jax, jax.numpy as jnp
        import numpy as np
        B, M, N, DIM, DH, H = (8, 1024, 64, 256, 128, 8)
        INNER = DH * H
        EPS = 1e-05

        def _layernorm(x, g, b):
            mu = jnp.mean(x, axis=-1, keepdims=True)
            var = jnp.var(x, axis=-1, keepdims=True)
            return (x - mu) * jax.lax.rsqrt(var + EPS) * g + b
        key = jax.random.key(seed)
        ks = jax.random.split(key, 8)
        sd = 0.02
        return {'x': jax.random.normal(ks[0], (B, M, DIM), jnp.float32), 'latents': jax.random.normal(ks[1], (B, N, DIM), jnp.float32), 'gamma_media': jnp.ones((DIM,), jnp.float32), 'beta_media': jnp.zeros((DIM,), jnp.float32), 'gamma_lat': jnp.ones((DIM,), jnp.float32), 'beta_lat': jnp.zeros((DIM,), jnp.float32), 'Wq': jax.random.normal(ks[2], (DIM, INNER), jnp.float32) * sd, 'bq': jnp.zeros((INNER,), jnp.float32), 'Wkv': jax.random.normal(ks[3], (DIM, 2 * INNER), jnp.float32) * sd, 'bkv': jnp.zeros((2 * INNER,), jnp.float32), 'Wo': jax.random.normal(ks[4], (INNER, DIM), jnp.float32) * sd, 'bo': jnp.zeros((DIM,), jnp.float32)}
    _L0_xattn_all = _L0_xattn_setup()
    _L0_xattn_in = {k: v for k, v in _L0_xattn_all.items() if k in ('gamma_media', 'beta_media', 'gamma_lat', 'beta_lat', 'Wq', 'bq', 'Wkv', 'bkv', 'Wo', 'bo')}
    del _L0_xattn_all

    def _L0_ffn_setup():
        import jax, jax.numpy as jnp
        import numpy as np
        import math
        B, S, H = (8, 1024, 256)
        E, I, K = (8, 512, 2)
        CAP_FACTOR = 1.0

        def _router(x, expert_embeddings):
            dot = jnp.einsum('bsh,eh->bse', x, expert_embeddings)
            n = dot.shape[0] * dot.shape[1]
            dot2 = dot.reshape(n, E)
            vals, idx = jax.lax.top_k(dot2, K)
            rows = jnp.arange(n)[:, None]
            masked = jnp.full_like(dot2, -jnp.inf).at[rows, idx].set(vals)
            return jax.nn.softmax(masked, axis=-1)
        key = jax.random.key(seed)
        k1, k2, k3, k4 = jax.random.split(key, 4)

        def kaiming(k, shape):
            bound = math.sqrt(3.0 / shape[-1])
            return jax.random.uniform(k, shape, jnp.float32, -bound, bound)
        x = jax.random.normal(k1, (B, S, H), jnp.float32)
        expert_embeddings = kaiming(k2, (E, H))
        first_linear = kaiming(k3, (E, I, H))
        second_linear = kaiming(k4, (E, H, I))
        return {'x': x, 'expert_embeddings': expert_embeddings, 'first_linear': first_linear, 'second_linear': second_linear}
    _L0_ffn_all = _L0_ffn_setup()
    _L0_ffn_in = {k: v for k, v in _L0_ffn_all.items() if k in ('expert_embeddings', 'first_linear', 'second_linear')}
    del _L0_ffn_all
    return {'x': x, 'ctx_1024': ctx_1024, 'L0_attn_in_w': _L0_attn_in['in_w'], 'L0_attn_in_b': _L0_attn_in['in_b'], 'L0_attn_conv_w': _L0_attn_in['conv_w'], 'L0_attn_conv_b': _L0_attn_in['conv_b'], 'L0_attn_xp_w': _L0_attn_in['xp_w'], 'L0_attn_xp_b': _L0_attn_in['xp_b'], 'L0_attn_out_w': _L0_attn_in['out_w'], 'L0_attn_out_b': _L0_attn_in['out_b'], 'L0_xattn_gamma_media': _L0_xattn_in['gamma_media'], 'L0_xattn_beta_media': _L0_xattn_in['beta_media'], 'L0_xattn_gamma_lat': _L0_xattn_in['gamma_lat'], 'L0_xattn_beta_lat': _L0_xattn_in['beta_lat'], 'L0_xattn_Wq': _L0_xattn_in['Wq'], 'L0_xattn_bq': _L0_xattn_in['bq'], 'L0_xattn_Wkv': _L0_xattn_in['Wkv'], 'L0_xattn_bkv': _L0_xattn_in['bkv'], 'L0_xattn_Wo': _L0_xattn_in['Wo'], 'L0_xattn_bo': _L0_xattn_in['bo'], 'L0_ffn_expert_embeddings': _L0_ffn_in['expert_embeddings'], 'L0_ffn_first_linear': _L0_ffn_in['first_linear'], 'L0_ffn_second_linear': _L0_ffn_in['second_linear']}

def reference(x, ctx_1024, L0_attn_in_w, L0_attn_in_b, L0_attn_conv_w, L0_attn_conv_b, L0_attn_xp_w, L0_attn_xp_b, L0_attn_out_w, L0_attn_out_b, L0_xattn_gamma_media, L0_xattn_beta_media, L0_xattn_gamma_lat, L0_xattn_beta_lat, L0_xattn_Wq, L0_xattn_bq, L0_xattn_Wkv, L0_xattn_bkv, L0_xattn_Wo, L0_xattn_bo, L0_ffn_expert_embeddings, L0_ffn_first_linear, L0_ffn_second_linear):
    import jax
    import jax.numpy as jnp

    def _L0_attn_ref(x, in_w, in_b, conv_w, conv_b, xp_w, xp_b, out_w, out_b):
        import jax, jax.numpy as jnp
        import numpy as np
        D_STATE = 16
        D_CONV = 4

        def silu(x):
            return x * jax.nn.sigmoid(x)

        def _reference_tuple_inner(x, in_w, in_b, conv_w, conv_b, xp_w, xp_b, out_w, out_b):
            B, S, D = x.shape
            h = x @ in_w.T + in_b
            hc = jax.lax.conv_general_dilated(h.transpose(0, 2, 1), conv_w, window_strides=(1,), padding=[(D_CONV - 1, 0)], feature_group_count=conv_w.shape[0], dimension_numbers=('NCH', 'OIH', 'NCH')) + conv_b[None, :, None]
            h = silu(hc.transpose(0, 2, 1))
            xp = h @ xp_w.T + xp_b
            a = jnp.exp(-jnp.exp(xp[..., :D_STATE]))
            b = silu(xp[..., D_STATE:]) * jnp.sum(h, axis=-1, keepdims=True)

            def step(state, ab):
                a_t, b_t = ab
                state = state * a_t + b_t
                return (state, state)
            init = jnp.zeros((B, D_STATE), x.dtype)
            final_state, ys = jax.lax.scan(step, init, (a.transpose(1, 0, 2), b.transpose(1, 0, 2)))
            out = ys.transpose(1, 0, 2) @ out_w.T + out_b
            return (out, final_state)
        return _reference_tuple_inner(x, in_w, in_b, conv_w, conv_b, xp_w, xp_b, out_w, out_b)[0]

    def _L0_xattn_ref(x, latents, gamma_media, beta_media, gamma_lat, beta_lat, Wq, bq, Wkv, bkv, Wo, bo):
        import jax, jax.numpy as jnp
        import numpy as np
        B, M, N, DIM, DH, H = (8, 1024, 64, 256, 128, 8)
        INNER = DH * H
        EPS = 1e-05

        def _layernorm(x, g, b):
            mu = jnp.mean(x, axis=-1, keepdims=True)
            var = jnp.var(x, axis=-1, keepdims=True)
            return (x - mu) * jax.lax.rsqrt(var + EPS) * g + b
        b = x.shape[0]
        xn = _layernorm(x, gamma_media, beta_media)
        ln = _layernorm(latents, gamma_lat, beta_lat)
        q = ln @ Wq + bq
        kv_input = jnp.concatenate([xn, ln], axis=1)
        kv = kv_input @ Wkv + bkv
        k, v = jnp.split(kv, 2, axis=-1)

        def to_heads(t):
            return t.reshape(b, t.shape[1], H, DH).transpose(0, 2, 1, 3)
        q, k, v = (to_heads(q), to_heads(k), to_heads(v))
        q = q * DH ** (-0.5)
        sim = jnp.einsum('bhid,bhjd->bhij', q, k)
        attn = jax.nn.softmax(sim, axis=-1)
        out = jnp.einsum('bhij,bhjd->bhid', attn, v)
        out = out.transpose(0, 2, 1, 3).reshape(b, -1, INNER)
        return out @ Wo + bo

    def _L0_ffn_ref(x, expert_embeddings, first_linear, second_linear):
        import jax, jax.numpy as jnp
        import numpy as np
        import math
        B, S, H = (8, 1024, 256)
        E, I, K = (8, 512, 2)
        CAP_FACTOR = 1.0

        def _router(x, expert_embeddings):
            dot = jnp.einsum('bsh,eh->bse', x, expert_embeddings)
            n = dot.shape[0] * dot.shape[1]
            dot2 = dot.reshape(n, E)
            vals, idx = jax.lax.top_k(dot2, K)
            rows = jnp.arange(n)[:, None]
            masked = jnp.full_like(dot2, -jnp.inf).at[rows, idx].set(vals)
            return jax.nn.softmax(masked, axis=-1)
        batch, seq, hidden = x.shape
        n_tokens = batch * seq
        expert_capacity = math.ceil(n_tokens / E * CAP_FACTOR)
        weights = _router(x, expert_embeddings)
        ones = (weights > 0).astype(weights.dtype)
        cap_ones = jnp.where(jnp.cumsum(ones, axis=0) <= expert_capacity, ones, 0.0)
        caw = weights * cap_ones
        vals, idx = jax.lax.top_k(caw.T, expert_capacity)
        index = idx.reshape(-1)
        x_flat = x.reshape(n_tokens, hidden)
        tokens = x_flat[index].reshape(E, expert_capacity, hidden)
        inter = jax.nn.relu(jnp.einsum('ech,eih->eci', tokens, first_linear))
        out = jnp.einsum('eci,ehi->ech', inter, second_linear)
        out = out * vals[:, :, None]
        final = jnp.zeros((n_tokens, hidden), x.dtype).at[index].add(out.reshape(-1, hidden))
        return final.reshape(x.shape)
    x = _layernorm(x + _L0_attn_ref(x, L0_attn_in_w, L0_attn_in_b, L0_attn_conv_w, L0_attn_conv_b, L0_attn_xp_w, L0_attn_xp_b, L0_attn_out_w, L0_attn_out_b), axis=-1)
    x = _layernorm(x + _L0_xattn_ref(ctx_1024, x, L0_xattn_gamma_media, L0_xattn_beta_media, L0_xattn_gamma_lat, L0_xattn_beta_lat, L0_xattn_Wq, L0_xattn_bq, L0_xattn_Wkv, L0_xattn_bkv, L0_xattn_Wo, L0_xattn_bo), axis=-1)
    x = _layernorm(x + _L0_ffn_ref(x, L0_ffn_expert_embeddings, L0_ffn_first_linear, L0_ffn_second_linear), axis=-1)
    return x

_drawn_inputs = setup_inputs


def setup_inputs(seed=0):
    import zlib

    import numpy as np

    out = dict(_drawn_inputs(seed))
    spreads = {'L0_xattn_gamma_media': (1.0, 0.6),
     'L0_xattn_beta_media': (0.0, 0.517),
     'L0_xattn_gamma_lat': (1.0, 0.2),
     'L0_xattn_beta_lat': (0.0, 0.1),
     'L0_xattn_bq': (0.0, 0.667),
     'L0_xattn_bkv': (0.0, 0.1),
     'L0_xattn_bo': (0.0, 0.1)}
    factors = {'L0_xattn_Wq': 3.037}
    for name, (base, spread) in spreads.items():
        noise = np.random.default_rng([zlib.crc32(name.encode()), seed]).standard_normal(out[name].shape)
        drawn = base * np.exp(spread * noise) if base else spread * noise
        out[name] = jnp.asarray(drawn.astype(out[name].dtype))
    for name, factor in factors.items():
        out[name] = (out[name] * factor).astype(out[name].dtype)
    return out
```

```python
from contextlib import ExitStack

import concourse.bass as bass
from concourse import mybir

ACT = mybir.ActivationFunctionType
ALU = mybir.AluOpType
AX = mybir.AxisListType
F32 = mybir.dt.float32
F32R = mybir.dt.float32r
BF16 = mybir.dt.bfloat16
U32 = mybir.dt.uint32

H = 8
E = 8
NC = 77
NK = 333
NP = 334
ROW = 272
EPS = 1e-5
FAR = 65536.0

C_INB, C_CB, C_CW, C_XPB, C_BQ, C_BKV, C_GM, C_BM, C_GL, C_BL, C_E = 0, 4, 8, 24, 25, 33, 49, 51, 53, 55, 57
C_END = 73
K_ID, K_TRI, K_IOTA, K_BASE, K_TOK, K_DUMP = 0, 128, 256, 272, 288, 290
K_END = 294


class Program:

    PIPE = 180.0

    def __init__(self, nc, sem):
        self.nc = nc
        self.sem = sem
        self.ops = {}
        self.turns = {}

    def op(self, engine, name, waits, cost, rank, issue):
        assert name not in self.ops, name
        self.ops[name] = dict(engine=engine, name=name, waits=list(waits), cost=cost, rank=rank,
                              issue=issue, slot=None, late=0.0)

    def dma(self, engine, name, waits, slot, rank, issue, cost=60.0, late=2500.0):
        self.op(engine, name, waits, cost, rank, issue)
        self.ops[name].update(slot=slot, late=late)

    def order(self):
        for o in self.ops.values():
            o["waits"] = [w for w in o["waits"] if w is not None]
            for w in o["waits"]:
                assert w in self.ops, (o["name"], w)
        left = {n: len(set(o["waits"])) for n, o in self.ops.items()}
        after = {}
        for n, o in self.ops.items():
            for w in set(o["waits"]):
                after.setdefault(w, []).append(n)
        ready, end = {}, {}
        engines = sorted({o["engine"] for o in self.ops.values()})
        cand = {g: [] for g in engines}
        free = {g: 0.0 for g in engines}
        queue = {g: [] for g in engines}
        for n, o in self.ops.items():
            if not left[n]:
                ready[n] = 0.0
                cand[o["engine"]].append(n)
        todo = len(self.ops)
        while todo:
            best = None
            for g in engines:
                if cand[g]:
                    s = max(free[g], min(ready[n] for n in cand[g]))
                    if best is None or s < best[0]:
                        best = (s, g)
            assert best is not None, [n for n in left if left[n]][:20]
            s, g = best
            n = min((n for n in cand[g] if ready[n] <= s), key=lambda n: (self.ops[n]["rank"], ready[n]))
            cand[g].remove(n)
            o = self.ops[n]
            free[g] = s + o["cost"]
            end[n] = free[g] + o["late"]
            queue[g].append(o)
            todo -= 1
            for m in after.get(n, ()):
                left[m] -= 1
                if not left[m]:
                    ready[m] = max(end[w] + self.PIPE for w in self.ops[m]["waits"])
                    cand[self.ops[m]["engine"]].append(m)
        self.planned = max(end.values())
        return queue

    def emit(self):
        queue = self.order()
        wanted = {w for o in self.ops.values() for w in o["waits"]}
        count, mark = {}, {}
        for g, ops in queue.items():
            for o in ops:
                if o["slot"]:
                    count[o["slot"]] = count.get(o["slot"], 0) + 16
                    mark[o["name"]] = (o["slot"], count[o["slot"]])
                elif o["name"] in wanted:
                    count[g] = count.get(g, 0) + 1
                    mark[o["name"]] = (g, count[g])
        sems = {s: self.sem("s_" + s) for s in count}

        def run(g):
            def body(eng):
                seen = {}
                for o in queue.get(g, ()):
                    need = {}
                    for w in o["waits"]:
                        s, v = mark[w]
                        need[s] = max(v, need.get(s, 0))
                    for s, v in need.items():
                        if seen.get(s, 0) < v:
                            eng.wait_ge(sems[s], v)
                            seen[s] = v
                    last = o["issue"](eng)
                    if o["name"] in mark:
                        last.then_inc(sems[mark[o["name"]][0]], 16 if o["slot"] else 1)
            return body

        with self.nc.Block() as block:
            block.sync(run("sync"))
            block.tensor(run("tensor"))
            block.scalar(run("scalar"))
            block.vector(run("vector"))
            block.gpsimd(run("gpsimd"))


def decoder_layer(nc, x, xT, ctx_in, cols, consts, in_w, xp_w, out_w, Wq, Wkv, Wo, bo, w1, w2, out):
    NT = x.shape[0]
    NB = NT // 256
    CAP = NT // E
    CT = CAP // 128
    NI = NB * H
    SCALE = 128.0 ** -0.5

    xs = nc.dram_tensor("xs", [NT, ROW], F32, kind="Internal").ap()
    acc = nc.dram_tensor("acc", [NT + CAP, 256], F32, kind="Internal").ap()

    es = ExitStack()
    with es:
        sem = lambda name: es.enter_context(nc.semaphore(name))
        P = Program(nc, sem)
        op, dma = P.op, P.dma

        class Arena:
            def __init__(self, name, size, dt):
                self.t = es.enter_context(nc.sbuf_tensor(name, [128, size], dt))
                self.size, self.at = size, 0

            def take(self, *shape, at=None):
                n = 1
                for d in shape:
                    n *= d
                if at is None:
                    at = self.at
                    self.at += n
                    assert self.at <= self.size, (self.at, self.size)
                v = self.t[:, at:at + n]
                if len(shape) == 2:
                    v = v.rearrange("p (a b) -> p a b", a=shape[0])
                if len(shape) == 3:
                    v = v.rearrange("p (a b c) -> p a b c", a=shape[0], b=shape[1])
                return v

        R = Arena("R", 33850, F32R)
        F = Arena("F", 16400, F32)

        WQ = [R.take(2, 1024) for _ in range(2)]
        r_wkv = R.at
        WKV = [R.take(2, 2048) for _ in range(2)]
        WO = [R.take(8, 256) for _ in range(2)]
        r_s1 = R.at
        INW = [R.take(2, 512) for _ in range(2)]
        XPW = [R.take(4, 80) for _ in range(2)]
        OW = [R.take(256) for _ in range(2)]
        XS = [R.take(2, 256) for _ in range(2)]
        GS = [R.take(4, 256) for _ in range(2)]
        YS = [R.take(256) for _ in range(2)]
        KV = [[R.take(2, NP) for _ in range(2)] for _ in range(2)]
        QS = [[R.take(256) for _ in range(2)] for _ in range(2)]
        KS = [[R.take(NP) for _ in range(2)] for _ in range(2)]
        VS = [[R.take(3, 256) for _ in range(2)] for _ in range(2)]
        PTS = [R.take(768) for _ in range(2)]
        OS = [[R.take(256) for _ in range(2)] for _ in range(2)]
        FW1 = [[R.take(2, 512, at=b + 1024 * k) for k in range(2)] for b in (r_s1, r_wkv)]
        FW2 = [[R.take(4, 256, at=b + 2048 + 1024 * k) for k in range(2)] for b in (r_s1, r_wkv)]
        FX = [[R.take(2, CAP, at=r_wkv + 4096 + 2048 * s + 2 * CAP * k) for k in range(2)] for s in range(2)]
        FI = [R.take(4, CAP, at=4 * CAP * k) for k in range(2)]

        CO = F.take(C_END)
        KO = F.take(K_END)
        BQS = F.take(H)
        HXB = F.take(1)
        MH = F.take(2)
        RUN = F.take(E)
        BO = F.take(256)
        f_s1 = F.at
        XTR = [F.take(2, 256) for _ in range(2)]
        XR = [F.take(2, 256) for _ in range(2)]
        HP = F.take(4, 259)
        Z = F.take(4, 256)
        ZP = F.take(256)
        TH = F.take(4, 256)
        EA, A, TB, ZB, BB, YF = [F.take(256) for _ in range(6)]
        Y1 = F.take(2, 256)
        X1 = F.take(2, 256)
        Z1 = F.take(2, 256)
        LT = F.take(2, 256)
        CR = F.take(256)
        CZ = F.take(256)
        CTX = F.take(2, NC)
        X1B = [F.take(2, 256) for _ in range(3)]
        PM = [F.take(2, NP) for _ in range(2)]
        X2E = [F.take(2, ROW) for _ in range(2)]
        f_y2 = F.at
        Y2 = F.take(2, 256)
        X2T = F.take(2, 256)
        LGT = F.take(256)
        LG = F.take(2, 8)
        M8 = F.take(2, 8)
        IF = F.take(2, 2)
        DW = F.take(2, 4)
        OH = F.take(2, 2, 8)
        V8 = F.take(2, 8)
        G8 = F.take(2, 8)
        PR = F.take(2, 2, 8)
        SL = F.take(2, 2)
        NM = F.take(2, 2)
        RS = F.take(2, 2)
        stats = {}
        for k in ("a", "b", "c", "d"):
            stats[k] = (F.take(2, 6), F.take(2, 2), F.take(2))
        tail_stats = (F.take(32, 6), F.take(32, 2), F.take(32), F.take(32))
        at_pm = PM[0]
        f_pm = f_y2 - 2 * 2 * ROW - 2 * 2 * NP
        STG = [F.take(1024, at=f_pm), F.take(1024, at=f_y2 - 4 * ROW - 1536 - 2 * 2 * NP)]
        INIT = F.take(CT, ROW, at=f_y2 - 4 * ROW)
        INIT_ALL = F.take(4 * ROW, at=f_y2 - 4 * ROW)
        XSL = [F.take(CT, ROW, at=f_s1 + 5400 + CT * ROW * s) for s in range(2)]
        YO = [F.take(CT, 256, at=f_s1 + 5400 + 2 * 1088 + CT * 256 * s) for s in range(2)]
        RW1 = [F.take(2, 512, at=f_s1 + 2048 * s) for s in range(2)]
        RW2 = [F.take(4, 256, at=f_s1 + 2048 * s + 1024) for s in range(2)]
        NCH = NT // 512
        AC = [F.take(4, 256, at=f_s1 + 1024 * s) for s in range(NCH)]
        assert f_s1 + 5400 + 2 * 1088 + 2 * 1024 <= f_y2 and f_s1 + 1024 * NCH <= f_y2

        I8 = es.enter_context(nc.sbuf_tensor("I8", [128, 2, 8], U32))
        IX = es.enter_context(nc.sbuf_tensor("IX", [128, 2, 4], U32))
        IE = es.enter_context(nc.sbuf_tensor("IE", [128, 2, 4], U32))
        TRI = es.enter_context(nc.sbuf_tensor("TRI", [128, 128], BF16))
        ONE = es.enter_context(nc.sbuf_tensor("ONE", [128, 128], BF16))
        OHB = es.enter_context(nc.sbuf_tensor("OHB", [128, 2, 8], BF16))

        PS = es.enter_context(nc.psum_tensor("PS", [128, 8 * 512], F32))
        bank = lambda k: PS[:, 512 * k:512 * (k + 1)]
        SA = [bank(0), bank(1)]
        PT = PS[:, 1024:1024 + 768]
        PO = PS[:, 1024 + 768:2048]
        PW = bank(4)
        D0, D1, D2 = bank(5), bank(6), bank(7)

        ident = KO[:, K_ID:K_ID + 128]
        pre = lambda i, name, *a: name.format(*a) if i >= 0 else None

        tc = lambda n: 65 + 1.04 * n
        ac = lambda n: 150 + 0.833 * n
        pc = lambda n: 150 + 2.1 * n

        def hi_lo(tag, raw, hi, lo, n, waits, rank, scale=1.0, free=(), lo_on="vector", rows=slice(0, 128)):
            op("scalar", tag + ".h", [*waits, *free], ac(n), rank,
               lambda e: e.activation(hi, raw, ACT.Copy, scale=scale))
            if lo_on == "gpsimd":
                op("gpsimd", tag + ".l", [tag + ".h", *waits, *free], pc(n), rank,
                   lambda e: e.tensor_tensor(lo, raw, hi.bitcast(F32), ALU.subtract))
                return
            op("vector", tag + ".l", [tag + ".h", *waits, *free], tc(n), rank,
               lambda e: e.scalar_tensor_tensor(lo, raw, scale, hi.bitcast(F32), ALU.mult, ALU.subtract))

        def split3(e, dst, w, xr, first, last):
            for n, (i, j) in enumerate(((0, 0), (0, 1), (1, 0))):
                r = e.matmul(dst, w[i], xr[j], start=first and n == 0, stop=last and n == 2,
                             skip_group_check=True)
            return r


        dma("sync", "ld.cols", [], "ld.cols", -90, lambda e: e.dma_start(CO, cols))
        dma("sync", "ld.consts", [], "ld.consts", -80, lambda e: e.dma_start(KO, consts))
        dma("sync", "ld.bo", [], "ld.bo", -50, lambda e: e.dma_start(BO, bo.partition_broadcast(128)))

        raw_in = [
            ("inw", in_w, lambda W: W, INW, 1.0, 2, -100),
            ("wq0", Wq[:, :, 0:512], lambda W: W[:, :, 0:512], WQ, SCALE, 2, -60),
            ("wk0", Wkv[:, :, 0:512], lambda W: W[:, :, 0:512], WKV, 1.0, 2, -60),
            ("wv0", Wkv[:, :, 1024:1536], lambda W: W[:, :, 1024:1536], WKV, 1.0, 2, -60),
            ("wo0", Wo[:, 0:4, :], lambda W: W[:, 0:4, :], WO, 1.0, 4, -50),
            ("wq1", Wq[:, :, 512:1024], lambda W: W[:, :, 512:1024], WQ, SCALE, 2, -50),
            ("wk1", Wkv[:, :, 512:1024], lambda W: W[:, :, 512:1024], WKV, 1.0, 2, -50),
            ("wv1", Wkv[:, :, 1536:2048], lambda W: W[:, :, 1536:2048], WKV, 1.0, 2, -50),
            ("wo1", Wo[:, 4:8, :], lambda W: W[:, 4:8, :], WO, 1.0, 4, -50),
        ]
        for n, (tag, src, view, W, scale, a, rank) in enumerate(raw_in):
            st = STG[n % 2].rearrange("p (a b) -> p a b", a=a)
            before = [raw_in[n - 2][0] + ".l"] if n >= 2 else []
            dma("sync", "ld." + tag, before, f"ld.stg{n % 2}", rank,
                lambda e, st=st, src=src: e.dma_start(st, src))
            hi_lo(tag, st, view(W[0]), view(W[1]), 1024, ["ld." + tag], rank, scale)
        STG_FREE = [raw_in[-1][0] + ".l", raw_in[-2][0] + ".l"]

        XPR = F.take(4, 32, at=f_y2)
        OWR = F.take(256, at=f_y2 + 128)
        dma("sync", "ld.xpw", [], "ld.xpw", -85, lambda e: e.dma_start(XPR, xp_w))
        dma("sync", "ld.ow", [], "ld.ow", -70, lambda e: e.dma_start(OWR[0:17, :], out_w))
        for k in range(2):
            op("gpsimd", f"xpw.z{k}", [], 400, -90,
               lambda e, k=k: e.memset(XPW[k][:, :, 0:64].bitcast(F32), 0.0))
            op("gpsimd", f"xpw.s{k}", [], 200, -90,
               lambda e, k=k: e.memset(XPW[k][:, :, 64:80].bitcast(F32), 0.25 * (1 - k)))
            op("gpsimd", f"ow.z{k}", [], 300, -70, lambda e, k=k: e.memset(OW[k].bitcast(F32), 0.0))
            op("gpsimd", f"ys.z{k}", [], 300, -70,
               lambda e, k=k: e.memset(YS[k].bitcast(F32), 1.0 - k))
            for s in range(2):
                op("gpsimd", f"kv.z{k}{s}", [], 100, -50,
                   lambda e, k=k, s=s: e.memset(KV[s][k][:, :, NK:NP].bitcast(F32), 0.0))
        for g in range(2):
            hi_lo(f"xpw{g}", XPR[:, :, 16 * g:16 * g + 16], XPW[0][:, :, 32 * g:32 * g + 16],
                  XPW[1][:, :, 32 * g:32 * g + 16], 64, ["ld.xpw", "xpw.z0", "xpw.z1"], -80, 0.5)
        hi_lo("ow", OWR[0:17, :], OW[0][0:17, :], OW[1][0:17, :], 256, ["ld.ow", "ow.z0", "ow.z1"], -60)
        XPW_OK = ["xpw0.l", "xpw1.l", "xpw.s0", "xpw.s1"]
        OW_OK = ["ow.l", "ys.z0", "ys.z1"]

        op("gpsimd", "hp.z", [], 100, -95, lambda e: e.memset(HP[:, :, 0:3], 0.0))
        op("gpsimd", "mh", [], 100, -90, lambda e: e.memset(MH, -0.5))
        op("gpsimd", "run.z", [], 100, -50, lambda e: e.memset(RUN, 0.0))
        op("gpsimd", "init.z", [], 900, -30, lambda e: e.memset(INIT_ALL, 0.0))
        op("vector", "pt.z", [], 800, -60, lambda e: e.memset(PS[:, 1024:2048], 0.0))
        op("vector", "bqs", ["ld.cols"], 80, -50,
           lambda e: e.tensor_scalar(BQS, CO[:, C_BQ:C_BQ + H], SCALE, None, ALU.mult))
        op("vector", "hxb", ["ld.cols"], 80, -80,
           lambda e: e.tensor_scalar(HXB, CO[:, C_XPB:C_XPB + 1], 0.5, None, ALU.mult))
        op("vector", "tri", ["ld.consts"], 100, -40,
           lambda e: e.tensor_copy(TRI[:, :], KO[:, K_TRI:K_TRI + 128]))
        op("vector", "one", [], 100, -40, lambda e: e.memset(ONE[:, :], 1.0))
        op("vector", "init.id", ["init.z", "ld.consts"], 80, -30,
           lambda e: e.tensor_copy(INIT[:, :, 256:257], KO[:, K_DUMP:K_DUMP + CT].unsqueeze(2)))
        for n in range(E):
            dma("sync", f"init.{n}", ["init.id"], "init", -20,
                lambda e, n=n: e.dma_start(xs[n * CAP:(n + 1) * CAP, :].rearrange("(t p) n -> p t n", p=128), INIT))
        dma("sync", "init.acc", ["init.id"], "init", -20,
            lambda e: e.dma_start(acc[NT:NT + CAP, :].rearrange("(t p) n -> p t n", p=128), INIT[:, :, 0:256]))
        INIT_OK = "init.acc"


        def norm(tag, kind, src, dst, waits, rank, free=(), again=None, rows=128, tiles=2):
            st, mv, rs = stats[kind]
            r = slice(0, rows)
            ag = [again] if again else []
            for t in range(tiles):
                op("vector", f"{tag}.s{t}", [*waits, *ag], 345, rank,
                   lambda e, t=t: e.bn_stats(st[r, t, :], src(t)))
                op("vector", f"{tag}.m{t}", [f"{tag}.s{t}", *ag], 80, rank,
                   lambda e, t=t: e.bn_aggr(mv[r, t, :], st[r, t, :]))
            op("vector", f"{tag}.v", [f"{tag}.m{t}" for t in range(tiles)] + ag, 80, rank,
               lambda e: e.tensor_scalar(rs[r, 0:tiles], mv[r, 0:tiles, 1], EPS, None, ALU.add))
            op("gpsimd", f"{tag}.r", [f"{tag}.v", "mh"], 640, rank,
               lambda e: e.tensor_tensor(rs[r, 0:tiles], rs[r, 0:tiles], MH[r, 0:tiles], ALU.pow))
            for t in range(tiles):
                op("vector", f"{tag}.a{t}", [f"{tag}.r", *free], 330, rank,
                   lambda e, t=t: e.tensor_scalar(dst(t), src(t), mv[r, t, 0:1], rs[r, t:t + 1],
                                                  ALU.subtract, ALU.mult))
            return [f"{tag}.a{t}" for t in range(tiles)]


        d2_order, d2_end = [], {}

        def d2(name, ends):
            d2_end[name] = ends

        for k in range(-1, NB + 1):
            n, r = k + 1, k - 1
            if n < NB:
                d2_order += [f"cT{n}", f"in{n}.0", f"in{n}.1"]
            if r >= 0:
                d2_order += [f"rT{r}", f"lg{r}", f"lgT{r}"]
            if n < NB:
                d2_order += [f"xp{n}"]
            if r >= 0:
                d2_order += [f"cum{r}"]
            if n < NB:
                d2_order += [f"out{n}", f"zT{n}"]
        d2_place = {n: k for k, n in enumerate(d2_order)}

        def d2_turn(name):
            k = d2_place[name]
            return ("turn", d2_order[k - 1]) if k else None


        def stage1(b):
            s = b % 2
            rk = lambda f: 8 * (b - 1) - 4 + 8 * f
            p = b - 1
            tok = slice(256 * b, 256 * b + 256)
            dma("sync", f"ld.xt{b}", [pre(b - 2, "xl{}.l", b - 2)], f"ld.xt{s}", rk(-1) - 60,
                lambda e: e.dma_start(XTR[s], xT[:, tok].rearrange("(c p) n -> p c n", p=128)))
            dma("sync", f"ld.x{b}", [pre(b - 2, "y1{}", b - 2)], f"ld.x{s}", rk(-1) - 50,
                lambda e: e.dma_start(XR[s], x[tok, :].rearrange("(t p) n -> p t n", p=128)))
            hi_lo(f"xl{b}", XTR[s], XS[0], XS[1], 512, [f"ld.xt{b}"], rk(0), free=[pre(p, "in{}.1", p)],
                  lo_on="gpsimd")
            for j in range(2):
                def mm(e, j=j):
                    for m in (2 * j, 2 * j + 1):
                        for c in range(2):
                            w = [INW[k][:, c, 128 * m:128 * m + 128] for k in range(2)]
                            r = split3(e, D2[:, 256 * (m % 2):256 * (m % 2) + 256], w,
                                       [XS[k][:, c, :] for k in range(2)], m % 2 == 0 and c == 0, c == 1)
                    return r
                op("tensor", f"in{b}.{j}", [f"xl{b}.l", "inw.l", d2_turn(f"in{b}.{j}")], 1320, rk(0.1 + 0.1 * j), mm)
                d2(f"in{b}.{j}", [f"hp{b}.{2 * j}", f"hp{b}.{2 * j + 1}"])
                for m in (2 * j, 2 * j + 1):
                    op("scalar", f"hp{b}.{m}", [f"in{b}.{j}", "ld.cols", pre(p, "z{}.{}.3", p, m)], 420,
                       rk(0.1 + 0.1 * j),
                       lambda e, m=m: e.activation(HP[:, m, 3:259], D2[:, 256 * (m % 2):256 * (m % 2) + 256],
                                                   ACT.Identity, bias=CO[:, C_INB + m:C_INB + m + 1]))
                    cw = lambda k, m=m: CO[:, C_CW + 4 * m + k:C_CW + 4 * m + k + 1]
                    op("gpsimd", f"z{b}.{m}.0", [f"hp{b}.{m}", "hp.z", "ld.cols", pre(p, "g{}", p)], 460, rk(0.2),
                       lambda e, m=m, cw=cw: e.tensor_scalar(Z[:, m, :], HP[:, m, 3:259], cw(3),
                                                             CO[:, C_CB + m:C_CB + m + 1], ALU.mult, ALU.add))
                    for k in range(1, 4):
                        if m == 3:
                            op("gpsimd", f"zp{b}.{k}", [f"hp{b}.{m}", f"z{b}.3.{k - 1}"], 460, rk(0.2),
                               lambda e, m=m, k=k, cw=cw: e.tensor_scalar(ZP, HP[:, m, 3 - k:259 - k], cw(3 - k), 0.0,
                                                                          ALU.mult, ALU.add))
                            op("gpsimd", f"z{b}.{m}.{k}", [f"zp{b}.{k}"], 700, rk(0.2),
                               lambda e, m=m: e.tensor_tensor(Z[:, m, :], Z[:, m, :], ZP, ALU.add))
                            continue
                        op("vector", f"z{b}.{m}.{k}", [f"z{b}.{m}.{k - 1}"], 340, rk(0.2),
                           lambda e, m=m, k=k, cw=cw: e.scalar_tensor_tensor(
                               Z[:, m, :], HP[:, m, 3 - k:259 - k], cw(3 - k), Z[:, m, :], ALU.mult, ALU.add))
            op("scalar", f"th{b}", [f"z{b}.{m}.3" for m in range(4)] + [pre(p, "gs{}.l", p)], 1000, rk(0.4),
               lambda e: e.activation(TH, Z, ACT.Tanh, scale=0.5))
            op("vector", f"g{b}", [f"th{b}"], 1140, rk(0.4),
               lambda e: e.scalar_tensor_tensor(TH, TH, 1.0, Z, ALU.add, ALU.mult))
            hi_lo(f"gs{b}", TH, GS[0], GS[1], 1024, [f"g{b}"], rk(0.45), free=[pre(p, "xp{}", p)],
                  lo_on="gpsimd")

            def xp(e):
                for m in range(4):
                    r = split3(e, D2[0:80, 0:256], [XPW[k][:, m, :] for k in range(2)],
                               [GS[k][:, m, :] for k in range(2)], m == 0, m == 3)
                return r
            op("tensor", f"xp{b}", [f"gs{b}.l", *XPW_OK, d2_turn(f"xp{b}")], 1320, rk(0.5), xp)
            d2(f"xp{b}", [f"ea{b}", f"tb{b}", f"zb{b}", f"bb{b}"])
            op("scalar", f"ea{b}", [f"xp{b}", pre(p, "a{}", p)], 420, rk(0.5),
               lambda e: e.activation(EA[0:16, :], D2[0:16, 0:256], ACT.Exp, bias=CO[0:16, C_XPB:C_XPB + 1]))
            op("scalar", f"tb{b}", [f"xp{b}", "hxb", pre(p, "u{}", p)], 420, rk(0.5),
               lambda e: e.activation(TB[0:16, :], D2[32:48, 0:256], ACT.Tanh, scale=0.5, bias=HXB[32:48, :]))
            op("scalar", f"a{b}", [f"ea{b}", pre(p, "scan{}", p)], 370, rk(0.5),
               lambda e: e.activation(A[0:16, :], EA[0:16, :], ACT.Exp, scale=-1.0))
            op("vector", f"zb{b}", [f"tb{b}", pre(p, "u{}", p)], 390, rk(0.5),
               lambda e: e.tensor_scalar(ZB[0:16, :], D2[32:48, 0:256], CO[32:48, C_XPB:C_XPB + 1], None, ALU.add))
            op("vector", f"u{b}", [f"tb{b}", f"zb{b}"], 335, rk(0.5),
               lambda e: e.scalar_tensor_tensor(ZB[0:16, :], TB[0:16, :], 1.0, ZB[0:16, :], ALU.add, ALU.mult))
            op("vector", f"bb{b}", [f"u{b}", pre(p, "scan{}", p)], 335, rk(0.5),
               lambda e: e.tensor_tensor(BB[0:16, :], D2[64:80, 0:256], ZB[0:16, :], ALU.mult))
            op("vector", f"scan{b}", [f"a{b}", f"bb{b}", pre(p, "ys{}.l", p)], 340, rk(0.5),
               lambda e: e.tensor_tensor_scan(YF[0:16, :], A[0:16, :], BB[0:16, :], 0.0, ALU.mult, ALU.add))
            hi_lo(f"ys{b}", YF[0:16, :], YS[0][0:16, :], YS[1][0:16, :], 256, [f"scan{b}", *OW_OK], rk(0.55),
                  free=[pre(p, "out{}", p)])

            def mo(e):
                for t in range(2):
                    r = split3(e, D2[:, 256 * t:256 * t + 256],
                               [YS[k][0:64, 128 * t:128 * t + 128] for k in range(2)],
                               [OW[k][0:64, :] for k in range(2)], t == 0, True)
                return r
            op("tensor", f"out{b}", [f"ys{b}.l", *OW_OK, d2_turn(f"out{b}")], 660, rk(0.6), mo)
            d2(f"out{b}", [f"y1{b}"])
            op("vector", f"y1{b}", [f"out{b}", f"ld.x{b}", pre(p, "n1{}.a1", p), pre(p, "n1{}.a0", p)], 600, rk(0.6),
               lambda e: e.tensor_tensor(Y1.rearrange("p t n -> p (t n)"), D2,
                                         XR[s].rearrange("p t n -> p (t n)"), ALU.add))
            n1 = norm(f"n1{b}", "a", lambda t: Y1[:, t, :], lambda t: X1[:, t, :], [f"y1{b}"], rk(0.65),
                      free=[pre(p, "x1b{}", p), pre(p, "n2{}.a1", p), pre(p, "n2{}.a0", p)],
                      again=pre(p, "n1{}.a1", p))
            op("gpsimd", f"x1b{b}", [*n1, "ld.bo", pre(b - 3, "y2{}", b - 3), *STG_FREE], 1230, rk(0.8),
               lambda e: e.tensor_tensor(X1B[b % 3], X1, BO.unsqueeze(1).to_broadcast([128, 2, 256]), ALU.add))
            n2 = norm(f"n2{b}", "b", lambda t: X1[:, t, :], lambda t: Z1[:, t, :], n1, rk(0.7),
                      free=[pre(p, "zT{}", p)], again=pre(p, "n2{}.a1", p))

            def zt(e):
                for c in range(2):
                    for t in range(2):
                        r = e.transpose(D2[:, 256 * c + 128 * t:256 * c + 128 * t + 128],
                                        Z1[:, t, 128 * c:128 * c + 128], ident)
                return r
            op("tensor", f"zT{b}", [*n2, "ld.consts", d2_turn(f"zT{b}")], 450, rk(0.75), zt)
            d2(f"zT{b}", [f"lt{b}.0", f"lt{b}.1"])
            for c in range(2):
                op("vector", f"lt{b}.{c}", [f"zT{b}", "ld.cols", pre(p, "kv{}.l", p)], 455, rk(0.75),
                   lambda e, c=c: e.tensor_scalar(LT[:, c, :], D2[:, 256 * c:256 * c + 256],
                                                  CO[:, C_GL + c:C_GL + c + 1], CO[:, C_BL + c:C_BL + c + 1],
                                                  ALU.mult, ALU.add))
            q = 8 * (b - 2) + 7
            old = [pre(b - 2, w, q) for w in ("Q{}", "K{}")] + [pre(b - 2, w, q // 2) for w in ("V{}", "Vc{}")]
            hi_lo(f"kv{b}", LT, KV[s][0][:, :, 0:256], KV[s][1][:, :, 0:256], 512,
                  [f"lt{b}.0", f"lt{b}.1"], rk(0.8), free=old, lo_on="gpsimd")

            dma("sync", f"ld.c{b}", [pre(p, "nc{}.a0", p)], "ld.c", rk(-1) - 40,
                lambda e: e.dma_start(CR[0:NC, :], ctx_in[b]))
            n3 = norm(f"nc{b}", "c", lambda t: CR[0:NC, :], lambda t: CZ[0:NC, :], [f"ld.c{b}"], rk(0),
                      free=[pre(p, "cT{}", p)], again=pre(p, "nc{}.a0", p), rows=NC, tiles=1)

            def ct(e):
                for c in range(2):
                    r = e.transpose(D2[:, NC * c:NC * c + NC], CZ[0:NC, 128 * c:128 * c + 128],
                                    KO[0:NC, K_ID:K_ID + NC])
                return r
            op("tensor", f"cT{b}", [*n3, "ld.consts", d2_turn(f"cT{b}")], 250, rk(0), ct)
            d2(f"cT{b}", [f"ct{b}.0", f"ct{b}.1"])
            for c in range(2):
                op("vector", f"ct{b}.{c}", [f"cT{b}", "ld.cols", pre(p, "kc{}.l", p)], 270, rk(0),
                   lambda e, c=c: e.tensor_scalar(CTX[:, c, :], D2[:, NC * c:NC * c + NC],
                                                  CO[:, C_GM + c:C_GM + c + 1], CO[:, C_BM + c:C_BM + c + 1],
                                                  ALU.mult, ALU.add))
            hi_lo(f"kc{b}", CTX, KV[s][0][:, :, 256:NK], KV[s][1][:, :, 256:NK], 154,
                  [f"ct{b}.0", f"ct{b}.1"], rk(0.1), free=old)


        def head(b, h):
            i = 8 * b + h
            s, s2, half = b % 2, i % 2, h // 4
            kv = KV[s]
            Qb, Kb, Pb, Ob = QS[s2], KS[s2], PM[s2], OS[s2]
            pr = i // 2
            Vb = VS[pr % 2]
            ready = [f"kv{b}.l", f"kv.z0{s}", f"kv.z1{s}"]

            def proj(e, W, off, dst, n):
                for c in range(2):
                    r = split3(e, dst[:, 0:n], [W[k][:, c, off:off + 128] for k in range(2)],
                               [kv[k][:, c, 0:n] for k in range(2)], c == 0, c == 1)
                return r
            first = i % 2 == 0
            op("tensor", f"Q{i}", [*ready, f"wq{half}.l", pre(i - 1, "q{}.l", i - 1) if first else f"vl{pr}"],
               660, i - 1.3, lambda e: proj(e, WQ, 128 * h, D0, 256))
            op("scalar", f"q{i}.h", [f"Q{i}", "bqs", pre(i - 2, "S{}.1", i - 2)], 420, i - 1.2,
               lambda e: e.activation(Qb[0], D0[:, 0:256], ACT.Identity, bias=BQS[:, h:h + 1]))
            op("vector", f"q{i}.l", [f"q{i}.h"], 400, i - 1.2,
               lambda e: e.scalar_tensor_tensor(Qb[1], D0[:, 0:256], BQS[:, h:h + 1], Qb[0].bitcast(F32),
                                                ALU.add, ALU.subtract))
            op("tensor", f"K{i}", [*ready, f"kc{b}.l", f"wk{half}.l",
                                   pre(i - 1, "k{}.l", i - 1) if first else f"vcl{pr}"],
               850, i - 1.3, lambda e: proj(e, WKV, 128 * h, D1, NP))
            bk = CO[:, C_BKV + h:C_BKV + h + 1]
            op("scalar", f"k{i}.h", [f"K{i}", pre(i - 2, "S{}.1", i - 2)], 490, i - 1.2,
               lambda e: e.activation(Kb[0], D1[:, 0:NP], ACT.Identity, bias=bk))
            op("vector", f"k{i}.l", [f"k{i}.h"], 480, i - 1.2,
               lambda e: e.scalar_tensor_tensor(Kb[1], D1[:, 0:NP], bk, Kb[0].bitcast(F32), ALU.add, ALU.subtract))
            if first:
                vo = 1024 + 128 * h

                def vproj(e, dst, a, m, one):
                    for c in range(2):
                        r = split3(e, dst, [kv[k][:, c, a:a + m] for k in range(2)],
                                   [WKV[k][:, c, vo:vo + 256] for k in range(2)], c == 0 and one, c == 1)
                    return r

                def v01(e):
                    vproj(e, D0[:, 0:256], 0, 128, True)
                    return vproj(e, D0[:, 256:512], 128, 128, False)
                vfree = pre(pr - 2, "PV{}", 2 * (pr - 2) + 1)
                op("tensor", f"V{pr}", [*ready, f"wv{half}.l", f"q{i}.l"], 1320, i - 1, v01)
                op("scalar", f"vh{pr}", [f"V{pr}", vfree], 580, i - 1,
                   lambda e: e.activation(Vb[0][:, 0:2, :], D0.rearrange("p (a b) -> p a b", a=2), ACT.Copy))
                op("vector", f"vl{pr}", [f"vh{pr}"], 600, i - 1,
                   lambda e: e.tensor_tensor(Vb[1][:, 0:2, :], D0.rearrange("p (a b) -> p a b", a=2),
                                             Vb[0][:, 0:2, :].bitcast(F32), ALU.subtract))
                op("tensor", f"Vc{pr}", [*ready, f"kc{b}.l", f"wv{half}.l", f"k{i}.l"], 660, i - 1,
                   lambda e: vproj(e, D1[0:NC, 0:256], 256, NC, True))
                op("scalar", f"vch{pr}", [f"Vc{pr}", vfree], 370, i - 1,
                   lambda e: e.activation(Vb[0][0:NC, 2, :], D1[0:NC, 0:256], ACT.Copy))
                op("vector", f"vcl{pr}", [f"vch{pr}"], 335, i - 1,
                   lambda e: e.tensor_tensor(Vb[1][0:NC, 2, :], D1[0:NC, 0:256], Vb[0][0:NC, 2, :].bitcast(F32),
                                             ALU.subtract))
            nm, rs = NM[:, s2, :], RS[:, s2, :]
            for t in range(2):
                op("tensor", f"S{i}.{t}", [f"q{i}.l", f"k{i}.l", pre(i - 1, "x{}.{}", i - 1, t)], 420, i - 0.6,
                   lambda e, t=t: split3(e, SA[t][:, 0:NP], [Qb[k][:, 128 * t:128 * t + 128] for k in range(2)],
                                         Kb, True, True))
                op("vector", f"m{i}.{t}", [f"S{i}.{t}", pre(i - 2, "x{}.{}", i - 2, t)], 420, i - 0.5,
                   lambda e, t=t: e.tensor_reduce(nm[:, t:t + 1], SA[t][:, 0:NK], AX.X, ALU.max, negate=True))
                op("scalar", f"x{i}.{t}", [f"m{i}.{t}", pre(i - 2, "T{}", i - 2), pre(i - 2, "r{}", i - 2),
                                           *STG_FREE], 560, i - 0.5,
                   lambda e, t=t: e.activation(Pb[:, t, 0:NK], SA[t][:, 0:NK], ACT.Exp, bias=nm[:, t:t + 1],
                                               accum_out=rs[:, t:t + 1]))
            op("vector", f"r{i}", [f"x{i}.0", f"x{i}.1"], 85, i - 0.4, lambda e: e.reciprocal(rs, rs))
            for t in range(2):
                op("gpsimd", f"p{i}.{t}", [f"r{i}"], 560, i - 0.4,
                   lambda e, t=t: e.tensor_scalar(Pb[:, t, 0:NK], Pb[:, t, 0:NK], rs[:, t:t + 1], 0.0,
                                                  ALU.mult, ALU.add))

            def tr(e):
                for k in range(3):
                    n = 128 if k < 2 else NC
                    for t in range(2):
                        r = e.transpose(PT[0:n, 256 * k + 128 * t:256 * k + 128 * t + 128],
                                        Pb[:, t, 128 * k:128 * k + n], ident)
                return r
            op("tensor", f"T{i}", [f"p{i}.0", f"p{i}.1", "pt.z", pre(i - 1, "o{}.l", i - 1)], 660, i, tr)
            op("scalar", f"pt{i}.h", [f"T{i}", pre(i - 1, "PV{}", i - 1)], 790, i,
               lambda e: e.activation(PTS[0], PT, ACT.Copy))
            op("vector", f"pt{i}.l", [f"pt{i}.h"], 870, i,
               lambda e: e.tensor_tensor(PTS[1], PT, PTS[0].bitcast(F32), ALU.subtract))

            def pv(e):
                for k in range(3):
                    n = 128 if k < 2 else NC
                    c0 = 128 * (h % 2)
                    r = split3(e, PO, [Vb[j][0:n, k, c0:c0 + 128] for j in range(2)],
                               [PTS[j][0:n, 256 * k:256 * k + 256] for j in range(2)], k == 0, k == 2)
                return r
            op("tensor", f"PV{i}", [f"pt{i}.l", f"vl{pr}", f"vcl{pr}"], 1000, i + 0.3, pv)
            bv = CO[:, C_BKV + 8 + h:C_BKV + 9 + h]
            op("scalar", f"o{i}.h", [f"PV{i}", pre(i - 2, "W{}", i - 2)], 420, i + 0.3,
               lambda e: e.activation(Ob[0], PO, ACT.Identity, bias=bv))
            op("vector", f"o{i}.l", [f"o{i}.h"], 400, i + 0.3,
               lambda e: e.scalar_tensor_tensor(Ob[1], PO, bv, Ob[0].bitcast(F32), ALU.add, ALU.subtract))

            def mw(e):
                for t in range(2):
                    r = split3(e, PW[:, 256 * t:256 * t + 256], [Ob[k][:, 128 * t:128 * t + 128] for k in range(2)],
                               [WO[k][:, h, :] for k in range(2)], h == 0 and t == 0, h == 7)
                return r
            op("tensor", f"W{i}", [f"o{i}.l", f"wo{half}.l", pre(b - 1, "y2{}", b - 1) if h == 0 else None],
               660, i + 0.6, mw)


        def route(b):
            s, p = b % 2, b - 1
            X = X2E[s]
            rk = lambda f: 8 * b + 8 + 2 * f
            free = [pre(b - 2, "st{}", b - 2)] + [pre(b - 2, "sc{}.{}", b - 2, k) for k in range(4)]
            if b < 2:
                free = [INIT_OK]
            op("vector", f"y2{b}", [f"W{8 * b + 7}", f"x1b{b}", pre(p, "n4{}.a1", p), pre(p, "n4{}.a0", p),
                                    "xpw0.l", "xpw1.l", "ow.l"], 600, rk(0) - 1,
               lambda e: e.tensor_tensor(Y2.rearrange("p t n -> p (t n)"), PW,
                                         X1B[b % 3].rearrange("p t n -> p (t n)"), ALU.add))
            n4 = norm(f"n4{b}", "d", lambda t: Y2[:, t, :], lambda t: X[:, t, 0:256], [f"y2{b}"], rk(0),
                      free=free, again=pre(p, "n4{}.a1", p))
            dma("sync", f"st{b}", n4, f"st{s}", rk(0), lambda e: e.dma_start(
                acc[256 * b:256 * b + 256, :].rearrange("(t p) n -> p t n", p=128), X[:, :, 0:256]))
            op("vector", f"id{b}", [*free, "ld.consts"], 80, rk(0),
               lambda e: e.tensor_scalar(X[:, :, 256], KO[:, K_TOK:K_TOK + 2], 256.0 * b, None, ALU.add))

            def rt(e):
                for c in range(2):
                    for t in range(2):
                        r = e.transpose(D2[:, 256 * c + 128 * t:256 * c + 128 * t + 128],
                                        X[:, t, 128 * c:128 * c + 128], ident)
                return r
            op("tensor", f"rT{b}", [*n4, d2_turn(f"rT{b}")], 450, rk(0.1), rt)
            d2(f"rT{b}", [f"x2t{b}"])
            op("scalar", f"x2t{b}", [f"rT{b}", pre(p, "lg{}", p), "xpw0.l", "xpw1.l", "ow.l"], 580, rk(0.1),
               lambda e: e.activation(X2T.rearrange("p c n -> p (c n)"), D2, ACT.Copy))

            def lg(e):
                for c in range(2):
                    r = e.matmul(D2[0:8, 0:256], CO[:, C_E + 8 * c:C_E + 8 * c + 8], X2T[:, c, :],
                                 start=c == 0, stop=c == 1)
                return r
            op("tensor", f"lg{b}", [f"x2t{b}", d2_turn(f"lg{b}")], 870, rk(0.2), lg)
            d2(f"lg{b}", [f"lgc{b}"])
            op("vector", f"lgc{b}", [f"lg{b}", pre(p, "lgT{}", p)], 335, rk(0.2),
               lambda e: e.tensor_copy(LGT[0:8, :], D2[0:8, 0:256]))

            def lt(e):
                for t in range(2):
                    r = e.transpose(D2[:, 8 * t:8 * t + 8], LGT[0:8, 128 * t:128 * t + 128], KO[0:8, K_ID:K_ID + 8])
                return r
            op("tensor", f"lgT{b}", [f"lgc{b}", d2_turn(f"lgT{b}")], 100, rk(0.3), lt)
            d2(f"lgT{b}", [f"l8{b}"])
            v = lambda name, waits, issue, f=0.4, cost=90: op("vector", f"{name}{b}", waits, cost, rk(f), issue)
            n = lambda name: f"{name}{b}"
            o = lambda name: pre(p, "{}{}", name, p)
            iota = KO[:, K_IOTA:K_IOTA + 8]
            v("l8", [n("lgT"), o("ix1.")], lambda e: e.tensor_copy(LG, D2[:, 0:16].rearrange("p (a b) -> p a b", a=2)))
            for t in range(2):
                v(f"mx{t}.", [n("l8"), o("d")], lambda e, t=t: e.max(M8[:, t, :], LG[:, t, :]))
                v(f"ix{t}.", [n(f"mx{t}."), o("if")], lambda e, t=t: e.max_index(I8[:, t, :], M8[:, t, :], LG[:, t, :]))
            v("if", [n("ix0."), n("ix1."), o("oh1.1.")], lambda e: e.tensor_copy(IF, I8[:, :, 0:2]))
            v("d", [n("mx0."), n("mx1."), o("e")],
              lambda e: e.tensor_tensor(DW[:, :, 0], M8[:, :, 1], M8[:, :, 0], ALU.subtract))
            op("scalar", n("e"), [n("d"), o("w2"), o("dn")], 230, rk(0.4),
               lambda e: e.activation(DW[:, :, 1], DW[:, :, 0], ACT.Exp))
            v("dn", [n("e"), o("w1")], lambda e: e.tensor_scalar(DW[:, :, 0], DW[:, :, 1], 1.0, None, ALU.add))
            v("w1", [n("dn"), o("w81.")], lambda e: e.reciprocal(DW[:, :, 2], DW[:, :, 0]))
            v("w2", [n("w1"), o("w81.")], lambda e: e.tensor_tensor(DW[:, :, 3], DW[:, :, 1], DW[:, :, 2], ALU.mult))
            v("gt", [n("w2"), o("oh1.1.")],
              lambda e: e.tensor_scalar(DW[:, :, 0], DW[:, :, 3], 0.0, None, ALU.is_gt))
            for t in range(2):
                v(f"oh{t}.0.", [n("if"), o("pr0.")],
                  lambda e, t=t: e.tensor_scalar(OH[:, 0, t, :], iota, IF[:, t, 0:1], None, ALU.is_equal))
                v(f"oh{t}.1.", [n("if"), n("gt"), o("pr1.")],
                  lambda e, t=t: e.tensor_scalar(OH[:, 1, t, :], iota, IF[:, t, 1:2], DW[:, t, 0:1],
                                                 ALU.is_equal, ALU.mult))
            ohs = [n(f"oh{t}.{j}.") for t in range(2) for j in range(2)]
            v("ob", [*ohs, o("cum")], lambda e: e.tensor_tensor(OHB[:, :, :], OH[:, 0], OH[:, 1], ALU.add))
            for t in range(2):
                w8 = X[:, t, 257:265]
                v(f"wa{t}.", [n(f"oh{t}.0."), n("w1"), *free],
                  lambda e, t=t, w8=w8: e.tensor_scalar(w8, OH[:, 0, t, :], DW[:, t, 2:3], None, ALU.mult))
                v(f"w8{t}.", [n(f"wa{t}."), n(f"oh{t}.1."), n("w2")],
                  lambda e, t=t, w8=w8: e.scalar_tensor_tensor(w8, OH[:, 1, t, :], DW[:, t, 3:4], w8,
                                                               ALU.mult, ALU.add))

            def cum(e):
                m = lambda dst, w, t, a, z: e.matmul(D2[:, 8 * dst:8 * dst + 8], w[:, :], OHB[:, t, :], start=a,
                                                     stop=z, skip_group_check=True)
                m(0, TRI, 0, True, True)
                m(1, ONE, 0, False, False)
                m(1, TRI, 1, False, True)
                m(2, ONE, 0, False, False)
                return m(2, ONE, 1, False, True)
            op("tensor", n("cum"), [n("ob"), "tri", "one", d2_turn(f"cum{b}")], 130, rk(0.5), cum)
            d2(f"cum{b}", [n("pos"), n("run")])
            v("pos", [n("cum"), o("run"), "run.z", o("pr1."), o("pr0.")], lambda e: e.tensor_tensor(
                V8, D2[:, 0:16].rearrange("p (a b) -> p a b", a=2),
                RUN.unsqueeze(1).to_broadcast([128, 2, 8]), ALU.add), 0.5)
            v("run", [n("pos")], lambda e: e.tensor_tensor(RUN, RUN, D2[:, 16:24], ALU.add), 0.5)
            v("g8", [n("pos"), o("v8")], lambda e: e.tensor_scalar(G8, V8, float(CAP), FAR, ALU.is_gt, ALU.mult), 0.5)
            v("v7", [n("g8")], lambda e: e.tensor_tensor(
                V8, V8, KO[:, K_BASE:K_BASE + 16].rearrange("p (a b) -> p a b", a=2), ALU.add), 0.5)
            v("v8", [n("v7")], lambda e: e.tensor_tensor(V8, V8, G8, ALU.add), 0.5)
            for j in range(2):
                v(f"pr{j}.", [n("v8"), *ohs, o("sl")],
                  lambda e, j=j: e.tensor_tensor(PR[:, j], OH[:, j], V8, ALU.mult), 0.5)
            v("sl", [n("pr0."), n("pr1."), o("sx")],
              lambda e: e.tensor_reduce(SL.rearrange("p a b -> p (a b)"), PR.rearrange("p a b c -> p (a b) c"),
                                        AX.X, ALU.add), 0.5)
            old = [pre(b - 2, "sc{}.{}", b - 2, k) for k in range(4)]
            v("sx", [n("sl"), *old], lambda e: e.tensor_scalar(
                IX[:, s, :], SL.rearrange("p a b -> p (a b)"), FAR, None, ALU.add), 0.5)
            for k in range(4):
                dma("gpsimd", f"sc{b}.{k}", [n("sx"), *n4, n("id"), n("w80."), n("w81."), INIT_OK], f"sc{s}",
                    rk(0.6), lambda e, k=k: e.indirect_dma_start(
                        out=xs, out_offset=bass.IndirectOffsetOnAxis(ap=IX[:, s, k:k + 1], axis=0),
                        in_=X[:, k % 2, :], in_offset=None, bounds_check=NT - 1, oob_is_err=False), cost=1050)


        lastq = NI - 1
        S1_DONE = [f"out{NB - 1}", f"y1{NB - 1}", f"gs{NB - 1}.l", f"ys{NB - 1}.l", f"xp{NB - 1}"]
        QKV_DONE = [f"Q{lastq}", f"K{lastq}", f"V{lastq // 2}", f"Vc{lastq // 2}"]
        ROUTED = [f"sc{b}.{k}" for b in (NB - 2, NB - 1) for k in range(4)]
        W1B = [5, 6, 7, 4]

        def expert(g):
            s = g % 2
            X, Y, IH, W1, W2 = XSL[s], YO[s], FI, FW1[s], FW2[s]
            rk = lambda f: 8 * NB + 10 + 8 * g + 8 * f
            start = S1_DONE if s == 0 else [*QKV_DONE, *S1_DONE]
            p = g - 1
            for k, (raw, src, W, after) in enumerate(((RW1[s], w1[g], W1, "U"), (RW2[s], w2[g], W2, "Y"))):
                dma("sync", f"ld.f{g}.{k}", [*S1_DONE, pre(g - 2, "fw{}.{}.l", g - 2, k)], f"ld.f{s}{k}", rk(-2),
                    lambda e, raw=raw, src=src: e.dma_start(raw, src))
                last = f"U{g - 2}.3" if k == 0 else f"Y{g - 2}.{CT - 1}"
                hi_lo(f"fw{g}.{k}", raw, W[0], W[1], 1024, [f"ld.f{g}.{k}"], rk(-1.2),
                      free=start if g < 2 else [last], lo_on="gpsimd")
            dma("sync", f"ld.g{g}", [*ROUTED, *S1_DONE, pre(g - 2, "yo{}.{}", g - 2, CT - 1), pre(g - 2, "fT{}", g - 2),
                                     f"n4{NB - 1}.a0", pre(g - 2, "ie{}", g - 2)],
                f"ld.g{s}", rk(-1.5), lambda e: e.dma_start(
                    X, xs[g * CAP:(g + 1) * CAP, :].rearrange("(t p) n -> p t n", p=128)))
            op("vector", f"ie{g}", [f"ld.g{g}"] + [pre(g - 2, "sa{}.{}", g - 2, t) for t in range(CT)], 90, rk(0),
               lambda e: e.tensor_copy(IE[:, s, 0:CT], X[:, :, 256]))

            def ft(e):
                for c in range(2):
                    for t in range(CT):
                        r = e.transpose(SA[c][:, 128 * t:128 * t + 128], X[:, t, 128 * c:128 * c + 128], ident)
                return r
            op("tensor", f"fT{g}", [f"ld.g{g}", pre(p, "fx{}.1.l", p), f"x{lastq}.0", f"x{lastq}.1"], 880, rk(0), ft)
            for c in range(2):
                free = QKV_DONE if g < 2 else [f"U{g - 2}.3"]
                op("scalar", f"fx{g}.{c}.h", [f"fT{g}", *free], ac(CAP), rk(0.1),
                   lambda e, c=c: e.activation(FX[s][0][:, c, :], SA[c][:, 0:CAP], ACT.Copy))
                op("vector", f"fx{g}.{c}.l", [f"fx{g}.{c}.h"], tc(CAP), rk(0.1),
                   lambda e, c=c: e.tensor_tensor(FX[s][1][:, c, :], SA[c][:, 0:CAP],
                                                  FX[s][0][:, c, :].bitcast(F32), ALU.subtract))
            for m in range(4):
                pb = bank(W1B[m])[:, 0:CAP]

                def up(e, m=m, pb=pb):
                    for c in range(2):
                        r = split3(e, pb, [W1[k][:, c, 128 * m:128 * m + 128] for k in range(2)],
                                   [FX[s][k][:, c, :] for k in range(2)], c == 0, c == 1)
                    return r
                free = [pre(p, "i{}.{}.l", p, m)] if g else [f"y2{NB - 1}", f"run{NB - 1}", f"pos{NB - 1}",
                                                            f"k{lastq}.l", f"q{lastq}.l"]
                op("tensor", f"U{g}.{m}", [f"fx{g}.0.l", f"fx{g}.1.l", f"fw{g}.0.l", *free], 1320,
                   rk(0.2 + 0.1 * m), up)
                free = [pre(p, "Y{}.{}", p, CT - 1)] if g else QKV_DONE
                op("scalar", f"i{g}.{m}.h", [f"U{g}.{m}", *free], ac(CAP), rk(0.2 + 0.1 * m),
                   lambda e, m=m, pb=pb: e.activation(IH[0][:, m, :], pb, ACT.Relu))
                op("vector", f"i{g}.{m}.l", [f"i{g}.{m}.h"], tc(CAP), rk(0.2 + 0.1 * m),
                   lambda e, m=m, pb=pb: e.scalar_tensor_tensor(IH[1][:, m, :], pb, 0.0,
                                                                IH[0][:, m, :].bitcast(F32), ALU.max, ALU.subtract))
            for t in range(CT):
                pb = bank(2 + t % 2)[:, 0:256]

                def down(e, t=t, pb=pb):
                    for m in range(4):
                        r = split3(e, pb, [IH[k][:, m, 128 * t:128 * t + 128] for k in range(2)],
                                   [W2[k][:, m, :] for k in range(2)], m == 0, m == 3)
                    return r
                k = g * CT + t - 2
                free = f"yo{k // CT}.{k % CT}" if k >= 0 else f"o{lastq}.l"
                op("tensor", f"Y{g}.{t}", [f"i{g}.{m}.l" for m in range(4)] + [f"fw{g}.1.l", free], 1320,
                   rk(0.6 + 0.1 * t), down)
                op("scalar", f"yo{g}.{t}", [f"Y{g}.{t}"] + [pre(g - 2, "sa{}.{}", g - 2, k) for k in range(CT)]
                   + [f"n4{NB - 1}.a0"],
                   480, rk(0.6 + 0.1 * t), lambda e, t=t, pb=pb: e.activation(
                       Y[:, t, :], pb, ACT.Copy, scale=X[:, t, 257 + g:258 + g]))
                dma("gpsimd", f"sa{g}.{t}", [f"yo{g}.{t}", f"ie{g}"] + [pre(p, "sa{}.{}", p, k) for k in range(CT)]
                    + [f"st{NB - 1}", f"st{NB - 2}", INIT_OK],
                    f"sa{s}", rk(0.8 + 0.1 * t), lambda e, t=t: e.indirect_dma_start(
                        out=acc, out_offset=bass.IndirectOffsetOnAxis(ap=IE[:, s, t:t + 1], axis=0),
                        in_=Y[:, t, :], in_offset=None, bounds_check=NT + CAP - 1, oob_is_err=True,
                        compute_op=ALU.add), cost=1050)


        def finish():
            added = [f"sa{g}.{t}" for g in (E - 2, E - 1) for t in range(CT)]
            st, mv, rs, nr = tail_stats
            rk = 8 * NB + 8 * E + 40
            for n in range(NCH):
                rows = slice(512 * n, 512 * n + 512)
                dma("sync", f"ld.a{n}", added, f"ld.a{n}", rk + n,
                    lambda e, n=n, rows=rows: e.dma_start(AC[n], acc[rows, :].rearrange("(t p) n -> p t n", p=128)))
                for t in range(4):
                    k = 4 * n + t
                    op("vector", f"f.s{k}", [f"ld.a{n}"], 345, rk + n,
                       lambda e, n=n, t=t, k=k: e.bn_stats(st[:, k, :], AC[n][:, t, :]))
                    op("vector", f"f.m{k}", [f"f.s{k}"], 80, rk + n,
                       lambda e, k=k: e.bn_aggr(mv[:, k, :], st[:, k, :]))
                c = slice(4 * n, 4 * n + 4)
                op("vector", f"f.v{n}", [f"f.m{4 * n + t}" for t in range(4)], 80, rk + n,
                   lambda e, c=c: e.tensor_scalar(rs[:, c], mv[:, c, 1], EPS, None, ALU.add))
                op("gpsimd", f"f.r{n}", [f"f.v{n}", "mh4"], 640, rk + n,
                   lambda e, c=c: e.tensor_tensor(rs[:, c], rs[:, c], MH4, ALU.pow))
                op("vector", f"f.n{n}", [f"f.r{n}"], 80, rk + n,
                   lambda e, c=c: e.scalar_tensor_tensor(nr[:, c], mv[:, c, 0], -1.0, rs[:, c], ALU.mult, ALU.mult))
                for t in range(4):
                    k = 4 * n + t
                    op("scalar", f"f.o{k}", [f"f.n{n}"], 490, rk + n,
                       lambda e, n=n, t=t, k=k: e.activation(AC[n][:, t, :], AC[n][:, t, :], ACT.Identity,
                                                             bias=nr[:, k:k + 1], scale=rs[:, k:k + 1]))
                dma("sync", f"st.o{n}", [f"f.o{4 * n + t}" for t in range(4)], "st.o", rk + n,
                    lambda e, n=n, rows=rows: e.dma_start(out[rows, :].rearrange("(t p) n -> p t n", p=128), AC[n]))
            op("sync", "end", [f"st.o{n}" for n in range(NCH)], 10, rk + 50, lambda e: None)

        MH4 = F.take(4)
        op("gpsimd", "mh4", [], 100, -40, lambda e: e.memset(MH4, -0.5))

        for b in range(NB):
            stage1(b)
            for h in range(H):
                head(b, h)
            route(b)
        for g in range(E):
            expert(g)
        finish()
        for o in P.ops.values():
            flat = []
            for w in o["waits"]:
                flat += d2_end[w[1]] if isinstance(w, tuple) else [w]
            o["waits"] = flat
        P.emit()
        return P



def layout(inputs):
    import numpy as np
    f = lambda n: np.asarray(inputs[n], dtype=np.float32)
    L = {}
    xx = f("x")
    nt = xx.shape[0] * xx.shape[1]
    cap = nt // E
    L["x"] = xx.reshape(nt, 256)
    L["xT"] = xx.reshape(nt, 256).T
    L["ctx_in"] = f("ctx_1024")
    cols = np.zeros((128, C_END), np.float32)
    part = lambda v: v.reshape(-1, 128).T
    cols[:, C_INB:C_INB + 4] = part(f("L0_attn_in_b"))
    cols[:, C_CB:C_CB + 4] = part(f("L0_attn_conv_b"))
    cols[:, C_CW:C_CW + 16] = f("L0_attn_conv_w").reshape(4, 128, 4).transpose(1, 0, 2).reshape(128, 16)
    cols[0:16, C_XPB] = f("L0_attn_xp_b")[0:16]
    cols[32:48, C_XPB] = f("L0_attn_xp_b")[16:32]
    cols[:, C_BQ:C_BQ + 8] = part(f("L0_xattn_bq"))
    cols[:, C_BKV:C_BKV + 16] = part(f("L0_xattn_bkv"))
    cols[:, C_GM:C_GM + 2] = part(f("L0_xattn_gamma_media"))
    cols[:, C_BM:C_BM + 2] = part(f("L0_xattn_beta_media"))
    cols[:, C_GL:C_GL + 2] = part(f("L0_xattn_gamma_lat"))
    cols[:, C_BL:C_BL + 2] = part(f("L0_xattn_beta_lat"))
    cols[:, C_E:C_E + 16] = f("L0_ffn_expert_embeddings").T.reshape(2, 128, 8).transpose(1, 0, 2).reshape(128, 16)
    L["cols"] = cols
    k = np.zeros((128, K_END), np.float32)
    k[:, K_ID:K_ID + 128] = np.eye(128)
    k[:, K_TRI:K_TRI + 128] = np.triu(np.ones((128, 128)))
    k[:, K_IOTA:K_IOTA + 16] = np.tile(np.arange(8), 2)
    k[:, K_BASE:K_BASE + 16] = np.tile(cap * np.arange(8) - 1 - FAR, 2)
    k[:, K_TOK:K_TOK + 2] = np.arange(128)[:, None] + 128 * np.arange(2)
    k[:, K_DUMP:K_DUMP + 4] = nt + np.arange(128)[:, None] + 128 * np.arange(4)
    L["consts"] = k
    c = lambda w: w.reshape(-1, 128, w.shape[-1]).transpose(1, 0, 2)
    L["in_w"] = c(f("L0_attn_in_w").T)
    L["xp_w"] = c(f("L0_attn_xp_w").T)
    L["out_w"] = np.concatenate([f("L0_attn_out_w").T, f("L0_attn_out_b")[None]], 0)
    L["Wq"] = c(f("L0_xattn_Wq"))
    L["Wkv"] = c(f("L0_xattn_Wkv"))
    L["Wo"] = c(f("L0_xattn_Wo"))
    L["bo"] = f("L0_xattn_bo")
    L["w1"] = f("L0_ffn_first_linear").transpose(0, 2, 1).reshape(E, 2, 128, 512).transpose(0, 2, 1, 3)
    L["w2"] = f("L0_ffn_second_linear").transpose(0, 2, 1).reshape(E, 4, 128, 256).transpose(0, 2, 1, 3)
    return {n: np.ascontiguousarray(a) for n, a in L.items()}


_INS = ["x", "xT", "ctx_in", "cols", "consts", "in_w", "xp_w", "out_w", "Wq", "Wkv", "Wo", "bo", "w1", "w2"]


def kernel(**inputs):
    import numpy as _np
    import concourse.bacc as _bacc
    from concourse import mybir as _mybir
    from concourse.bass_utils import run_bass_kernel_spmd as _run

    nc = _bacc.Bacc("TRN2", target_bir_lowering=False, num_devices=1)
    L = layout(inputs)
    arrays, args = {}, []
    for name in _INS:
        a = L[name]
        arrays[f"in_{name}_dram"] = a
        args.append(nc.dram_tensor(f"in_{name}_dram", a.shape, _mybir.dt.from_np(a.dtype), kind="ExternalInput").ap())
    nt = L["x"].shape[0]
    args.append(nc.dram_tensor("out_0_dram", [nt, 256], F32, kind="ExternalOutput").ap())
    decoder_layer(nc, *args)
    r = _run(nc, [arrays], core_ids=[0])
    return _np.asarray(r.results[0]["out_0_dram"]).reshape(nt // 256, 256, 256)
```

```python
from contextlib import ExitStack

import concourse.bass as bass
from concourse import mybir

ACT = mybir.ActivationFunctionType
ALU = mybir.AluOpType
AX = mybir.AxisListType
F32 = mybir.dt.float32
F32R = mybir.dt.float32r
BF16 = mybir.dt.bfloat16
U32 = mybir.dt.uint32

H = 8
E = 8
NC = 77
NK = 333
NP = 334
ROW = 272
EPS = 1e-5
FAR = 65536.0

C_INB, C_CB, C_CW, C_XPB, C_BQ, C_BKV, C_GM, C_BM, C_GL, C_BL, C_E = 0, 4, 8, 24, 25, 33, 49, 51, 53, 55, 57
C_END = 73
K_ID, K_TRI, K_IOTA, K_BASE, K_TOK, K_DUMP = 0, 128, 256, 272, 288, 290
K_END = 294


RANK = dict(Q=-1.3, q=-1.2, V=-1.0, v=-1.0, S=-0.6, m=-0.5, x=-0.5, r=-0.4, T=0.0, pt=0.0, PV=0.3, o=0.3, W=0.6,
            s1=-4.0, s1x=8.0, rt=8.0, rtx=2.0)


class Program:

    LAG = {"tensor": dict(tensor=200, scalar=197, vector=196, gpsimd=200, sync=100),
           "scalar": dict(tensor=300, scalar=150, vector=152, gpsimd=175, sync=100),
           "vector": dict(tensor=256, scalar=128, vector=127, gpsimd=155, sync=100),
           "gpsimd": dict(tensor=200, scalar=110, vector=58, gpsimd=88, sync=100),
           "sync": dict(tensor=100, scalar=100, vector=100, gpsimd=100, sync=100)}

    def __init__(self, nc, sem):
        self.nc = nc
        self.sem = sem
        self.ops = {}
        self.turns = {}

    def op(self, engine, name, waits, cost, rank, issue):
        assert name not in self.ops, name
        self.ops[name] = dict(engine=engine, name=name, waits=list(waits), cost=cost, rank=rank,
                              issue=issue, slot=None, late=0.0, move=0.0)

    def dma(self, engine, name, waits, slot, rank, issue, cost=470.0, kb=256):
        self.op(engine, name, waits, cost, rank, issue)
        self.ops[name].update(slot=slot, late=1900.0, move=kb * 1024 / 350.0)

    def order(self):
        for o in self.ops.values():
            o["waits"] = [w for w in o["waits"] if w is not None]
            for w in o["waits"]:
                assert w in self.ops, (o["name"], w)
        left = {n: len(set(o["waits"])) for n, o in self.ops.items()}
        after = {}
        for n, o in self.ops.items():
            for w in set(o["waits"]):
                after.setdefault(w, []).append(n)
        ready, end, moved = {}, {}, 0.0
        engines = sorted({o["engine"] for o in self.ops.values()})
        cand = {g: [] for g in engines}
        free = {g: 0.0 for g in engines}
        queue = {g: [] for g in engines}
        for n, o in self.ops.items():
            if not left[n]:
                ready[n] = 0.0
                cand[o["engine"]].append(n)
        todo = len(self.ops)
        while todo:
            best = None
            for g in engines:
                if cand[g]:
                    s = max(free[g], min(ready[n] for n in cand[g]))
                    if best is None or s < best[0]:
                        best = (s, g)
            assert best is not None, [n for n in left if left[n]][:20]
            s, g = best
            n = min((n for n in cand[g] if ready[n] <= s), key=lambda n: (self.ops[n]["rank"], ready[n]))
            cand[g].remove(n)
            o = self.ops[n]
            free[g] = s + o["cost"]
            end[n] = free[g]
            if o["slot"]:
                moved = max(moved, free[g] + 700.0) + o["move"]
                end[n] = moved + 1100.0
            queue[g].append(o)
            todo -= 1
            for m in after.get(n, ()):
                left[m] -= 1
                if not left[m]:
                    ready[m] = max(end[w] + self.LAG[self.ops[w]["engine"]][self.ops[m]["engine"]]
                                   for w in self.ops[m]["waits"])
                    cand[self.ops[m]["engine"]].append(m)
        self.planned = max(end.values())
        self.endt = end
        return queue

    def emit(self):
        queue = self.order()
        wanted = {w for o in self.ops.values() for w in o["waits"]}
        count, mark = {}, {}
        for g, ops in queue.items():
            for o in ops:
                if o["slot"]:
                    count[o["slot"]] = count.get(o["slot"], 0) + 16
                    mark[o["name"]] = (o["slot"], count[o["slot"]])
                elif o["name"] in wanted:
                    count[g] = count.get(g, 0) + 1
                    mark[o["name"]] = (g, count[g])
        sems = {s: self.sem("s_" + s) for s in count}

        def run(g):
            def body(eng):
                seen = {}
                for o in queue.get(g, ()):
                    need = {}
                    for w in o["waits"]:
                        s, v = mark[w]
                        need[s] = max(v, need.get(s, 0))
                    for s, v in need.items():
                        if seen.get(s, 0) < v:
                            eng.wait_ge(sems[s], v)
                            seen[s] = v
                    last = o["issue"](eng)
                    if o["name"] in mark:
                        last.then_inc(sems[mark[o["name"]][0]], 16 if o["slot"] else 1)
            return body

        with self.nc.Block() as block:
            block.sync(run("sync"))
            block.tensor(run("tensor"))
            block.scalar(run("scalar"))
            block.vector(run("vector"))
            block.gpsimd(run("gpsimd"))


def decoder_layer(nc, x, xT, ctx_in, cols, consts, in_w, xp_w, out_w, Wq, Wkv, Wo, bo, w1, w2, out):
    NT = x.shape[0]
    RK = RANK
    NB = NT // 256
    CAP = NT // E
    CT = CAP // 128
    NI = NB * H
    SCALE = 128.0 ** -0.5

    xs = nc.dram_tensor("xs", [NT, ROW], F32, kind="Internal").ap()
    acc = nc.dram_tensor("acc", [NT + CAP, 256], F32, kind="Internal").ap()

    es = ExitStack()
    with es:
        sem = lambda name: es.enter_context(nc.semaphore(name))
        P = Program(nc, sem)
        op, dma = P.op, P.dma

        class Arena:
            def __init__(self, name, size, dt):
                self.t = es.enter_context(nc.sbuf_tensor(name, [128, size], dt))
                self.size, self.at = size, 0

            def take(self, *shape, at=None):
                n = 1
                for d in shape:
                    n *= d
                if at is None:
                    at = self.at
                    self.at += n
                    assert self.at <= self.size, (self.at, self.size)
                v = self.t[:, at:at + n]
                if len(shape) == 2:
                    v = v.rearrange("p (a b) -> p a b", a=shape[0])
                if len(shape) == 3:
                    v = v.rearrange("p (a b c) -> p a b c", a=shape[0], b=shape[1])
                return v

        R = Arena("R", 36040, F32R)
        F = Arena("F", 16100, F32)

        WQ = [R.take(2, 1024) for _ in range(2)]
        r_wkv = R.at
        WKV = [R.take(2, 2048) for _ in range(2)]
        r_wo = R.at
        WO = [R.take(8, 256) for _ in range(2)]
        r_s1 = R.at
        INW = [R.take(2, 512) for _ in range(2)]
        XPW = [R.take(4, 80) for _ in range(2)]
        OW = R.take(256)
        XS = [R.take(2, 256) for _ in range(2)]
        GS = [R.take(4, 256) for _ in range(2)]
        YS = R.take(256)
        KV = [[R.take(2, NP) for _ in range(2)] for _ in range(2)]
        QS = [[R.take(256) for _ in range(2)] for _ in range(3)]
        KS = [[R.take(NP) for _ in range(2)] for _ in range(3)]
        VS = [[R.take(3, 256) for _ in range(2)] for _ in range(2)]
        PTS = [[R.take(768) for _ in range(2)] for _ in range(2)]
        OS = [[R.take(256) for _ in range(2)] for _ in range(2)]
        FW1 = [[R.take(2, 512, at=b + 1024 * k) for k in range(2)] for b in (r_s1, r_wkv)]
        FW2 = [[R.take(4, 256, at=b + 2048 + 1024 * k) for k in range(2)] for b in (r_s1, r_wkv)]
        FX = [[R.take(2, CAP, at=r_wkv + 4096 + 2048 * s + 2 * CAP * k) for k in range(2)] for s in range(2)]
        FI = [[R.take(4, CAP, at=b + 4 * CAP * k) for k in range(2)] for b in (0, r_wo)]

        CO = F.take(C_END)
        KO = F.take(K_END)
        BQS = F.take(H)
        HXB = F.take(1)
        MH = F.take(4)
        RUN = F.take(E)
        BO = F.take(256)
        f_s1 = F.at
        XTR = [F.take(2, 256) for _ in range(2)]
        XR = [F.take(2, 256) for _ in range(2)]
        HP = F.take(4, 259)
        Z = F.take(4, 256)
        ZP = F.take(256)
        TH = F.take(4, 256)
        A, TB, ZB, YF = [F.take(256) for _ in range(4)]
        Y1 = F.take(2, 256)
        f_z1 = F.at
        Z1 = F.take(2, 256)
        LT = F.take(2, 256)
        CR = F.take(256)
        CZ = F.take(256)
        CTX = F.take(2, NC)
        f_x1b = F.at
        X1B = [F.take(2, 256) for _ in range(3)]
        f_pm = F.at
        PM = [F.take(2, NP) for _ in range(2)]
        X2E = [F.take(2, ROW) for _ in range(2)]
        f_y2 = F.at
        Y2 = F.take(2, 256)
        X2T = F.take(2, 256)
        LGT = F.take(256)
        LG = F.take(2, 8)
        M8 = F.take(2, 8)
        IF = F.take(2, 2)
        DW = F.take(2, 4)
        GT = F.take(2)
        OH = F.take(2, 2, 8)
        V8 = F.take(2, 8)
        G8 = F.take(2, 8)
        PR = F.take(2, 2, 8)
        SL = F.take(2, 2)
        NM = F.take(2, 2)
        RS = F.take(2, 2)
        stats = {}
        for k in ("a", "c", "d"):
            stats[k] = (F.take(2, 6), F.take(2, 2), F.take(4), F.take(4))
        tail_stats = (F.take(32, 6), F.take(32, 2), F.take(32), F.take(32))
        STG = [F.take(1024, at=k) for k in (f_pm, f_x1b, f_z1)]
        INIT = F.take(CT, ROW, at=f_y2 - 4 * ROW)
        INIT_ALL = F.take(4 * ROW, at=f_y2 - 4 * ROW)
        XSL = [F.take(CT, ROW, at=f_s1 + 5400 + CT * ROW * s) for s in range(2)]
        YO = [F.take(CT, 256, at=f_s1 + 5400 + 2 * 1088 + CT * 256 * s) for s in range(2)]
        RW1 = [F.take(2, 512, at=f_s1 + 2048 * s) for s in range(2)]
        RW2 = [F.take(4, 256, at=f_s1 + 2048 * s + 1024) for s in range(2)]
        NCH = NT // 256
        AC = [F.take(2, 256, at=f_s1 + 512 * s) for s in range(NCH)]
        assert f_s1 + 5400 + 2 * 1088 + 2 * 1024 <= f_y2 and f_s1 + 512 * NCH <= f_y2

        I8 = es.enter_context(nc.sbuf_tensor("I8", [128, 2, 8], U32))
        IX = es.enter_context(nc.sbuf_tensor("IX", [128, 2, 4], U32))
        IE = es.enter_context(nc.sbuf_tensor("IE", [128, 2, 4], U32))
        TRI = es.enter_context(nc.sbuf_tensor("TRI", [128, 128], BF16))
        ONE = es.enter_context(nc.sbuf_tensor("ONE", [128, 128], BF16))
        OHB = es.enter_context(nc.sbuf_tensor("OHB", [128, 2, 8], BF16))

        PS = es.enter_context(nc.psum_tensor("PS", [128, 8 * 512], F32))
        bank = lambda k: PS[:, 512 * k:512 * (k + 1)]
        SA = [bank(0), bank(1)]
        PT = PS[:, 1024:1024 + 768]
        PO = PS[:, 1024 + 768:2048]
        PW = bank(4)
        D0, D1, D2 = bank(5), bank(6), bank(7)

        ident = KO[:, K_ID:K_ID + 128]
        pre = lambda i, name, *a: name.format(*a) if i >= 0 else None

        tc = lambda n: 65 + 1.04 * n
        ac = lambda n: 94 + 0.833 * n
        pc = lambda n: 150 + 2.1 * n

        def hi_lo(tag, raw, hi, lo, n, waits, rank, scale=1.0, free=(), lo_on="vector", rows=slice(0, 128)):
            op("scalar", tag + ".h", [*waits, *free], ac(n), rank,
               lambda e: e.activation(hi, raw, ACT.Copy, scale=scale))
            if lo_on == "gpsimd":
                op("gpsimd", tag + ".l", [tag + ".h", *waits, *free], pc(n), rank,
                   lambda e: e.tensor_tensor(lo, raw, hi.bitcast(F32), ALU.subtract))
                return
            op("vector", tag + ".l", [tag + ".h", *waits, *free], tc(n), rank,
               lambda e: e.scalar_tensor_tensor(lo, raw, scale, hi.bitcast(F32), ALU.mult, ALU.subtract))

        def split3(e, dst, w, xr, first, last):
            for n, (i, j) in enumerate(((0, 0), (0, 1), (1, 0))):
                r = e.matmul(dst, w[i], xr[j], start=first and n == 0, stop=last and n == 2,
                             skip_group_check=True)
            return r


        dma("sync", "ld.cols", [], "ld.cols", -98, lambda e: e.dma_start(CO, cols), kb=37)
        dma("sync", "ld.consts", [], "ld.consts", -96, lambda e: e.dma_start(KO, consts), kb=147)
        dma("sync", "ld.bo", [], "ld.bo", -50, lambda e: e.dma_start(BO, bo.partition_broadcast(128)), kb=128)

        raw_in = [
            ("inw", in_w, lambda W: W, INW, 1.0, 2, -100, 0, "vector"),
            ("wq0", Wq[:, :, 0:512], lambda W: W[:, :, 0:512], WQ, SCALE, 2, -5.9, 1, "vector"),
            ("wk0", Wkv[:, :, 0:512], lambda W: W[:, :, 0:512], WKV, 1.0, 2, -5.8, 2, "gpsimd"),
            ("wv0", Wkv[:, :, 1024:1536], lambda W: W[:, :, 1024:1536], WKV, 1.0, 2, -5.7, 0, "gpsimd"),
            ("wq1", Wq[:, :, 512:1024], lambda W: W[:, :, 512:1024], WQ, SCALE, 2, -5.2, 0, "vector"),
            ("wo0", Wo[:, 0:4, :], lambda W: W[:, 0:4, :], WO, 1.0, 4, -5.5, 1, "gpsimd"),
            ("wk1", Wkv[:, :, 512:1024], lambda W: W[:, :, 512:1024], WKV, 1.0, 2, -5, 1, "gpsimd"),
            ("wv1", Wkv[:, :, 1536:2048], lambda W: W[:, :, 1536:2048], WKV, 1.0, 2, -4.5, 0, "gpsimd"),
            ("wo1", Wo[:, 4:8, :], lambda W: W[:, 4:8, :], WO, 1.0, 4, -4.4, 1, "gpsimd"),
        ]
        stage_user = {}
        for tag, src, view, W, scale, a, rank, n, lo_on in raw_in:
            st = STG[n].rearrange("p (a b) -> p a b", a=a)
            before = [stage_user[n] + ".l"] if n in stage_user else []
            stage_user[n] = tag
            dma("sync", "ld." + tag, before, f"ld.stg{n}", rank - 60,
                lambda e, st=st, src=src: e.dma_start(st, src), kb=512)
            hi_lo(tag, st, view(W[0]), view(W[1]), 1024, ["ld." + tag], rank, scale, lo_on=lo_on)
        STG_FREE = ["wv1.l", "wo1.l"]

        XPR = F.take(4, 32, at=f_y2)
        OWR = F.take(256, at=f_y2 + 128)
        dma("sync", "ld.xpw", [], "ld.xpw", -85, lambda e: e.dma_start(XPR, xp_w), kb=64)
        for k in range(3):
            n = 16 if k == 1 else 17
            dma("sync", f"ld.ow{k}", [], "ld.ow", -70,
                lambda e, k=k, n=n: e.dma_start(OWR[32 * k:32 * k + n, :], out_w[0:n, :]), kb=17)
        for k in range(2):
            op("gpsimd", f"xpw.z{k}", [], 400, -90,
               lambda e, k=k: e.memset(XPW[k][:, :, 0:64].bitcast(F32), 0.0))
            op("gpsimd", f"xpw.s{k}", [], 200, -90,
               lambda e, k=k: e.memset(XPW[k][:, :, 64:80].bitcast(F32), 0.25 * (1 - k)))
            for s in range(2):
                op("gpsimd", f"kv.z{k}{s}", [], 100, -50,
                   lambda e, k=k, s=s: e.memset(KV[s][k][:, :, NK:NP].bitcast(F32), 0.0))
        for g in range(2):
            hi_lo(f"xpw{g}", XPR[:, :, 16 * g:16 * g + 16], XPW[0][:, :, 32 * g:32 * g + 16],
                  XPW[1][:, :, 32 * g:32 * g + 16], 64, ["ld.xpw", "xpw.z0", "xpw.z1"], -80, 0.5)
        op("gpsimd", "ow.z", [], 300, -70, lambda e: e.memset(OW[0:96, :].bitcast(F32), 0.0))
        op("gpsimd", "ys.z", [], 300, -70, lambda e: e.memset(YS[0:96, :].bitcast(F32), 1.0))
        for k, n in ((0, 17), (1, 16), (2, 17)):
            r = slice(32 * k, 32 * k + n)
            op("scalar", f"ow{k}", ["ld.ow2", "ow.z"], 370, -60,
               lambda e, r=r: e.activation(OW[r, :], OWR[r, :], ACT.Copy))
        op("vector", "ow.l", ["ow2"], 335, -60,
           lambda e: e.tensor_tensor(OW[64:81, :], OWR[64:81, :], OW[64:81, :].bitcast(F32), ALU.subtract))
        XPW_OK = ["xpw0.l", "xpw1.l", "xpw.s0", "xpw.s1"]
        OW_OK = ["ow0", "ow1", "ow.l", "ys.z"]

        op("gpsimd", "hp.z", [], 100, -95, lambda e: e.memset(HP[:, :, 0:3], 0.0))
        op("gpsimd", "mh", [], 100, -90, lambda e: e.memset(MH, -0.5))
        op("gpsimd", "run.z", [], 100, -50, lambda e: e.memset(RUN, 0.0))
        op("gpsimd", "init.z", [], 900, -30, lambda e: e.memset(INIT_ALL, 0.0))
        op("vector", "bqs", ["ld.cols"], 80, -50,
           lambda e: e.tensor_scalar(BQS, CO[:, C_BQ:C_BQ + H], SCALE, None, ALU.mult))
        op("vector", "hxb", ["ld.cols"], 80, -80,
           lambda e: e.tensor_scalar(HXB, CO[:, C_XPB:C_XPB + 1], 0.5, None, ALU.mult))
        op("vector", "tri", ["ld.consts"], 100, -40,
           lambda e: e.tensor_copy(TRI[:, :], KO[:, K_TRI:K_TRI + 128]))
        op("vector", "one", [], 100, -40, lambda e: e.memset(ONE[:, :], 1.0))
        op("vector", "init.id", ["init.z", "ld.consts"], 80, -30,
           lambda e: e.tensor_copy(INIT[:, :, 256:257], KO[:, K_DUMP:K_DUMP + CT].unsqueeze(2)))
        for n in range(E):
            dma("sync", f"init.{n}", ["init.id"], "init", -20,
                lambda e, n=n: e.dma_start(xs[n * CAP:(n + 1) * CAP, :].rearrange("(t p) n -> p t n", p=128), INIT), kb=136 * CT)
        dma("sync", "init.acc", ["init.id"], "init", -20,
            lambda e: e.dma_start(acc[NT:NT + CAP, :].rearrange("(t p) n -> p t n", p=128), INIT[:, :, 0:256]), kb=128 * CT)
        INIT_OK = "init.acc"


        def norm(tag, kind, src, dst, waits, rank, free=(), again=(), rows=128, tiles=2,
                 on=("vector", "scalar")):
            st, mv, rs, nr = stats[kind]
            r = slice(0, rows)
            ag = list(again)
            for t in range(tiles):
                op("vector", f"{tag}.s{t}", [*waits, *ag], 345, rank,
                   lambda e, t=t: e.bn_stats(st[r, t, :], src(t)))
                op("vector", f"{tag}.m{t}", [f"{tag}.s{t}", *ag], 80, rank,
                   lambda e, t=t: e.bn_aggr(mv[r, t, :], st[r, t, :]))
            op("vector", f"{tag}.v", [f"{tag}.m{t}" for t in range(tiles)] + ag, 80, rank,
               lambda e: e.tensor_scalar(rs[r, 0:tiles], mv[r, 0:tiles, 1], EPS, None, ALU.add))
            op("gpsimd", f"{tag}.r", [f"{tag}.v", "mh"], 640, rank,
               lambda e: e.tensor_tensor(rs[r, 0:tiles], rs[r, 0:tiles], MH[r, 0:tiles], ALU.pow))
            if "scalar" in on[0:tiles]:
                op("vector", f"{tag}.n", [f"{tag}.r", *ag], 80, rank,
                   lambda e: e.scalar_tensor_tensor(nr[r, 0:tiles], mv[r, 0:tiles, 0], -1.0, rs[r, 0:tiles],
                                                    ALU.mult, ALU.mult))
            for t in range(tiles):
                if on[t] == "scalar":
                    op("scalar", f"{tag}.a{t}", [f"{tag}.n", *free], 409, rank,
                       lambda e, t=t: e.activation(dst(t), src(t), ACT.Identity, bias=nr[r, t:t + 1],
                                                   scale=rs[r, t:t + 1]))
                    continue
                op("vector", f"{tag}.a{t}", [f"{tag}.r", *free], 330, rank,
                   lambda e, t=t: e.tensor_scalar(dst(t), src(t), mv[r, t, 0:1], rs[r, t:t + 1],
                                                  ALU.subtract, ALU.mult))
            return [f"{tag}.a{t}" for t in range(tiles)]


        d2_order, d2_end = [], {}

        def d2(name, ends):
            d2_end[name] = ends

        for k in range(-1, NB + 1):
            n, r = k + 1, k - 1
            if n < NB:
                d2_order += [f"cT{n}", f"in{n}.0", f"in{n}.1"] if n else ["in0.0", "in0.1"]
            if r >= 0:
                d2_order += [f"rT{r}", f"lg{r}", f"lgT{r}"]
            if n < NB:
                d2_order += [f"xp{n}"]
            if r >= 0:
                d2_order += [f"cum{r}"]
            if n < NB:
                d2_order += [f"out{n}", f"zT{n}"] if n else ["out0", "cT0", "zT0"]
        d2_place = {n: k for k, n in enumerate(d2_order)}

        def d2_turn(name):
            k = d2_place[name]
            return ("turn", d2_order[k - 1]) if k else None


        def stage1(b):
            s = b % 2
            aside = "gpsimd" if b else "vector"
            rk = lambda f: 8 * (b - 1) + RK["s1"] + RK["s1x"] * f
            p = b - 1
            parts = [(0, 4)] if b else [(0, 2), (2, 4)]
            tok = slice(256 * b, 256 * b + 256)
            dma("sync", f"ld.xt{b}", [pre(b - 2, "xl{}.l", b - 2)], f"ld.xt{s}", rk(-1) - 83 if b == 0 else rk(-0.5),
                lambda e: e.dma_start(XTR[s], xT[:, tok].rearrange("(c p) n -> p c n", p=128)))
            dma("sync", f"ld.x{b}", [pre(b - 2, "y1{}", b - 2)], f"ld.x{s}", rk(-0.5),
                lambda e: e.dma_start(XR[s], x[tok, :].rearrange("(t p) n -> p t n", p=128)))
            hi_lo(f"xl{b}", XTR[s], XS[0], XS[1], 512, [f"ld.xt{b}"], rk(0), free=[pre(p, "in{}.1", p)],
                  lo_on=aside)
            for j in range(2):
                def mm(e, j=j):
                    for m in (2 * j, 2 * j + 1):
                        for c in range(2):
                            w = [INW[k][:, c, 128 * m:128 * m + 128] for k in range(2)]
                            r = split3(e, D2[:, 256 * (m % 2):256 * (m % 2) + 256], w,
                                       [XS[k][:, c, :] for k in range(2)], m % 2 == 0 and c == 0, c == 1)
                    return r
                op("tensor", f"in{b}.{j}", [f"xl{b}.l", "inw.l", d2_turn(f"in{b}.{j}")], 1320, rk(0.1 + 0.1 * j), mm)
                d2(f"in{b}.{j}", [f"hp{b}.{2 * j}", f"hp{b}.{2 * j + 1}"])
                for m in (2 * j, 2 * j + 1):
                    op("scalar", f"hp{b}.{m}", [f"in{b}.{j}", "ld.cols", pre(p, "z{}.{}.3", p, m)], 420,
                       rk(0.1 + 0.1 * j),
                       lambda e, m=m: e.activation(HP[:, m, 3:259], D2[:, 256 * (m % 2):256 * (m % 2) + 256],
                                                   ACT.Identity, bias=CO[:, C_INB + m:C_INB + m + 1]))
                    cw = lambda k, m=m: CO[:, C_CW + 4 * m + k:C_CW + 4 * m + k + 1]
                    op("gpsimd", f"z{b}.{m}.0", [f"hp{b}.{m}", "hp.z", "ld.cols", *[f"g{p}.{k}" for k in (range(2) if b == 1 else range(1 if b else 0))]], 540, rk(0.2),
                       lambda e, m=m, cw=cw: e.tensor_scalar(Z[:, m, :], HP[:, m, 3:259], cw(3),
                                                             CO[:, C_CB + m:C_CB + m + 1], ALU.mult, ALU.add))
                    for k in range(1, 4):
                        if m == 3 and b:
                            op("gpsimd", f"zp{b}.{k}", [f"hp{b}.{m}", f"z{b}.3.{k - 1}"], 457, rk(0.2),
                               lambda e, m=m, k=k, cw=cw: e.tensor_scalar(ZP, HP[:, m, 3 - k:259 - k], cw(3 - k), 0.0,
                                                                          ALU.mult, ALU.add))
                            op("gpsimd", f"z{b}.{m}.{k}", [f"zp{b}.{k}"], 700, rk(0.2),
                               lambda e, m=m: e.tensor_tensor(Z[:, m, :], Z[:, m, :], ZP, ALU.add))
                            continue
                        op("vector", f"z{b}.{m}.{k}", [f"z{b}.{m}.{k - 1}"], 396, rk(0.2),
                           lambda e, m=m, k=k, cw=cw: e.scalar_tensor_tensor(
                               Z[:, m, :], HP[:, m, 3 - k:259 - k], cw(3 - k), Z[:, m, :], ALU.mult, ALU.add))
            for k, (m0, m1) in enumerate(parts):
                n, ms = 256 * (m1 - m0), slice(m0, m1)
                op("scalar", f"th{b}.{k}", [f"z{b}.{m}.3" for m in range(m0, m1)] + [f"gs{p}.{j}.l" for j in (range(2) if b == 1 else range(1 if b else 0))], ac(n),
                   rk(0.4), lambda e, ms=ms: e.activation(TH[:, ms, :], Z[:, ms, :], ACT.Tanh, scale=0.5))
                op("vector", f"g{b}.{k}", [f"th{b}.{k}"], tc(n), rk(0.4),
                   lambda e, ms=ms: e.scalar_tensor_tensor(TH[:, ms, :], TH[:, ms, :], 1.0, Z[:, ms, :],
                                                           ALU.add, ALU.mult))
                hi_lo(f"gs{b}.{k}", TH[:, ms, :], GS[0][:, ms, :], GS[1][:, ms, :], n, [f"g{b}.{k}"], rk(0.45),
                      free=[pre(p, "xp{}", p)], lo_on=aside)

            def xp(e):
                for m in range(4):
                    r = split3(e, D2[0:80, 0:256], [XPW[k][:, m, :] for k in range(2)],
                               [GS[k][:, m, :] for k in range(2)], m == 0, m == 3)
                return r
            op("tensor", f"xp{b}", [*[f"gs{b}.{k}.l" for k in range(len(parts))], *XPW_OK, d2_turn(f"xp{b}")], 1320, rk(0.5), xp)
            d2(f"xp{b}", [f"ea{b}", f"tb{b}", f"zb{b}", f"bb{b}"])
            op("scalar", f"ea{b}", [f"xp{b}", pre(p, "scan{}", p)], 420, rk(0.5),
               lambda e: e.activation(A[0:16, :], D2[0:16, 0:256], ACT.Exp, bias=CO[0:16, C_XPB:C_XPB + 1]))
            op("scalar", f"tb{b}", [f"xp{b}", "hxb", pre(p, "u{}", p)], 420, rk(0.5),
               lambda e: e.activation(TB[0:16, :], D2[32:48, 0:256], ACT.Tanh, scale=0.5, bias=HXB[32:48, :]))
            op("scalar", f"a{b}", [f"ea{b}"], 370, rk(0.5),
               lambda e: e.activation(A[0:16, :], A[0:16, :], ACT.Exp, scale=-1.0))
            op("vector", f"zb{b}", [f"tb{b}", pre(p, "scan{}", p)], 390, rk(0.5),
               lambda e: e.tensor_scalar(ZB[0:16, :], D2[32:48, 0:256], CO[32:48, C_XPB:C_XPB + 1], None, ALU.add))
            op("vector", f"u{b}", [f"tb{b}", f"zb{b}"], 335, rk(0.5),
               lambda e: e.scalar_tensor_tensor(ZB[0:16, :], TB[0:16, :], 1.0, ZB[0:16, :], ALU.add, ALU.mult))
            op("vector", f"bb{b}", [f"u{b}"], 335, rk(0.5),
               lambda e: e.tensor_tensor(ZB[0:16, :], D2[64:80, 0:256], ZB[0:16, :], ALU.mult))
            op("vector", f"scan{b}", [f"a{b}", f"bb{b}", pre(p, "ys{}.l", p)], 335, rk(0.5),
               lambda e: e.tensor_tensor_scan(YF[0:16, :], A[0:16, :], ZB[0:16, :], 0.0, ALU.mult, ALU.add))
            for k in (0, 2):
                op("scalar", f"yh{b}.{k}", [f"scan{b}", "ys.z", pre(p, "out{}", p)], 370, rk(0.55),
                   lambda e, k=k: e.activation(YS[32 * k:32 * k + 16, :], YF[0:16, :], ACT.Copy))
            op("vector", f"ys{b}.l", [f"yh{b}.0", "ys.z", pre(p, "out{}", p)], 335, rk(0.55),
               lambda e: e.tensor_tensor(YS[32:48, :], YF[0:16, :], YS[0:16, :].bitcast(F32), ALU.subtract))

            def mo(e):
                for t in range(2):
                    r = e.matmul(D2[:, 256 * t:256 * t + 256], YS[0:96, 128 * t:128 * t + 128], OW[0:96, :],
                                 start=t == 0, stop=True, skip_group_check=True)
                return r
            op("tensor", f"out{b}", [f"ys{b}.l", f"yh{b}.2", *OW_OK, d2_turn(f"out{b}")], 220, rk(0.6), mo)
            d2(f"out{b}", [f"y1{b}"])
            op("vector", f"y1{b}", [f"out{b}", f"ld.x{b}", *([f"n1{p}.{k}" for k in ("x0", "x1", "z0", "z1")] if b else [])], 600, rk(0.6),
               lambda e: e.tensor_tensor(Y1.rearrange("p t n -> p (t n)"), D2,
                                         XR[s].rearrange("p t n -> p (t n)"), ALU.add))
            st, mv, rs, nr = stats["a"]
            again = [f"n1{p}.{k}" for k in ("x0", "x1", "z0", "z1")] if b else []
            for t in range(2):
                op("vector", f"n1{b}.s{t}", [f"y1{b}", *again], 335, rk(0.65),
                   lambda e, t=t: e.bn_stats(st[:, t, :], Y1[:, t, :]))
                op("vector", f"n1{b}.m{t}", [f"n1{b}.s{t}", *again], 75, rk(0.65),
                   lambda e, t=t: e.bn_aggr(mv[:, t, :], st[:, t, :]))
            ms = [f"n1{b}.m0", f"n1{b}.m1"]
            op("vector", f"n1{b}.v", ms + again, 71, rk(0.65),
               lambda e: e.tensor_scalar(rs[:, 0:2], mv[:, :, 1], EPS, None, ALU.add))
            op("vector", f"n1{b}.w", ms + again, 71, rk(0.65),
               lambda e: e.tensor_scalar(rs[:, 2:4], mv[:, :, 1], 1.0 + EPS, EPS * EPS, ALU.mult, ALU.add))
            op("gpsimd", f"n1{b}.r", [f"n1{b}.v", f"n1{b}.w", "mh"], 640, rk(0.65),
               lambda e: e.tensor_tensor(rs, rs, MH, ALU.pow))
            op("vector", f"n1{b}.n", [f"n1{b}.r", *again], 80, rk(0.65),
               lambda e: e.scalar_tensor_tensor(nr.rearrange("p (a b) -> p a b", a=2),
                                                mv[:, :, 0].unsqueeze(1).to_broadcast([128, 2, 2]), -1.0,
                                                rs.rearrange("p (a b) -> p a b", a=2), ALU.mult, ALU.mult))
            for k, dst, on in (("z", Z1, ("vector", "scalar")), ("x", X1B[b % 3], ("scalar", "scalar"))):
                old = [pre(p, "zT{}", p), "wk0.l"] if k == "z" else [pre(b - 3, "y2{}", b - 3), *STG_FREE]
                f = rk(0.68) if k == "z" else rk(0.8)
                for t in range(2):
                    c = t if k == "x" else 2 + t
                    if on[t] == "scalar":
                        op("scalar", f"n1{b}.{k}{t}", [f"n1{b}.n", *old], 409, f,
                           lambda e, t=t, c=c, dst=dst: e.activation(dst[:, t, :], Y1[:, t, :], ACT.Identity,
                                                                     bias=nr[:, c:c + 1], scale=rs[:, c:c + 1]))
                        continue
                    op("vector", f"n1{b}.{k}{t}", [f"n1{b}.r", *old], 323, f,
                       lambda e, t=t, c=c, dst=dst: e.tensor_scalar(dst[:, t, :], Y1[:, t, :], mv[:, t, 0:1],
                                                                    rs[:, c:c + 1], ALU.subtract, ALU.mult))
            n2 = [f"n1{b}.z0", f"n1{b}.z1"]
            X1 = X1B[b % 3]
            op("gpsimd", f"x1b{b}", [f"n1{b}.x0", f"n1{b}.x1", "ld.bo"], 1230, rk(0.8),
               lambda e: e.tensor_tensor(X1, X1, BO.unsqueeze(1).to_broadcast([128, 2, 256]), ALU.add))

            def zt(e):
                for c in range(2):
                    for t in range(2):
                        r = e.transpose(D2[:, 256 * c + 128 * t:256 * c + 128 * t + 128],
                                        Z1[:, t, 128 * c:128 * c + 128], ident)
                return r
            op("tensor", f"zT{b}", [*n2, "ld.consts", d2_turn(f"zT{b}")], 450, rk(0.75), zt)
            d2(f"zT{b}", [f"lt{b}.0", f"lt{b}.1"])
            for c in range(2):
                op("vector", f"lt{b}.{c}", [f"zT{b}", "ld.cols", "wk0.l", pre(p, "kv{}.l", p)], 455, rk(0.75),
                   lambda e, c=c: e.tensor_scalar(LT[:, c, :], D2[:, 256 * c:256 * c + 256],
                                                  CO[:, C_GL + c:C_GL + c + 1], CO[:, C_BL + c:C_BL + c + 1],
                                                  ALU.mult, ALU.add))
            q = 8 * (b - 2) + 7
            old = [pre(b - 2, w, q) for w in ("Q{}", "K{}")] + [pre(b - 2, w, q // 2) for w in ("V{}", "Vc{}")]
            hi_lo(f"kv{b}", LT, KV[s][0][:, :, 0:256], KV[s][1][:, :, 0:256], 512,
                  [f"lt{b}.0", f"lt{b}.1"], rk(0.8), free=old, lo_on=aside)

            dma("sync", f"ld.c{b}", [pre(p, "nc{}.a0", p)], "ld.c", rk(-0.5),
                lambda e: e.dma_start(CR[0:NC, :], ctx_in[b]), kb=77)
            n3 = norm(f"nc{b}", "c", lambda t: CR[0:NC, :], lambda t: CZ[0:NC, :], [f"ld.c{b}"], rk(0),
                      free=[pre(p, "cT{}", p)], again=[pre(p, "nc{}.a0", p)], rows=NC, tiles=1)

            def ct(e):
                for c in range(2):
                    r = e.transpose(D2[:, NC * c:NC * c + NC], CZ[0:NC, 128 * c:128 * c + 128],
                                    KO[0:NC, K_ID:K_ID + NC])
                return r
            op("tensor", f"cT{b}", [*n3, "ld.consts", d2_turn(f"cT{b}")], 130, rk(0), ct)
            d2(f"cT{b}", [f"ct{b}.0", f"ct{b}.1"])
            for c in range(2):
                op("vector", f"ct{b}.{c}", [f"cT{b}", "ld.cols", pre(p, "kc{}.l", p)], 270, rk(0),
                   lambda e, c=c: e.tensor_scalar(CTX[:, c, :], D2[:, NC * c:NC * c + NC],
                                                  CO[:, C_GM + c:C_GM + c + 1], CO[:, C_BM + c:C_BM + c + 1],
                                                  ALU.mult, ALU.add))
            hi_lo(f"kc{b}", CTX, KV[s][0][:, :, 256:NK], KV[s][1][:, :, 256:NK], 154,
                  [f"ct{b}.0", f"ct{b}.1"], rk(0.1), free=old)


        def head(b, h):
            i = 8 * b + h
            s, s2, half = b % 2, i % 2, h // 4
            kv = KV[s]
            Qb, Kb, Pb, Ob = QS[i % 3], KS[i % 3], PM[s2], OS[s2]
            pr = i // 2
            Vb = VS[pr % 2]
            ready = [f"kv{b}.l", f"kv.z0{s}", f"kv.z1{s}"]

            def proj(e, W, off, dst, n):
                for c in range(2):
                    r = split3(e, dst[:, 0:n], [W[k][:, c, off:off + 128] for k in range(2)],
                               [kv[k][:, c, 0:n] for k in range(2)], c == 0, c == 1)
                return r
            first = i % 2 == 0
            op("tensor", f"Q{i}", [*ready, f"wq{half}.l", pre(i - 1, "q{}.l", i - 1) if first else f"vl{pr}"],
               660, i + RK["Q"], lambda e: proj(e, WQ, 128 * h, D0, 256))
            op("scalar", f"q{i}.h", [f"Q{i}", "bqs", pre(i - 3, "S{}.1", i - 3)], 358, i + RK["q"],
               lambda e: e.activation(Qb[0], D0[:, 0:256], ACT.Identity, bias=BQS[:, h:h + 1]))
            op("vector", f"q{i}.l", [f"q{i}.h"], 400, i + RK["q"],
               lambda e: e.scalar_tensor_tensor(Qb[1], D0[:, 0:256], BQS[:, h:h + 1], Qb[0].bitcast(F32),
                                                ALU.add, ALU.subtract))
            op("tensor", f"K{i}", [*ready, f"kc{b}.l", f"wk{half}.l",
                                   pre(i - 1, "k{}.l", i - 1) if first else f"vcl{pr}"],
               850, i + RK["Q"], lambda e: proj(e, WKV, 128 * h, D1, NP))
            bk = CO[:, C_BKV + h:C_BKV + h + 1]
            op("scalar", f"k{i}.h", [f"K{i}", pre(i - 3, "S{}.1", i - 3)], 424, i + RK["q"],
               lambda e: e.activation(Kb[0], D1[:, 0:NP], ACT.Identity, bias=bk))
            op("vector", f"k{i}.l", [f"k{i}.h"], 480, i + RK["q"],
               lambda e: e.scalar_tensor_tensor(Kb[1], D1[:, 0:NP], bk, Kb[0].bitcast(F32), ALU.add, ALU.subtract))
            if first:
                vo = 1024 + 128 * h

                def vproj(e, dst, a, m, one):
                    for c in range(2):
                        r = split3(e, dst, [kv[k][:, c, a:a + m] for k in range(2)],
                                   [WKV[k][:, c, vo:vo + 256] for k in range(2)], c == 0 and one, c == 1)
                    return r

                def v01(e):
                    vproj(e, D0[:, 0:256], 0, 128, True)
                    return vproj(e, D0[:, 256:512], 128, 128, False)
                vfree = pre(pr - 2, "PV{}", 2 * (pr - 2) + 1)
                op("tensor", f"V{pr}", [*ready, f"wv{half}.l", f"q{i}.l"], 1310, i + RK["V"], v01)
                op("scalar", f"vh{pr}", [f"V{pr}", vfree], 520, i + RK["v"],
                   lambda e: e.activation(Vb[0][:, 0:2, :], D0.rearrange("p (a b) -> p a b", a=2), ACT.Copy))
                op("vector", f"vl{pr}", [f"vh{pr}"], 600, i + RK["v"],
                   lambda e: e.tensor_tensor(Vb[1][:, 0:2, :], D0.rearrange("p (a b) -> p a b", a=2),
                                             Vb[0][:, 0:2, :].bitcast(F32), ALU.subtract))
                op("tensor", f"Vc{pr}", [*ready, f"kc{b}.l", f"wv{half}.l", f"k{i}.l"], 655, i + RK["V"],
                   lambda e: vproj(e, D1[0:NC, 0:256], 256, NC, True))
                op("scalar", f"vch{pr}", [f"Vc{pr}", vfree], 307, i + RK["v"],
                   lambda e: e.activation(Vb[0][0:NC, 2, :], D1[0:NC, 0:256], ACT.Copy))
                op("vector", f"vcl{pr}", [f"vch{pr}"], 335, i + RK["v"],
                   lambda e: e.tensor_tensor(Vb[1][0:NC, 2, :], D1[0:NC, 0:256], Vb[0][0:NC, 2, :].bitcast(F32),
                                             ALU.subtract))
            nm, rs = NM[:, s2, :], RS[:, s2, :]
            for t in range(2):
                op("tensor", f"S{i}.{t}", [f"q{i}.l", f"k{i}.l", pre(i - 1, "x{}.{}", i - 1, t)], 420, i + RK["S"],
                   lambda e, t=t: split3(e, SA[t][:, 0:NP], [Qb[k][:, 128 * t:128 * t + 128] for k in range(2)],
                                         Kb, True, True))
                op("vector", f"m{i}.{t}", [f"S{i}.{t}", pre(i - 2, "x{}.{}", i - 2, t)], 411, i + RK["m"],
                   lambda e, t=t: e.tensor_reduce(nm[:, t:t + 1], SA[t][:, 0:NK], AX.X, ALU.max, negate=True))
                op("scalar", f"x{i}.{t}", [f"m{i}.{t}", pre(i - 2, "T{}.0", i - 2), pre(i - 2, "T{}.1", i - 2), pre(i - 2, "r{}", i - 2),
                                           *STG_FREE], 515, i + RK["x"],
                   lambda e, t=t: e.activation(Pb[:, t, 0:NK], SA[t][:, 0:NK], ACT.Exp, bias=nm[:, t:t + 1],
                                               accum_out=rs[:, t:t + 1]))
            op("vector", f"r{i}", [f"x{i}.0", f"x{i}.1"], 85, i + RK["r"], lambda e: e.reciprocal(rs, rs))
            for t in range(2):
                op("gpsimd", f"p{i}.{t}", [f"r{i}"], 522, i + RK["r"],
                   lambda e, t=t: e.tensor_scalar(Pb[:, t, 0:NK], Pb[:, t, 0:NK], rs[:, t:t + 1], 0.0,
                                                  ALU.mult, ALU.add))

            Tb = PTS[s2]
            for u, (k0, k1, n, cost) in enumerate(((0, 2, 128, 440), (2, 3, NC, 220))):
                def tr(e, k0=k0, k1=k1, n=n):
                    for k in range(k0, k1):
                        for t in range(2):
                            r = e.transpose(PT[0:n, 256 * k + 128 * t:256 * k + 128 * t + 128],
                                            Pb[:, t, 128 * k:128 * k + n], ident)
                    return r
                c = slice(256 * k0, 256 * k1)
                op("tensor", f"T{i}.{u}", [f"p{i}.0", f"p{i}.1", pre(i - 1, "o{}.l" if u else "pt{}.0.l", i - 1)],
                   cost, i + RK["T"], tr)
                op("scalar", f"pt{i}.{u}.h", [f"T{i}.{u}", pre(i - 2, "PV{}", i - 2)], ac(256 * (k1 - k0)), i + RK["pt"],
                   lambda e, n=n, c=c: e.activation(Tb[0][0:n, c], PT[0:n, c], ACT.Copy))
                op("vector", f"pt{i}.{u}.l", [f"pt{i}.{u}.h"], tc(256 * (k1 - k0)), i + RK["pt"],
                   lambda e, n=n, c=c: e.tensor_tensor(Tb[1][0:n, c], PT[0:n, c], Tb[0][0:n, c].bitcast(F32),
                                                       ALU.subtract))

            def pv(e):
                for k in range(3):
                    n = 128 if k < 2 else NC
                    c0 = 128 * (h % 2)
                    r = split3(e, PO, [Vb[j][0:n, k, c0:c0 + 128] for j in range(2)],
                               [Tb[j][0:n, 256 * k:256 * k + 256] for j in range(2)], k == 0, k == 2)
                return r
            op("tensor", f"PV{i}", [f"pt{i}.0.l", f"pt{i}.1.l", f"vl{pr}", f"vcl{pr}"], 980, i + RK["PV"], pv)
            bv = CO[:, C_BKV + 8 + h:C_BKV + 9 + h]
            op("scalar", f"o{i}.h", [f"PV{i}", pre(i - 2, "W{}", i - 2)], 358, i + RK["o"],
               lambda e: e.activation(Ob[0], PO, ACT.Identity, bias=bv))
            op("vector", f"o{i}.l", [f"o{i}.h"], 400, i + RK["o"],
               lambda e: e.scalar_tensor_tensor(Ob[1], PO, bv, Ob[0].bitcast(F32), ALU.add, ALU.subtract))

            def mw(e):
                for t in range(2):
                    r = split3(e, PW[:, 256 * t:256 * t + 256], [Ob[k][:, 128 * t:128 * t + 128] for k in range(2)],
                               [WO[k][:, h, :] for k in range(2)], h == 0 and t == 0, h == 7)
                return r
            op("tensor", f"W{i}", [f"o{i}.l", f"wo{half}.l", pre(b - 1, "y2{}", b - 1) if h == 0 else None],
               655, i + RK["W"], mw)


        def route(b):
            s, p = b % 2, b - 1
            X = X2E[s]
            rk = lambda f: 8 * b + RK["rt"] + RK["rtx"] * f
            free = [pre(b - 2, "st{}", b - 2)] + [pre(b - 2, "sc{}.{}", b - 2, k) for k in range(4)]
            if b < 2:
                free = [INIT_OK]
            op("vector", f"y2{b}", [f"W{8 * b + 7}", f"x1b{b}", pre(p, "n4{}.a1", p), pre(p, "n4{}.a0", p),
                                    "xpw0.l", "xpw1.l", "ow.l"], 600, rk(0) - 1,
               lambda e: e.tensor_tensor(Y2.rearrange("p t n -> p (t n)"), PW,
                                         X1B[b % 3].rearrange("p t n -> p (t n)"), ALU.add))
            n4 = norm(f"n4{b}", "d", lambda t: Y2[:, t, :], lambda t: X[:, t, 0:256], [f"y2{b}"], rk(0),
                      free=free, again=[pre(p, "n4{}.a0", p), pre(p, "n4{}.a1", p)])
            dma("sync", f"st{b}", n4, f"st{s}", rk(0), lambda e: e.dma_start(
                acc[256 * b:256 * b + 256, :].rearrange("(t p) n -> p t n", p=128), X[:, :, 0:256]))
            op("vector", f"id{b}", [*n4, *free, "ld.consts"], 80, rk(0),
               lambda e: e.tensor_scalar(X[:, :, 256], KO[:, K_TOK:K_TOK + 2], 256.0 * b, None, ALU.add))

            def rt(e):
                for c in range(2):
                    for t in range(2):
                        r = e.transpose(D2[:, 256 * c + 128 * t:256 * c + 128 * t + 128],
                                        X[:, t, 128 * c:128 * c + 128], ident)
                return r
            op("tensor", f"rT{b}", [*n4, d2_turn(f"rT{b}")], 450, rk(0.1), rt)
            d2(f"rT{b}", [f"x2t{b}"])
            op("scalar", f"x2t{b}", [f"rT{b}", pre(p, "lg{}", p), "xpw0.l", "xpw1.l", "ow.l"], 580, rk(0.1),
               lambda e: e.activation(X2T.rearrange("p c n -> p (c n)"), D2, ACT.Copy))

            def lg(e):
                for c in range(2):
                    r = e.matmul(D2[0:8, 0:256], CO[:, C_E + 8 * c:C_E + 8 * c + 8], X2T[:, c, :],
                                 start=c == 0, stop=c == 1)
                return r
            op("tensor", f"lg{b}", [f"x2t{b}", d2_turn(f"lg{b}")], 870, rk(0.2), lg)
            d2(f"lg{b}", [f"lgc{b}"])
            op("vector", f"lgc{b}", [f"lg{b}", pre(p, "lgT{}", p)], 335, rk(0.2),
               lambda e: e.tensor_copy(LGT[0:8, :], D2[0:8, 0:256]))

            def lt(e):
                for t in range(2):
                    r = e.transpose(D2[:, 8 * t:8 * t + 8], LGT[0:8, 128 * t:128 * t + 128], KO[0:8, K_ID:K_ID + 8])
                return r
            op("tensor", f"lgT{b}", [f"lgc{b}", d2_turn(f"lgT{b}")], 100, rk(0.3), lt)
            d2(f"lgT{b}", [f"l8{b}"])
            v = lambda name, waits, issue, f=0.4, cost=90: op("vector", f"{name}{b}", waits, cost, rk(f), issue)
            n = lambda name: f"{name}{b}"
            o = lambda name: pre(p, "{}{}", name, p)
            iota = KO[:, K_IOTA:K_IOTA + 8]
            v("l8", [n("lgT"), o("ix1.")], lambda e: e.tensor_copy(LG, D2[:, 0:16].rearrange("p (a b) -> p a b", a=2)))
            for t in range(2):
                v(f"mx{t}.", [n("l8"), o("d")], lambda e, t=t: e.max(M8[:, t, :], LG[:, t, :]))
                v(f"ix{t}.", [n(f"mx{t}."), o("if")], lambda e, t=t: e.max_index(I8[:, t, :], M8[:, t, :], LG[:, t, :]))
            v("if", [n("ix0."), n("ix1."), o("oh1.1.")], lambda e: e.tensor_copy(IF, I8[:, :, 0:2]))
            v("d", [n("mx0."), n("mx1."), o("e")],
              lambda e: e.tensor_tensor(DW[:, :, 0], M8[:, :, 1], M8[:, :, 0], ALU.subtract))
            op("scalar", n("e"), [n("d"), o("w2"), o("dn")], 95, rk(0.4),
               lambda e: e.activation(DW[:, :, 1], DW[:, :, 0], ACT.Exp))
            v("dn", [n("e"), o("w1")], lambda e: e.tensor_scalar(DW[:, :, 0], DW[:, :, 1], 1.0, None, ALU.add))
            v("w1", [n("dn"), o("w81.")], lambda e: e.reciprocal(DW[:, :, 2], DW[:, :, 0]))
            v("w2", [n("w1"), o("w81.")], lambda e: e.tensor_tensor(DW[:, :, 3], DW[:, :, 1], DW[:, :, 2], ALU.mult))
            v("gt", [n("e"), o("oh0.1."), o("oh1.1.")],
              lambda e: e.tensor_scalar(GT, DW[:, :, 1], 0.0, None, ALU.is_gt))
            for t in range(2):
                v(f"oh{t}.0.", [n("if"), o("pr0.")],
                  lambda e, t=t: e.tensor_scalar(OH[:, 0, t, :], iota, IF[:, t, 0:1], None, ALU.is_equal))
                v(f"oh{t}.1.", [n("if"), n("gt"), o("pr1.")],
                  lambda e, t=t: e.tensor_scalar(OH[:, 1, t, :], iota, IF[:, t, 1:2], GT[:, t:t + 1],
                                                 ALU.is_equal, ALU.mult))
            ohs = [n(f"oh{t}.{j}.") for t in range(2) for j in range(2)]
            v("ob", [*ohs, o("cum")], lambda e: e.tensor_tensor(OHB[:, :, :], OH[:, 0], OH[:, 1], ALU.add))
            for t in range(2):
                w8 = X[:, t, 257:265]
                v(f"wa{t}.", [n(f"oh{t}.0."), n("w1"), *free],
                  lambda e, t=t, w8=w8: e.tensor_scalar(w8, OH[:, 0, t, :], DW[:, t, 2:3], None, ALU.mult))
                v(f"w8{t}.", [n(f"wa{t}."), n(f"oh{t}.1."), n("w2")],
                  lambda e, t=t, w8=w8: e.scalar_tensor_tensor(w8, OH[:, 1, t, :], DW[:, t, 3:4], w8,
                                                               ALU.mult, ALU.add))

            def cum(e):
                m = lambda dst, w, t, a, z: e.matmul(D2[:, 8 * dst:8 * dst + 8], w[:, :], OHB[:, t, :], start=a,
                                                     stop=z, skip_group_check=True)
                m(0, TRI, 0, True, True)
                m(1, ONE, 0, False, False)
                m(1, TRI, 1, False, True)
                m(2, ONE, 0, False, False)
                return m(2, ONE, 1, False, True)
            op("tensor", n("cum"), [n("ob"), "tri", "one", d2_turn(f"cum{b}")], 130, rk(0.5), cum)
            d2(f"cum{b}", [n("pos"), n("run")])
            v("pos", [n("cum"), o("run"), "run.z", o("pr1."), o("pr0.")], lambda e: e.tensor_tensor(
                V8, D2[:, 0:16].rearrange("p (a b) -> p a b", a=2),
                RUN.unsqueeze(1).to_broadcast([128, 2, 8]), ALU.add), 0.5)
            v("run", [n("pos")], lambda e: e.tensor_tensor(RUN, RUN, D2[:, 16:24], ALU.add), 0.5)
            v("g8", [n("pos"), o("v8")], lambda e: e.scalar_tensor_tensor(
                G8, V8, 1.0 / FAR, KO[:, K_BASE:K_BASE + 16].rearrange("p (a b) -> p a b", a=2),
                ALU.mult, ALU.add), 0.5)
            v("v8", [n("g8")], lambda e: e.scalar_tensor_tensor(V8, V8, float(CAP), G8, ALU.is_gt, ALU.add), 0.5)
            for j in range(2):
                v(f"pr{j}.", [n("v8"), *ohs, o("sl")],
                  lambda e, j=j: e.tensor_tensor(PR[:, j], OH[:, j], V8, ALU.mult), 0.5)
            v("sl", [n("pr0."), n("pr1."), o("sx")],
              lambda e: e.tensor_reduce(SL.rearrange("p a b -> p (a b)"), PR.rearrange("p a b c -> p (a b) c"),
                                        AX.X, ALU.add), 0.5)
            old = [pre(b - 2, "sc{}.{}", b - 2, k) for k in range(4)]
            v("sx", [n("sl"), *old], lambda e: e.tensor_scalar(
                IX[:, s, :], SL.rearrange("p a b -> p (a b)"), FAR, FAR, ALU.mult, ALU.add), 0.5)
            for k in range(4):
                dma("gpsimd", f"sc{b}.{k}", [n("sx"), *n4, n("id"), n("w80."), n("w81."), INIT_OK], f"sc{s}",
                    rk(0.6), lambda e, k=k: e.indirect_dma_start(
                        out=xs, out_offset=bass.IndirectOffsetOnAxis(ap=IX[:, s, k:k + 1], axis=0),
                        in_=X[:, k % 2, :], in_offset=None, bounds_check=NT - 1, oob_is_err=False), cost=1050,
                    kb=136)


        lastq = NI - 1
        S1_DONE = [f"out{NB - 1}", f"y1{NB - 1}", f"gs{NB - 1}.0.l", f"ys{NB - 1}.l", f"xp{NB - 1}"]
        QKV_DONE = [f"Q{lastq}", f"K{lastq}", f"V{lastq // 2}", f"Vc{lastq // 2}"]
        ROUTED = [f"sc{b}.{k}" for b in (NB - 2, NB - 1) for k in range(4)]
        W1B = [5, 6, 7, 4]

        def expert(g):
            s = g % 2
            X, Y, IH, W1, W2 = XSL[s], YO[s], FI[s], FW1[s], FW2[s]
            rk = lambda f: 8 * NB + 10 + 8 * g + 8 * f
            start = S1_DONE if s == 0 else [*QKV_DONE, *S1_DONE]
            p = g - 1
            for k, (raw, src, W, after) in enumerate(((RW1[s], w1[g], W1, "U"), (RW2[s], w2[g], W2, "Y"))):
                dma("sync", f"ld.f{g}.{k}", [*S1_DONE, pre(g - 2, "fw{}.{}.l", g - 2, k)], f"ld.f{s}{k}", rk(-2),
                    lambda e, raw=raw, src=src: e.dma_start(raw, src), kb=512)
                last = f"U{g - 2}.3" if k == 0 else f"Y{g - 2}.{CT - 1}"
                hi_lo(f"fw{g}.{k}", raw, W[0], W[1], 1024, [f"ld.f{g}.{k}"], rk(-1.2),
                      free=start if g < 2 else [last], lo_on="gpsimd")
            dma("sync", f"ld.g{g}", [*ROUTED, *S1_DONE, pre(g - 2, "yo{}.{}", g - 2, CT - 1), pre(g - 2, "fT{}", g - 2),
                                     f"n4{NB - 1}.a0", pre(g - 2, "ie{}", g - 2)],
                f"ld.g{s}", rk(-1.5), lambda e: e.dma_start(
                    X, xs[g * CAP:(g + 1) * CAP, :].rearrange("(t p) n -> p t n", p=128)), kb=136 * CT)
            op("vector", f"ie{g}", [f"ld.g{g}"] + [pre(g - 2, "sa{}.{}", g - 2, t) for t in range(CT)], 90, rk(0),
               lambda e: e.tensor_copy(IE[:, s, 0:CT], X[:, :, 256]))

            def ft(e):
                for c in range(2):
                    for t in range(CT):
                        r = e.transpose(SA[c][:, 128 * t:128 * t + 128], X[:, t, 128 * c:128 * c + 128], ident)
                return r
            op("tensor", f"fT{g}", [f"ld.g{g}", pre(p, "fx{}.1.l", p), f"x{lastq}.0", f"x{lastq}.1"], 880, rk(0), ft)
            for c in range(2):
                free = QKV_DONE if g < 2 else [f"U{g - 2}.3"]
                op("scalar", f"fx{g}.{c}.h", [f"fT{g}", *free], ac(CAP), rk(0.1),
                   lambda e, c=c: e.activation(FX[s][0][:, c, :], SA[c][:, 0:CAP], ACT.Copy))
                op("vector", f"fx{g}.{c}.l", [f"fx{g}.{c}.h"], tc(CAP), rk(0.1),
                   lambda e, c=c: e.tensor_tensor(FX[s][1][:, c, :], SA[c][:, 0:CAP],
                                                  FX[s][0][:, c, :].bitcast(F32), ALU.subtract))
            for m in range(4):
                pb = bank(W1B[m])[:, 0:CAP]

                def up(e, m=m, pb=pb):
                    for c in range(2):
                        r = split3(e, pb, [W1[k][:, c, 128 * m:128 * m + 128] for k in range(2)],
                                   [FX[s][k][:, c, :] for k in range(2)], c == 0, c == 1)
                    return r
                free = [pre(p, "i{}.{}.l", p, m)] if g else [f"y2{NB - 1}", f"run{NB - 1}", f"pos{NB - 1}",
                                                            f"k{lastq}.l", f"q{lastq}.l"]
                op("tensor", f"U{g}.{m}", [f"fx{g}.0.l", f"fx{g}.1.l", f"fw{g}.0.l", *free], 1320,
                   rk(0.2 + 0.1 * m), up)
                free = [pre(g - 2, "Y{}.{}", g - 2, CT - 1)] if g > 1 else [*QKV_DONE, f"W{lastq}"]
                op("scalar", f"i{g}.{m}.h", [f"U{g}.{m}", *free], ac(CAP), rk(0.2 + 0.1 * m),
                   lambda e, m=m, pb=pb: e.activation(IH[0][:, m, :], pb, ACT.Relu))
                op("vector", f"i{g}.{m}.l", [f"i{g}.{m}.h"], tc(CAP), rk(0.2 + 0.1 * m),
                   lambda e, m=m, pb=pb: e.scalar_tensor_tensor(IH[1][:, m, :], pb, 0.0,
                                                                IH[0][:, m, :].bitcast(F32), ALU.max, ALU.subtract))
            for t in range(CT):
                pb = bank(2 + t % 2)[:, 0:256]

                def down(e, t=t, pb=pb):
                    for m in range(4):
                        r = split3(e, pb, [IH[k][:, m, 128 * t:128 * t + 128] for k in range(2)],
                                   [W2[k][:, m, :] for k in range(2)], m == 0, m == 3)
                    return r
                k = g * CT + t - 2
                free = f"yo{k // CT}.{k % CT}" if k >= 0 else f"o{lastq}.l"
                op("tensor", f"Y{g}.{t}", [f"i{g}.{m}.l" for m in range(4)] + [f"fw{g}.1.l", free], 1320,
                   rk(0.6 + 0.1 * t), down)
                op("scalar", f"yo{g}.{t}", [f"Y{g}.{t}"] + [pre(g - 2, "sa{}.{}", g - 2, k) for k in range(CT)]
                   + [f"n4{NB - 1}.a0"],
                   480, rk(0.6 + 0.1 * t), lambda e, t=t, pb=pb: e.activation(
                       Y[:, t, :], pb, ACT.Copy, scale=X[:, t, 257 + g:258 + g]))
                dma("gpsimd", f"sa{g}.{t}", [f"yo{g}.{t}", f"ie{g}"] + [pre(p, "sa{}.{}", p, k) for k in range(CT)]
                    + [f"st{NB - 1}", f"st{NB - 2}", INIT_OK],
                    f"sa{s}", rk(0.8 + 0.1 * t), lambda e, t=t: e.indirect_dma_start(
                        out=acc, out_offset=bass.IndirectOffsetOnAxis(ap=IE[:, s, t:t + 1], axis=0),
                        in_=Y[:, t, :], in_offset=None, bounds_check=NT + CAP - 1, oob_is_err=True,
                        compute_op=ALU.add), cost=1050, kb=128)


        def finish():
            added = [f"sa{g}.{t}" for g in (E - 2, E - 1) for t in range(CT)]
            st, mv, rs, nr = tail_stats
            rk = 8 * NB + 8 * E + 40
            on = ("vector", "scalar", "gpsimd", "scalar")
            for n in range(NCH):
                rows = slice(256 * n, 256 * n + 256)
                dma("sync", f"ld.a{n}", added, f"ld.a{n}", rk + n,
                    lambda e, n=n, rows=rows: e.dma_start(AC[n], acc[rows, :].rearrange("(t p) n -> p t n", p=128)))
                for t in range(2):
                    k = 2 * n + t
                    op("vector", f"f.s{k}", [f"ld.a{n}"], 345, rk + n,
                       lambda e, n=n, t=t, k=k: e.bn_stats(st[:, k, :], AC[n][:, t, :]))
                    op("vector", f"f.m{k}", [f"f.s{k}"], 80, rk + n,
                       lambda e, k=k: e.bn_aggr(mv[:, k, :], st[:, k, :]))
                c = slice(2 * n, 2 * n + 2)
                op("vector", f"f.v{n}", [f"f.m{2 * n + t}" for t in range(2)], 80, rk + n,
                   lambda e, c=c: e.tensor_scalar(rs[:, c], mv[:, c, 1], EPS, None, ALU.add))
                op("gpsimd", f"f.r{n}", [f"f.v{n}", "mh"], 640, rk + n,
                   lambda e, c=c: e.tensor_tensor(rs[:, c], rs[:, c], MH[:, 0:2], ALU.pow))
                op("vector", f"f.n{n}", [f"f.r{n}"], 80, rk + n,
                   lambda e, c=c: e.scalar_tensor_tensor(nr[:, c], mv[:, c, 0], -1.0, rs[:, c], ALU.mult, ALU.mult))
                for t in range(2):
                    k = 2 * n + t
                    g = on[k % 4]
                    a = AC[n][:, t, :]
                    if g == "scalar":
                        f = lambda e, a=a, k=k: e.activation(a, a, ACT.Identity, bias=nr[:, k:k + 1],
                                                             scale=rs[:, k:k + 1])
                    else:
                        f = lambda e, a=a, k=k: e.tensor_scalar(a, a, rs[:, k:k + 1], nr[:, k:k + 1],
                                                                ALU.mult, ALU.add)
                    op(g, f"f.o{k}", [f"f.n{n}"], 490, rk + n, f)
                dma("sync", f"st.o{n}", [f"f.o{2 * n + t}" for t in range(2)], "st.o", rk + n,
                    lambda e, n=n, rows=rows: e.dma_start(out[rows, :].rearrange("(t p) n -> p t n", p=128), AC[n]))
            op("sync", "end", [f"st.o{n}" for n in range(NCH)], 10, rk + 50, lambda e: None)

        for b in range(NB):
            stage1(b)
            for h in range(H):
                head(b, h)
            route(b)
        for g in range(E):
            expert(g)
        finish()
        for o in P.ops.values():
            flat = []
            for w in o["waits"]:
                flat += d2_end[w[1]] if isinstance(w, tuple) else [w]
            o["waits"] = flat
        P.sizes = (R.at, F.at)
        P.emit()
        return P



def layout(inputs):
    import numpy as np
    f = lambda n: np.asarray(inputs[n], dtype=np.float32)
    L = {}
    xx = f("x")
    nt = xx.shape[0] * xx.shape[1]
    cap = nt // E
    L["x"] = xx.reshape(nt, 256)
    L["xT"] = xx.reshape(nt, 256).T
    L["ctx_in"] = f("ctx_1024")
    cols = np.zeros((128, C_END), np.float32)
    part = lambda v: v.reshape(-1, 128).T
    cols[:, C_INB:C_INB + 4] = part(f("L0_attn_in_b"))
    cols[:, C_CB:C_CB + 4] = part(f("L0_attn_conv_b"))
    cols[:, C_CW:C_CW + 16] = f("L0_attn_conv_w").reshape(4, 128, 4).transpose(1, 0, 2).reshape(128, 16)
    cols[0:16, C_XPB] = f("L0_attn_xp_b")[0:16]
    cols[32:48, C_XPB] = f("L0_attn_xp_b")[16:32]
    cols[:, C_BQ:C_BQ + 8] = part(f("L0_xattn_bq"))
    cols[:, C_BKV:C_BKV + 16] = part(f("L0_xattn_bkv"))
    cols[:, C_GM:C_GM + 2] = part(f("L0_xattn_gamma_media"))
    cols[:, C_BM:C_BM + 2] = part(f("L0_xattn_beta_media"))
    cols[:, C_GL:C_GL + 2] = part(f("L0_xattn_gamma_lat"))
    cols[:, C_BL:C_BL + 2] = part(f("L0_xattn_beta_lat"))
    cols[:, C_E:C_E + 16] = f("L0_ffn_expert_embeddings").T.reshape(2, 128, 8).transpose(1, 0, 2).reshape(128, 16)
    L["cols"] = cols
    k = np.zeros((128, K_END), np.float32)
    k[:, K_ID:K_ID + 128] = np.eye(128)
    k[:, K_TRI:K_TRI + 128] = np.triu(np.ones((128, 128)))
    k[:, K_IOTA:K_IOTA + 16] = np.tile(np.arange(8), 2)
    k[:, K_BASE:K_BASE + 16] = np.tile((cap * np.arange(8) - 1 - FAR) / FAR, 2)
    k[:, K_TOK:K_TOK + 2] = np.arange(128)[:, None] + 128 * np.arange(2)
    k[:, K_DUMP:K_DUMP + 4] = nt + np.arange(128)[:, None] + 128 * np.arange(4)
    L["consts"] = k
    c = lambda w: w.reshape(-1, 128, w.shape[-1]).transpose(1, 0, 2)
    L["in_w"] = c(f("L0_attn_in_w").T)
    L["xp_w"] = c(f("L0_attn_xp_w").T)
    L["out_w"] = np.concatenate([f("L0_attn_out_w").T, f("L0_attn_out_b")[None]], 0)
    L["Wq"] = c(f("L0_xattn_Wq"))
    L["Wkv"] = c(f("L0_xattn_Wkv"))
    L["Wo"] = c(f("L0_xattn_Wo"))
    L["bo"] = f("L0_xattn_bo")
    L["w1"] = f("L0_ffn_first_linear").transpose(0, 2, 1).reshape(E, 2, 128, 512).transpose(0, 2, 1, 3)
    L["w2"] = f("L0_ffn_second_linear").transpose(0, 2, 1).reshape(E, 4, 128, 256).transpose(0, 2, 1, 3)
    return {n: np.ascontiguousarray(a) for n, a in L.items()}


_INS = ["x", "xT", "ctx_in", "cols", "consts", "in_w", "xp_w", "out_w", "Wq", "Wkv", "Wo", "bo", "w1", "w2"]


def kernel(**inputs):
    import numpy as _np
    import concourse.bacc as _bacc
    from concourse import mybir as _mybir
    from concourse.bass_utils import run_bass_kernel_spmd as _run

    nc = _bacc.Bacc("TRN2", target_bir_lowering=False, num_devices=1)
    L = layout(inputs)
    arrays, args = {}, []
    for name in _INS:
        a = L[name]
        arrays[f"in_{name}_dram"] = a
        args.append(nc.dram_tensor(f"in_{name}_dram", a.shape, _mybir.dt.from_np(a.dtype), kind="ExternalInput").ap())
    nt = L["x"].shape[0]
    args.append(nc.dram_tensor("out_0_dram", [nt, 256], F32, kind="ExternalOutput").ap())
    decoder_layer(nc, *args)
    r = _run(nc, [arrays], core_ids=[0])
    return _np.asarray(r.results[0]["out_0_dram"]).reshape(nt // 256, 256, 256)
```

```python
from contextlib import ExitStack

import concourse.bass as bass
from concourse import mybir

ACT = mybir.ActivationFunctionType
ALU = mybir.AluOpType
AX = mybir.AxisListType
F32 = mybir.dt.float32
F32R = mybir.dt.float32r
BF16 = mybir.dt.bfloat16
U32 = mybir.dt.uint32

H = 8
E = 8
NC = 77
NK = 333
NP = 334
ROW = 272
EPS = 1e-5
FAR = 65536.0
EARLY = 3

C_INB, C_CB, C_CW, C_XPB, C_BQ, C_BKV, C_GM, C_BM, C_GL, C_BL, C_E = 0, 4, 8, 24, 25, 33, 49, 51, 53, 55, 57
C_END = 73
K_ID, K_TRI, K_IOTA, K_BASE, K_TOK, K_DUMP, K_LATE = 0, 128, 256, 272, 288, 290, 294
K_END = 302


RANK = dict(Q=-1.445, K=-1.313, q=-2.375, k=-4.412, V=-0.491, Vc=-1.049, v=0.521, vc=-1.59, S=-1.461,
            m=-0.856, x=0.312, r=-0.696, T0=0.287, T1=0.185, pt0=0.543, pt1=0.115, PV=0.812, o=-0.54,
            W=1.638, s1=-2.52, s1x=10.452, rt=7.622, rtx=3.156, wt=50, wv=27.619, ws=100, wg=100, gs=1,
            kvl=0, xl=1, pc=1, fT=-0.762, b1=-0.899, b2=0.0, wq1=-0.978, wk1=-3.911, wv1=3.431, wo1=4.049,
            wo0=-5.71)


WARM0 = ["one"] * 5 + ["hp0.1", "z0.0.0", "z0.0.1", "z0.1.2", "z0.2.1", "z0.2.2", "z0.2.3",
         "th0.0", "g0.0", "th0.1", "g0.1", "gs0.0.l", "ea0", "tb0", "a0", "zb0", "bb0", "scan0", "yh0.0", "ys0.l",
         "y10", "n10.s0", "n10.s1", "n10.w", "n10.rz", "n10.nz", "n10.z0", "lt0.0"]


class Program:

    LAG = {"tensor": dict(tensor=200, scalar=197, vector=196, gpsimd=200, sync=100),
           "scalar": dict(tensor=300, scalar=150, vector=152, gpsimd=175, sync=100),
           "vector": dict(tensor=256, scalar=128, vector=127, gpsimd=155, sync=100),
           "gpsimd": dict(tensor=200, scalar=110, vector=58, gpsimd=88, sync=100),
           "sync": dict(tensor=100, scalar=100, vector=100, gpsimd=100, sync=100)}

    WAIT = dict(tensor=RANK["wt"], vector=RANK["wv"], scalar=RANK["ws"], gpsimd=RANK["wg"], sync=0.0)

    def __init__(self, nc, sem):
        self.nc = nc
        self.sem = sem
        self.ops = {}
        self.turns = {}

    def op(self, engine, name, waits, cost, rank, issue):
        assert name not in self.ops, name
        self.ops[name] = dict(engine=engine, name=name, waits=list(waits), cost=cost, rank=rank,
                              issue=issue, behind=[], slot=None, late=0.0, move=0.0)

    def after(self, name, *others):
        self.ops[name]["behind"] = list(others)

    def dma(self, engine, name, waits, slot, rank, issue, cost=470.0, kb=256):
        self.op(engine, name, waits, cost, rank, issue)
        self.ops[name].update(slot=slot, late=1900.0, move=kb * 1024 / 350.0)

    def order(self):
        for o in self.ops.values():
            o["waits"] = [w for w in o["waits"] if w is not None]
            for w in o["waits"]:
                assert w in self.ops, (o["name"], w)
        left = {n: len({*o["waits"], *o["behind"]}) for n, o in self.ops.items()}
        lag = lambda w, m: 0 if w not in self.ops[m]["waits"] else self.LAG[self.ops[w]["engine"]][self.ops[m]["engine"]]
        after = {}
        for n, o in self.ops.items():
            for w in {*o["waits"], *o["behind"]}:
                after.setdefault(w, []).append(n)
        ready, end, moved = {}, {}, 0.0
        engines = sorted({o["engine"] for o in self.ops.values()})
        cand = {g: [] for g in engines}
        free = {g: 0.0 for g in engines}
        queue = {g: [] for g in engines}
        for n, o in self.ops.items():
            if not left[n]:
                ready[n] = 0.0
                cand[o["engine"]].append(n)
        todo = len(self.ops)
        while todo:
            best = None
            for g in engines:
                if cand[g]:
                    s = max(free[g], min(ready[n] for n in cand[g]))
                    if best is None or s < best[0]:
                        best = (s, g)
            assert best is not None, [n for n in left if left[n]][:20]
            s, g = best
            near = s + self.WAIT[g]
            n = min((n for n in cand[g] if ready[n] <= near), key=lambda n: (self.ops[n]["rank"], ready[n]))
            s = max(s, ready[n])
            cand[g].remove(n)
            o = self.ops[n]
            free[g] = s + o["cost"]
            end[n] = free[g]
            if o["slot"]:
                moved = max(moved, free[g] + 700.0) + o["move"]
                end[n] = moved + 1100.0
            queue[g].append(o)
            todo -= 1
            for m in after.get(n, ()):
                left[m] -= 1
                if not left[m]:
                    ready[m] = max(end[w] + lag(w, m)
                                   for w in [*self.ops[m]["waits"], *self.ops[m]["behind"]])
                    cand[self.ops[m]["engine"]].append(m)
        self.planned = max(end.values())
        self.endt = end
        return queue

    def emit(self):
        queue = self.order()
        wanted = {w for o in self.ops.values() for w in o["waits"]}
        count, mark = {}, {}
        for g, ops in queue.items():
            for o in ops:
                if o["slot"]:
                    count[o["slot"]] = count.get(o["slot"], 0) + 16
                    mark[o["name"]] = (o["slot"], count[o["slot"]])
                elif o["name"] in wanted:
                    count[g] = count.get(g, 0) + 1
                    mark[o["name"]] = (g, count[g])
        sems = {s: self.sem("s_" + s) for s in count}

        def run(g):
            def body(eng):
                seen = {}
                for o in queue.get(g, ()):
                    need = {}
                    for w in o["waits"]:
                        s, v = mark[w]
                        need[s] = max(v, need.get(s, 0))
                    for s, v in need.items():
                        if seen.get(s, 0) < v:
                            eng.wait_ge(sems[s], v)
                            seen[s] = v
                    last = o["issue"](eng)
                    if o["name"] in mark:
                        last.then_inc(sems[mark[o["name"]][0]], 16 if o["slot"] else 1)
            return body

        with self.nc.Block() as block:
            block.sync(run("sync"))
            block.tensor(run("tensor"))
            block.scalar(run("scalar"))
            block.vector(run("vector"))
            block.gpsimd(run("gpsimd"))


def decoder_layer(nc, x, xT, ctx_in, cols, consts, in_w, xp_w, out_w, Wq, Wkv, Wo, bo, w1, w2, out):
    NT = x.shape[0]
    RK = RANK
    NB = NT // 256
    CAP = NT // E
    CT = CAP // 128
    PT2 = max(CT, 2)
    PN = 128 * PT2
    NI = NB * H
    SCALE = 128.0 ** -0.5

    xs = nc.dram_tensor("xs", [NT + 256 * EARLY, ROW], F32, kind="Internal").ap()
    acc = nc.dram_tensor("acc", [NT + PN, 256], F32, kind="Internal").ap()

    es = ExitStack()
    with es:
        sem = lambda name: es.enter_context(nc.semaphore(name))
        P = Program(nc, sem)
        op, dma = P.op, P.dma

        class Arena:
            def __init__(self, name, size, dt):
                self.t = es.enter_context(nc.sbuf_tensor(name, [128, size], dt))
                self.size, self.at = size, 0

            def take(self, *shape, at=None):
                n = 1
                for d in shape:
                    n *= d
                if at is None:
                    at = self.at
                    self.at += n
                    assert self.at <= self.size, (self.at, self.size)
                v = self.t[:, at:at + n]
                if len(shape) == 2:
                    v = v.rearrange("p (a b) -> p a b", a=shape[0])
                if len(shape) == 3:
                    v = v.rearrange("p (a b c) -> p a b c", a=shape[0], b=shape[1])
                return v

        R = Arena("R", 37140, F32R)
        F = Arena("F", 15564, F32)

        WQ = [R.take(2, 1024) for _ in range(2)]
        r_wkv = R.at
        WKV = [R.take(2, 2048) for _ in range(2)]
        r_wo = R.at
        WO = [R.take(8, 256) for _ in range(2)]
        r_s1 = R.at
        INW = [R.take(2, 512) for _ in range(2)]
        XPW = [R.take(4, 80) for _ in range(2)]
        OW = R.take(256)
        XS = [R.take(2, 256) for _ in range(2)]
        GS = [R.take(4, 256) for _ in range(2)]
        YS = R.take(256)
        r_x = R.at
        XT2 = [R.take(2, 256) for _ in range(2)]
        ES = R.take(2, 40)
        r_ring = R.at
        KV = [[R.take(2, NP) for _ in range(2)] for _ in range(2)]
        QS = [[R.take(256) for _ in range(2)] for _ in range(3)]
        KS = [[R.take(NP) for _ in range(2)] for _ in range(3)]
        VS = [[R.take(3, 256) for _ in range(2)] for _ in range(2)]
        PTS = [[R.take(768) for _ in range(2)] for _ in range(2)]
        OS = [[R.take(256) for _ in range(2)] for _ in range(2)]
        r_fw = (r_s1, r_wkv, r_ring, r_ring + 4096, r_ring + 8192)
        FW1 = [[R.take(2, 512, at=b + 1024 * k) for k in range(2)] for b in r_fw]
        FW2 = [[R.take(4, 256, at=b + 2048 + 1024 * k) for k in range(2)] for b in r_fw]
        FX = [[R.take(2, PN, at=r_wkv + 4096 + 2048 * s + 2 * PN * k) for k in range(2)] for s in range(2)]
        FI = [[R.take(4, PN, at=b + 4 * PN * k) for k in range(2)] for b in (0, r_wo)]
        assert r_ring + 12288 <= R.at and r_fw[0] + 4096 <= r_x

        CO = F.take(C_END)
        KO = F.take(K_END)
        BQS = F.take(H)
        HXB = F.take(1)
        MH = F.take(4)
        RUN = F.take(E)
        BO = F.take(256)
        f_s1 = F.at
        XTR = [F.take(2, 256) for _ in range(2)]
        XR = [F.take(2, 256) for _ in range(2)]
        HP = F.take(4, 259)
        Z = F.take(4, 256)
        ZP = F.take(256)
        TH = F.take(4, 256)
        A, TB, ZB, YF = [F.take(256) for _ in range(4)]
        Y1 = F.take(2, 256)
        f_z1 = F.at
        Z1 = F.take(2, 256)
        LT = F.take(2, 256)
        CR = F.take(256)
        CZ = F.take(256)
        CTX = F.take(2, NC)
        f_x1b = F.at
        X1B = [F.take(2, 256) for _ in range(3)]
        f_pm = F.at
        PM = [F.take(2, NP) for _ in range(2)]
        f_x2e = F.at
        X2E = [F.take(2, ROW) for _ in range(2)]
        PAD = F.take(4, ROW, at=f_x2e)[:, :, 265:ROW]
        f_y2 = F.at
        Y2 = F.take(2, 256)
        f_lgt = F.at
        LGT = F.take(256)
        LG = F.take(2, 8)
        M8 = F.take(2, 8)
        IF = F.take(2, 2)
        DW = F.take(2, 4)
        GT = F.take(2)
        OH = F.take(2, 2, 8)
        V8 = F.take(2, 8)
        G8 = F.take(2, 8)
        PR = F.take(2, 2, 8)
        SL = F.take(2, 2)
        NM = F.take(2, 2)
        RS = F.take(2, 2)
        stats = {}
        for k in ("a", "c", "d"):
            stats[k] = (F.take(2, 6), F.take(2, 2), F.take(4), F.take(4))
        tail_stats = (F.take(32, 6), F.take(32, 2), F.take(32), F.take(32))
        STG = [F.take(1024), F.take(1024, at=f_x1b + 512), F.take(1024, at=f_z1),
               F.take(1024, at=f_x2e)]
        INIT_ALL = F.take(4 * ROW, at=f_pm)
        assert 4 * ROW <= 2 * 2 * NP
        INIT = INIT_ALL[:, 0:PT2 * ROW].rearrange("p (a b) -> p a b", a=PT2)
        RW1 = [F.take(2, 512, at=f_s1 + 2048 * s) for s in range(2)]
        RW2 = [F.take(4, 256, at=f_s1 + 2048 * s + 1024) for s in range(2)]
        XSL = [F.take(PT2, ROW, at=f_s1 + 4096 + PT2 * ROW * s) for s in range(2)]
        YO = [F.take(PT2, 256, at=f_s1 + 4096 + 2 * 1088 + PT2 * 256 * s) for s in range(2)]
        NCH = NT // 256
        AC = [F.take(2, 256, at=(f_x1b if n < 8 else f_s1) + 512 * (n % 8)) for n in range(NCH)]
        assert f_s1 + 4096 + 2 * 1088 + 2 * 1024 <= f_x1b and f_x1b + 512 * 8 <= f_lgt

        I8 = es.enter_context(nc.sbuf_tensor("I8", [128, 2, 8], U32))
        IX = es.enter_context(nc.sbuf_tensor("IX", [128, 2, 4], U32))
        IE = es.enter_context(nc.sbuf_tensor("IE", [128, 2, 4], U32))
        WE = es.enter_context(nc.sbuf_tensor("WE", [128, 2, 4], F32))
        TRI = es.enter_context(nc.sbuf_tensor("TRI", [128, 128], BF16))
        ONE = es.enter_context(nc.sbuf_tensor("ONE", [128, 128], BF16))
        OHB = es.enter_context(nc.sbuf_tensor("OHB", [128, 2, 8], BF16))

        PS = es.enter_context(nc.psum_tensor("PS", [128, 8 * 512], F32))
        bank = lambda k: PS[:, 512 * k:512 * (k + 1)]
        SA = [bank(0), bank(1)]
        PT = PS[:, 1024:1024 + 768]
        PO = PS[:, 1024 + 768:2048]
        PW = bank(4)
        D0, D1, D2 = bank(5), bank(6), bank(7)

        ident = KO[:, K_ID:K_ID + 128]
        pre = lambda i, name, *a: name.format(*a) if i >= 0 else None

        tc = lambda n: 65 + 1.04 * n
        ac = lambda n: 94 + 0.833 * n
        pc = lambda n: 150 + 2.1 * n

        def hi_lo(tag, raw, hi, lo, n, waits, rank, scale=1.0, free=(), lo_on="vector", rows=slice(0, 128)):
            op("scalar", tag + ".h", [*waits, *free], ac(n), rank,
               lambda e: e.activation(hi, raw, ACT.Copy, scale=scale))
            if lo_on == "gpsimd":
                op("gpsimd", tag + ".l", [tag + ".h", *waits, *free], pc(n), rank,
                   lambda e: e.tensor_tensor(lo, raw, hi.bitcast(F32), ALU.subtract))
                return
            op("vector", tag + ".l", [tag + ".h", *waits, *free], tc(n), rank,
               lambda e: e.scalar_tensor_tensor(lo, raw, scale, hi.bitcast(F32), ALU.mult, ALU.subtract))

        def split3(e, dst, w, xr, first, last):
            for n, (i, j) in enumerate(((0, 0), (0, 1), (1, 0))):
                r = e.matmul(dst, w[i], xr[j], start=first and n == 0, stop=last and n == 2,
                             skip_group_check=True)
            return r


        dma("sync", "ld.cols", [], "ld.cols", -98, lambda e: e.dma_start(CO, cols), kb=37)
        dma("sync", "ld.consts", [], "ld.consts", -96, lambda e: e.dma_start(KO, consts), kb=147)
        dma("sync", "ld.bo", [], "ld.bo", -50, lambda e: e.dma_start(BO, bo.partition_broadcast(128)), kb=128)

        raw_in = [
            ("wq0", Wq[:, :, 0:512], lambda W: W[:, :, 0:512], WQ, SCALE, 2, -5.9, 1, "vector"),
            ("wk0", Wkv[:, :, 0:512], lambda W: W[:, :, 0:512], WKV, 1.0, 2, -5.8, 2, "gpsimd"),
            ("wv0", Wkv[:, :, 1024:1536], lambda W: W[:, :, 1024:1536], WKV, 1.0, 2, -5.7, 0, "gpsimd"),
            ("wq1", Wq[:, :, 512:1024], lambda W: W[:, :, 512:1024], WQ, SCALE, 2, RK["wq1"], 0, "vector"),
            ("wo0", Wo[:, 0:4, :], lambda W: W[:, 0:4, :], WO, 1.0, 4, RK["wo0"], 3, "gpsimd"),
            ("wk1", Wkv[:, :, 512:1024], lambda W: W[:, :, 512:1024], WKV, 1.0, 2, RK["wk1"], 1, "gpsimd"),
            ("wv1", Wkv[:, :, 1536:2048], lambda W: W[:, :, 1536:2048], WKV, 1.0, 2, RK["wv1"], 0, "gpsimd"),
            ("wo1", Wo[:, 4:8, :], lambda W: W[:, 4:8, :], WO, 1.0, 4, RK["wo1"], 3, "gpsimd"),
        ]
        for j in range(2):
            st = STG[0][:, 512 * j:512 * j + 512].rearrange("p (a b) -> p a b", a=2)
            c = slice(256 * j, 256 * j + 256)
            dma("sync", f"ld.inw{j}", [], f"ld.inw{j}", -100 + 1.5 * j,
                lambda e, st=st, c=c: e.dma_start(st, in_w[:, :, c]))
            hi_lo(f"inw{j}", st, INW[0][:, :, c], INW[1][:, :, c], 512, [f"ld.inw{j}"], -100 + 2.5 * j)
        stage_user = {0: "inw1"}
        for nth, (tag, src, view, W, scale, a, rank, n, lo_on) in enumerate(raw_in):
            st = STG[n].rearrange("p (a b) -> p a b", a=a)
            before = [stage_user[n] + ".l"] if n in stage_user else []
            if before == ["inw1.l"]:
                before.append("inw0.l")
            stage_user[n] = tag
            dma("sync", "ld." + tag, before, f"ld.stg{n}", -66 + 0.1 * nth,
                lambda e, st=st, src=src: e.dma_start(st, src), kb=512)
            hi_lo(tag, st, view(W[0]), view(W[1]), 1024, ["ld." + tag], rank, scale, lo_on=lo_on)

        XPR = F.take(4, 32, at=f_y2)
        OWR = F.take(256, at=f_y2 + 128)
        dma("sync", "ld.xpw", [], "ld.xpw", -85, lambda e: e.dma_start(XPR, xp_w), kb=64)
        for k in range(3):
            n = 16 if k == 1 else 17
            dma("sync", f"ld.ow{k}", [], "ld.ow", -70,
                lambda e, k=k, n=n: e.dma_start(OWR[32 * k:32 * k + n, :], out_w[0:n, :]), kb=17)
        for k in range(2):
            op("gpsimd", f"xpw.z{k}", [], 400, -90,
               lambda e, k=k: e.memset(XPW[k][:, :, 0:64].bitcast(F32), 0.0))
            op("gpsimd", f"xpw.s{k}", [], 200, -90,
               lambda e, k=k: e.memset(XPW[k][:, :, 64:80].bitcast(F32), 0.25 * (1 - k)))
            for s in range(2):
                op("gpsimd", f"kv.z{k}{s}", [], 100, -50,
                   lambda e, k=k, s=s: e.memset(KV[s][k][:, :, NK:NP].bitcast(F32), 0.0))
        for g in range(2):
            hi_lo(f"xpw{g}", XPR[:, :, 16 * g:16 * g + 16], XPW[0][:, :, 32 * g:32 * g + 16],
                  XPW[1][:, :, 32 * g:32 * g + 16], 64, ["ld.xpw", "xpw.z0", "xpw.z1"], -80, 0.5)
        op("gpsimd", "ow.z", [], 300, -70, lambda e: e.memset(OW[0:96, :].bitcast(F32), 0.0))
        op("gpsimd", "ys.z", [], 300, -70, lambda e: e.memset(YS[0:96, :].bitcast(F32), 1.0))
        for k, n in ((0, 17), (1, 16), (2, 17)):
            r = slice(32 * k, 32 * k + n)
            op("scalar", f"ow{k}", ["ld.ow2", "ow.z"], 370, -60,
               lambda e, r=r: e.activation(OW[r, :], OWR[r, :], ACT.Copy))
        op("vector", "ow.l", ["ow2"], 335, -60,
           lambda e: e.tensor_tensor(OW[64:81, :], OWR[64:81, :], OW[64:81, :].bitcast(F32), ALU.subtract))
        op("gpsimd", "pad.z", ["wo1.l"], 100, -4, lambda e: e.memset(PAD, 0.0))
        XPW_OK = ["xpw0.l", "xpw1.l", "xpw.s0", "xpw.s1"]
        OW_OK = ["ow0", "ow1", "ow.l", "ys.z"]

        op("gpsimd", "es.z", [], 100, -40, lambda e: e.memset(ES.bitcast(F32), 0.0))
        CE = CO[:, C_E:C_E + 16].rearrange("p (a b) -> p a b", a=2)
        hi_lo("es", CE, ES[:, :, 0:8], ES[:, :, 32:40], 16, ["ld.cols", "es.z"], -30)
        op("gpsimd", "hp.z", [], 100, -95, lambda e: e.memset(HP[:, :, 0:3], 0.0))
        op("gpsimd", "mh", [], 100, -90, lambda e: e.memset(MH, -0.5))
        op("gpsimd", "run.z", [], 100, -50, lambda e: e.memset(RUN, 0.0))
        op("gpsimd", "init.z", [], 900, -30, lambda e: e.memset(INIT_ALL, 0.0))
        op("vector", "bqs", ["ld.cols"], 80, -50,
           lambda e: e.tensor_scalar(BQS, CO[:, C_BQ:C_BQ + H], SCALE, None, ALU.mult))
        op("vector", "hxb", ["ld.cols"], 80, -80,
           lambda e: e.tensor_scalar(HXB, CO[:, C_XPB:C_XPB + 1], 0.5, None, ALU.mult))
        op("vector", "tri", ["ld.consts"], 100, -40,
           lambda e: e.tensor_copy(TRI[:, :], KO[:, K_TRI:K_TRI + 128]))
        op("vector", "one", [], 100, -40, lambda e: e.memset(ONE[:, :], 1.0))
        op("vector", "init.id", ["init.z", "ld.consts"], 80, -30,
           lambda e: e.tensor_copy(INIT[:, :, 256:257], KO[:, K_DUMP:K_DUMP + PT2].unsqueeze(2)))
        for n in range(0, xs.shape[0], PN):
            m = min(PN, xs.shape[0] - n)
            dma("sync", f"init.{n}", ["init.id"], "init", -20,
                lambda e, n=n, m=m: e.dma_start(xs[n:n + m, :].rearrange("(p t) n -> p t n", p=128),
                                                INIT[:, 0:m // 128, :]), kb=136 * m // 128)
        dma("sync", "init.acc", ["init.id"], "init", -20,
            lambda e: e.dma_start(acc[NT:NT + PN, :].rearrange("(p t) n -> p t n", p=128), INIT[:, :, 0:256]), kb=128 * PT2)
        INIT_OK = "init.acc"


        def norm(tag, kind, src, dst, waits, rank, free=(), again=(), rows=128, tiles=2,
                 on=("vector", "scalar")):
            st, mv, rs, nr = stats[kind]
            r = slice(0, rows)
            ag = list(again)
            for t in range(tiles):
                op("vector", f"{tag}.s{t}", [*waits, *ag], 345, rank,
                   lambda e, t=t: e.bn_stats(st[r, t, :], src(t)))
                op("vector", f"{tag}.m{t}", [f"{tag}.s{t}", *ag], 80, rank,
                   lambda e, t=t: e.bn_aggr(mv[r, t, :], st[r, t, :]))
            op("vector", f"{tag}.v", [f"{tag}.m{t}" for t in range(tiles)] + ag, 80, rank,
               lambda e: e.tensor_scalar(rs[r, 0:tiles], mv[r, 0:tiles, 1], EPS, None, ALU.add))
            op("gpsimd", f"{tag}.r", [f"{tag}.v", "mh"], 640, rank,
               lambda e: e.tensor_tensor(rs[r, 0:tiles], rs[r, 0:tiles], MH[r, 0:tiles], ALU.pow))
            if "scalar" in on[0:tiles]:
                op("vector", f"{tag}.n", [f"{tag}.r", *ag], 80, rank,
                   lambda e: e.scalar_tensor_tensor(nr[r, 0:tiles], mv[r, 0:tiles, 0], -1.0, rs[r, 0:tiles],
                                                    ALU.mult, ALU.mult))
            for t in range(tiles):
                if on[t] == "scalar":
                    op("scalar", f"{tag}.a{t}", [f"{tag}.n", *free], 493, rank,
                       lambda e, t=t: e.activation(dst(t), src(t), ACT.Identity, bias=nr[r, t:t + 1],
                                                   scale=rs[r, t:t + 1]))
                    continue
                op("vector", f"{tag}.a{t}", [f"{tag}.r", *free], 330, rank,
                   lambda e, t=t: e.tensor_scalar(dst(t), src(t), mv[r, t, 0:1], rs[r, t:t + 1],
                                                  ALU.subtract, ALU.mult))
            return [f"{tag}.a{t}" for t in range(tiles)]


        d2_order, d2_end = [], {}

        def d2(name, ends):
            d2_end[name] = ends

        for k in range(0, NB + 1):
            n, r = k + 1, k - 1
            if n < NB:
                d2_order += [f"cT{n}", f"in{n}.0", f"in{n}.1"]
            if r >= 0:
                d2_order += [f"rT{r}", f"lg{r}", f"lgT{r}"]
            if n < NB:
                d2_order += [f"xp{n}"]
            if r >= 0:
                d2_order += [f"cum{r}"]
            if n < NB:
                d2_order += [f"out{n}", f"zT{n}"]
        d2_place = {n: k for k, n in enumerate(d2_order)}

        def d2_turn(name):
            k = d2_place.get(name, 0)
            return ("turn", d2_order[k - 1]) if k else None


        def stage1(b):
            s = b % 2
            aside = lambda k: "gpsimd" if b and RK[k] else "vector"
            rk = lambda f: 8 * (b - 1) + RK["s1"] + RK["s1x"] * f + {1: RK["b1"], 2: RK["b2"]}.get(b, 0)
            early = lambda *r: r[b] if b < 2 else rk(-0.5)
            p = b - 1
            done = lambda name: [name.format(p, k) for k in range(3 if b == 1 else 1 if b else 0)]
            parts = [(0, 4)] if b else [(0, 2), (2, 3), (3, 4)]
            tok = slice(256 * b, 256 * b + 256)
            B_in, B_xp, B_out, B_z, B_c = (([bank(0), bank(1)], bank(2), bank(3), [D1, bank(3)], D0) if b == 0
                                           else ([D2, D2], D2, D2, [D2, D2[:, 256:512]], D2))
            dma("sync", f"ld.xt{b}", [pre(b - 2, "xl{}.l", b - 2)], f"ld.xt{s}", early(-99, -67),
                lambda e: e.dma_start(XTR[s], xT[:, tok].rearrange("(c p) n -> p c n", p=128)))
            dma("sync", f"ld.x{b}", [pre(b - 2, "y1{}", b - 2)], f"ld.x{s}", early(-66.5, -64.5),
                lambda e: e.dma_start(XR[s], x[tok, :].rearrange("(t p) n -> p t n", p=128)))
            hi_lo(f"xl{b}", XTR[s], XS[0], XS[1], 512, [f"ld.xt{b}"], rk(0), free=[pre(p, "in{}.1", p)],
                  lo_on=aside("xl"))
            zlast = []
            for j in range(2):
                def mm(e, j=j):
                    for m in (2 * j, 2 * j + 1):
                        for c in range(2):
                            w = [INW[k][:, c, 128 * m:128 * m + 128] for k in range(2)]
                            r = split3(e, B_in[j][:, 256 * (m % 2):256 * (m % 2) + 256], w,
                                       [XS[k][:, c, :] for k in range(2)], m % 2 == 0 and c == 0, c == 1)
                    return r
                op("tensor", f"in{b}.{j}", [f"xl{b}.l", f"inw{j}.l", d2_turn(f"in{b}.{j}")], 1320, rk(0.1 + 0.1 * j), mm)
                d2(f"in{b}.{j}", [f"hp{b}.{2 * j}", f"hp{b}.{2 * j + 1}"])
                for m in (2 * j, 2 * j + 1):
                    op("scalar", f"hp{b}.{m}", [f"in{b}.{j}", "ld.cols", pre(p, "z{}.{}.3", p, m)], 358,
                       rk(0.1 + 0.1 * j),
                       lambda e, m=m, j=j: e.activation(HP[:, m, 3:259], B_in[j][:, 256 * (m % 2):256 * (m % 2) + 256],
                                                   ACT.Identity, bias=CO[:, C_INB + m:C_INB + m + 1]))
                    cw = lambda k, m=m: CO[:, C_CW + 4 * m + k:C_CW + 4 * m + k + 1]
                    if b == 0 and m:
                        op("scalar", f"z0.{m}.0", [f"hp0.{m}"], 307, rk(0.15 + 0.1 * j),
                           lambda e, m=m, cw=cw: e.activation(Z[:, m, :], HP[:, m, 3:259], ACT.Identity,
                                                              bias=CO[:, C_CB + m:C_CB + m + 1], scale=cw(3)))
                    else:
                        op("gpsimd", f"z{b}.{m}.0", [f"hp{b}.{m}", "hp.z", "ld.cols", *done("g{}.{}")], 540, rk(0.2),
                           lambda e, m=m, cw=cw: e.tensor_scalar(Z[:, m, :], HP[:, m, 3:259], cw(3),
                                                                 CO[:, C_CB + m:C_CB + m + 1], ALU.mult, ALU.add))
                    for k in range(1, 4):
                        if (m >= 4 - RK["pc"]) if b else m == 0:
                            op("gpsimd", f"zp{b}.{m}.{k}", [f"hp{b}.{m}", f"z{b}.{m}.{k - 1}", *zlast], 457, rk(0.2),
                               lambda e, m=m, k=k, cw=cw: e.tensor_scalar(ZP, HP[:, m, 3 - k:259 - k], cw(3 - k), 0.0,
                                                                          ALU.mult, ALU.add))
                            op("gpsimd", f"z{b}.{m}.{k}", [f"zp{b}.{m}.{k}"], 690, rk(0.2),
                               lambda e, m=m: e.tensor_tensor(Z[:, m, :], Z[:, m, :], ZP, ALU.add))
                            zlast = [f"z{b}.{m}.{k}"]
                            continue
                        op("vector", f"z{b}.{m}.{k}", [f"z{b}.{m}.{k - 1}"], 396, rk(0.2) + (0 if b else 0.01 * m),
                           lambda e, m=m, k=k, cw=cw: e.scalar_tensor_tensor(
                               Z[:, m, :], HP[:, m, 3 - k:259 - k], cw(3 - k), Z[:, m, :], ALU.mult, ALU.add))
            for k, (m0, m1) in enumerate(parts):
                n, ms = 256 * (m1 - m0), slice(m0, m1)
                op("scalar", f"th{b}.{k}", [f"z{b}.{m}.3" for m in range(m0, m1)] + done("gs{}.{}.l"), ac(n),
                   rk(0.4), lambda e, ms=ms: e.activation(TH[:, ms, :], Z[:, ms, :], ACT.Tanh, scale=0.5))
                op("vector", f"g{b}.{k}", [f"th{b}.{k}"], tc(n), rk(0.4),
                   lambda e, ms=ms: e.scalar_tensor_tensor(TH[:, ms, :], TH[:, ms, :], 1.0, Z[:, ms, :],
                                                           ALU.add, ALU.mult))
                hi_lo(f"gs{b}.{k}", TH[:, ms, :], GS[0][:, ms, :], GS[1][:, ms, :], n, [f"g{b}.{k}"], rk(0.45),
                      free=[pre(p, "xp{}", p)], lo_on="gpsimd" if b == 0 and k == 0 else aside("gs"))

            def xp(e):
                for m in range(4):
                    r = split3(e, B_xp[0:80, 0:256], [XPW[k][:, m, :] for k in range(2)],
                               [GS[k][:, m, :] for k in range(2)], m == 0, m == 3)
                return r
            op("tensor", f"xp{b}", [*[f"gs{b}.{k}.l" for k in range(len(parts))], *XPW_OK, d2_turn(f"xp{b}")], 1320, rk(0.5), xp)
            d2(f"xp{b}", [f"ea{b}", f"tb{b}", f"zb{b}", f"bb{b}"])
            op("scalar", f"ea{b}", [f"xp{b}", pre(p, "scan{}", p)], 358, rk(0.5),
               lambda e: e.activation(A[0:16, :], B_xp[0:16, 0:256], ACT.Exp, bias=CO[0:16, C_XPB:C_XPB + 1]))
            op("scalar", f"tb{b}", [f"xp{b}", "hxb", pre(p, "u{}", p)], 358, rk(0.5) - 0.01,
               lambda e: e.activation(TB[0:16, :], B_xp[32:48, 0:256], ACT.Tanh, scale=0.5, bias=HXB[32:48, :]))
            op("scalar", f"a{b}", [f"ea{b}"], 307, rk(0.5),
               lambda e: e.activation(A[0:16, :], A[0:16, :], ACT.Exp, scale=-1.0))
            op("vector", f"zb{b}", [f"tb{b}", pre(p, "scan{}", p)], 390, rk(0.5),
               lambda e: e.tensor_scalar(ZB[0:16, :], B_xp[32:48, 0:256], CO[32:48, C_XPB:C_XPB + 1], None, ALU.add))
            op("vector", f"u{b}", [f"tb{b}", f"zb{b}"], 335, rk(0.5),
               lambda e: e.scalar_tensor_tensor(ZB[0:16, :], TB[0:16, :], 1.0, ZB[0:16, :], ALU.add, ALU.mult))
            op("vector", f"bb{b}", [f"u{b}"], 335, rk(0.5),
               lambda e: e.tensor_tensor(ZB[0:16, :], B_xp[64:80, 0:256], ZB[0:16, :], ALU.mult))
            op("vector", f"scan{b}", [f"a{b}", f"bb{b}", pre(p, "ys{}.l", p)], 335, rk(0.5),
               lambda e: e.tensor_tensor_scan(YF[0:16, :], A[0:16, :], ZB[0:16, :], 0.0, ALU.mult, ALU.add))
            for k in (0, 2):
                op("scalar", f"yh{b}.{k}", [f"scan{b}", "ys.z", pre(p, "out{}", p)], 307, rk(0.55),
                   lambda e, k=k: e.activation(YS[32 * k:32 * k + 16, :], YF[0:16, :], ACT.Copy))
            op("vector", f"ys{b}.l", [f"yh{b}.0", "ys.z", pre(p, "out{}", p)], 335, rk(0.55),
               lambda e: e.tensor_tensor(YS[32:48, :], YF[0:16, :], YS[0:16, :].bitcast(F32), ALU.subtract))

            def mo(e):
                for t in range(2):
                    r = e.matmul(B_out[:, 256 * t:256 * t + 256], YS[0:96, 128 * t:128 * t + 128], OW[0:96, :],
                                 start=t == 0, stop=True, skip_group_check=True)
                return r
            op("tensor", f"out{b}", [f"ys{b}.l", f"yh{b}.2", *OW_OK, d2_turn(f"out{b}")], 220, rk(0.6), mo)
            d2(f"out{b}", [f"y1{b}"])
            op("vector", f"y1{b}", [f"out{b}", f"ld.x{b}", *([f"n1{p}.{k}" for k in ("x0", "x1", "z0", "z1")] if b else [])], 600, rk(0.6),
               lambda e: e.tensor_tensor(Y1.rearrange("p t n -> p (t n)"), B_out,
                                         XR[s].rearrange("p t n -> p (t n)"), ALU.add))
            st, mv, rs, nr = stats["a"]
            again = [f"n1{p}.{k}" for k in ("x0", "x1", "z0", "z1")] if b else []
            for t in range(2):
                op("vector", f"n1{b}.s{t}", [f"y1{b}", *again], 335, rk(0.65),
                   lambda e, t=t: e.bn_stats(st[:, t, :], Y1[:, t, :]))
                op("vector", f"n1{b}.m{t}", [f"n1{b}.s{t}", *again], 75, rk(0.65),
                   lambda e, t=t: e.bn_aggr(mv[:, t, :], st[:, t, :]))
            ms = [f"n1{b}.m0", f"n1{b}.m1"]
            op("vector", f"n1{b}.v", ms + again, 71, rk(0.65),
               lambda e: e.tensor_scalar(rs[:, 0:2], mv[:, :, 1], EPS, None, ALU.add))
            op("vector", f"n1{b}.w", ms + again, 71, rk(0.65),
               lambda e: e.tensor_scalar(rs[:, 2:4], mv[:, :, 1], 1.0 + EPS, EPS * EPS, ALU.mult, ALU.add))
            if b == 0:
                op("gpsimd", "n10.rz", ["n10.w", "mh"], 464, rk(0.65),
                   lambda e: e.tensor_tensor(rs[:, 2:4], rs[:, 2:4], MH[:, 0:2], ALU.pow))
                op("gpsimd", "n10.r", ["n10.v", "mh"], 464, rk(0.65) + 0.5,
                   lambda e: e.tensor_tensor(rs[:, 0:2], rs[:, 0:2], MH[:, 0:2], ALU.pow))
                op("vector", "n10.nz", ["n10.rz"], 80, rk(0.65),
                   lambda e: e.scalar_tensor_tensor(nr[:, 2:4], mv[:, :, 0], -1.0, rs[:, 2:4], ALU.mult, ALU.mult))
                op("vector", "n10.n", ["n10.r"], 80, rk(0.65) + 0.5,
                   lambda e: e.scalar_tensor_tensor(nr[:, 0:2], mv[:, :, 0], -1.0, rs[:, 0:2], ALU.mult, ALU.mult))
            else:
                op("gpsimd", f"n1{b}.r", [f"n1{b}.v", f"n1{b}.w", "mh"], 960, rk(0.65),
                   lambda e: e.tensor_tensor(rs, rs, MH, ALU.pow))
                op("vector", f"n1{b}.n", [f"n1{b}.r", *again], 80, rk(0.65),
                   lambda e: e.scalar_tensor_tensor(nr.rearrange("p (a b) -> p a b", a=2),
                                                    mv[:, :, 0].unsqueeze(1).to_broadcast([128, 2, 2]), -1.0,
                                                    rs.rearrange("p (a b) -> p a b", a=2), ALU.mult, ALU.mult))
            for k, dst, on in (("z", Z1, ("vector", "scalar")), ("x", X1B[b % 3], ("scalar", "scalar"))):
                old = [pre(p, "zT{}", p), "wk0.l"] if k == "z" else [pre(b - 3, "y2{}", b - 3), "wk1.l"]
                f = rk(0.68) if k == "z" else rk(0.8)
                scaled, moved = ("n10.rz", "n10.nz") if b == 0 and k == "z" else (f"n1{b}.r", f"n1{b}.n")
                for t in range(2):
                    c = t if k == "x" else 2 + t
                    if on[t] == "scalar":
                        op("scalar", f"n1{b}.{k}{t}", [moved, *old], 493, f,
                           lambda e, t=t, c=c, dst=dst: e.activation(dst[:, t, :], Y1[:, t, :], ACT.Identity,
                                                                     bias=nr[:, c:c + 1], scale=rs[:, c:c + 1]))
                        continue
                    op("vector", f"n1{b}.{k}{t}", [scaled, *old], 323, f,
                       lambda e, t=t, c=c, dst=dst: e.tensor_scalar(dst[:, t, :], Y1[:, t, :], mv[:, t, 0:1],
                                                                    rs[:, c:c + 1], ALU.subtract, ALU.mult))
            n2 = [f"n1{b}.z0", f"n1{b}.z1"]
            X1 = X1B[b % 3]
            op("gpsimd", f"x1b{b}", [f"n1{b}.x0", f"n1{b}.x1", "ld.bo"], 1230, rk(0.8),
               lambda e: e.tensor_tensor(X1, X1, BO.unsqueeze(1).to_broadcast([128, 2, 256]), ALU.add))

            def zt(e):
                for c in range(2):
                    for t in range(2):
                        r = e.transpose(B_z[c][:, 128 * t:128 * t + 128],
                                        Z1[:, t, 128 * c:128 * c + 128], ident)
                return r
            op("tensor", f"zT{b}", [*n2, "ld.consts", "y10", d2_turn(f"zT{b}")], 450, rk(0.75), zt)
            d2(f"zT{b}", [f"lt{b}.0", f"lt{b}.1"] + (["kv0.h0", "kv0.h1"] if b == 0 else []))
            for c in range(2):
                op("vector", f"lt{b}.{c}", [f"zT{b}", "kv0.h1" if b == 0 and c else None, "ld.cols", "wk0.l",
                                            pre(p, "kv{}.l", p)], 455, rk(0.75),
                   lambda e, c=c: e.tensor_scalar(LT[:, c, :], B_z[c][:, 0:256],
                                                  CO[:, C_GL + c:C_GL + c + 1], CO[:, C_BL + c:C_BL + c + 1],
                                                  ALU.mult, ALU.add))
            q = 8 * (b - 2) + 7
            old = [pre(b - 2, w, q) for w in ("Q{}", "K{}")] + [pre(b - 2, w, q // 2) for w in ("V{}", "Vc{}")]
            if b == 0:
                for c in range(2):
                    op("scalar", f"kv0.h{c}", ["zT0", "ld.cols"] + ([] if c else ["lt0.0"]), 358, rk(0.8),
                       lambda e, c=c: e.activation(KV[0][0][:, c, 0:256], B_z[c][:, 0:256], ACT.Identity,
                                                   bias=CO[:, C_BL + c:C_BL + c + 1], scale=CO[:, C_GL + c:C_GL + c + 1]))
                op("vector", "kv0.l", ["kv0.h0", "kv0.h1", "lt0.0", "lt0.1"], tc(512), rk(0.8),
                   lambda e: e.tensor_tensor(KV[0][1][:, :, 0:256], LT, KV[0][0][:, :, 0:256].bitcast(F32),
                                             ALU.subtract))
            else:
                hi_lo(f"kv{b}", LT, KV[s][0][:, :, 0:256], KV[s][1][:, :, 0:256], 512,
                      [f"lt{b}.0", f"lt{b}.1"], rk(0.8), free=old, lo_on=aside("kvl"))

            dma("sync", f"ld.c{b}", [pre(p, "nc{}.a0", p)], "ld.c", early(-95, -64.8),
                lambda e: e.dma_start(CR[0:NC, :], ctx_in[b]), kb=77)
            n3 = norm(f"nc{b}", "c", lambda t: CR[0:NC, :], lambda t: CZ[0:NC, :], [f"ld.c{b}"], rk(0),
                      free=[pre(p, "cT{}", p)], again=[pre(p, "nc{}.a0", p)], rows=NC, tiles=1)

            def ct(e):
                for c in range(2):
                    r = e.transpose(B_c[:, NC * c:NC * c + NC], CZ[0:NC, 128 * c:128 * c + 128],
                                    KO[0:NC, K_ID:K_ID + NC])
                return r
            op("tensor", f"cT{b}", [*n3, "ld.consts", d2_turn(f"cT{b}")], 130, rk(0), ct)
            d2(f"cT{b}", [f"ct{b}.0", f"ct{b}.1"])
            for c in range(2):
                op("vector", f"ct{b}.{c}", [f"cT{b}", "ld.cols", pre(p, "kc{}.l", p)], 270, rk(0),
                   lambda e, c=c: e.tensor_scalar(CTX[:, c, :], B_c[:, NC * c:NC * c + NC],
                                                  CO[:, C_GM + c:C_GM + c + 1], CO[:, C_BM + c:C_BM + c + 1],
                                                  ALU.mult, ALU.add))
            hi_lo(f"kc{b}", CTX, KV[s][0][:, :, 256:NK], KV[s][1][:, :, 256:NK], 154,
                  [f"ct{b}.0", f"ct{b}.1"], rk(0.1), free=old)


        def head(b, h):
            i = 8 * b + h
            s, s2, half = b % 2, i % 2, h // 4
            kv = KV[s]
            Qb, Kb, Pb, Ob = QS[i % 3], KS[i % 3], PM[s2], OS[s2]
            pr = i // 2
            ahead = pr < 2
            VC = bank(2)[0:NC, 256 * pr:256 * pr + 256] if ahead else D1[0:NC, 0:256]
            Vb = VS[pr % 2]
            ready = [f"kv{b}.l", f"kv.z0{s}", f"kv.z1{s}"]

            def proj(e, W, off, dst, n):
                for c in range(2):
                    r = split3(e, dst[:, 0:n], [W[k][:, c, off:off + 128] for k in range(2)],
                               [kv[k][:, c, 0:n] for k in range(2)], c == 0, c == 1)
                return r
            first = i % 2 == 0
            begin = (lambda *names: names) if i == 0 else (lambda *names: ())
            op("tensor", f"Q{i}", [*ready, *begin("ct0.0", "ct0.1"), f"wq{half}.l", pre(i - 1, "q{}.l", i - 1) if first else f"vl{pr}"],
               660, i + RK["Q"], lambda e: proj(e, WQ, 128 * h, D0, 256))
            op("scalar", f"q{i}.h", [f"Q{i}", "bqs", pre(i - 3, "S{}.1", i - 3)], 358, i + RK["q"],
               lambda e: e.activation(Qb[0], D0[:, 0:256], ACT.Identity, bias=BQS[:, h:h + 1]))
            op("vector", f"q{i}.l", [f"q{i}.h"], 400, i + RK["q"],
               lambda e: e.scalar_tensor_tensor(Qb[1], D0[:, 0:256], BQS[:, h:h + 1], Qb[0].bitcast(F32),
                                                ALU.add, ALU.subtract))
            op("tensor", f"K{i}", [*ready, *begin("lt0.0", "lt0.1", "kv0.h0", "kv0.h1"), f"kc{b}.l", f"wk{half}.l",
                                   pre(i - 1, "k{}.l", i - 1) if first or ahead else f"vcl{pr}"],
               850, i + RK["K"], lambda e: proj(e, WKV, 128 * h, D1, NP))
            bk = CO[:, C_BKV + h:C_BKV + h + 1]
            op("scalar", f"k{i}.h", [f"K{i}", pre(i - 3, "S{}.1", i - 3)], 424, i + RK["k"],
               lambda e: e.activation(Kb[0], D1[:, 0:NP], ACT.Identity, bias=bk))
            op("vector", f"k{i}.l", [f"k{i}.h"], 480, i + RK["k"],
               lambda e: e.scalar_tensor_tensor(Kb[1], D1[:, 0:NP], bk, Kb[0].bitcast(F32), ALU.add, ALU.subtract))
            if first:
                vo = 1024 + 128 * h

                def vproj(e, dst, a, m, one):
                    for c in range(2):
                        r = split3(e, dst, [kv[k][:, c, a:a + m] for k in range(2)],
                                   [WKV[k][:, c, vo:vo + 256] for k in range(2)], c == 0 and one, c == 1)
                    return r

                def v01(e):
                    vproj(e, D0[:, 0:256], 0, 128, True)
                    return vproj(e, D0[:, 256:512], 128, 128, False)
                vfree = pre(pr - 2, "PV{}", 2 * (pr - 2) + 1)
                op("tensor", f"V{pr}", [*ready, f"wv{half}.l", f"q{i}.l"], 1310, i + RK["V"], v01)
                op("scalar", f"vh{pr}", [f"V{pr}", vfree], 478, i + RK["v"],
                   lambda e: e.activation(Vb[0][:, 0:2, :], D0.rearrange("p (a b) -> p a b", a=2), ACT.Copy))
                op("vector", f"vl{pr}", [f"vh{pr}"], 600, i + RK["v"],
                   lambda e: e.tensor_tensor(Vb[1][:, 0:2, :], D0.rearrange("p (a b) -> p a b", a=2),
                                             Vb[0][:, 0:2, :].bitcast(F32), ALU.subtract))
                op("tensor", f"Vc{pr}", [f"kc{b}.l", f"wv{half}.l", *([*ready, f"k{i}.l"] if not ahead else ["vcl0"] if pr else ["bb0", "zb0", "ea0", "tb0"])],
                   655, -8 if ahead else i + RK["Vc"], lambda e: vproj(e, VC, 256, NC, True))
                op("scalar", f"vch{pr}", [f"Vc{pr}", vfree], 264, i + RK["vc"],
                   lambda e: e.activation(Vb[0][0:NC, 2, :], VC, ACT.Copy))
                op("vector", f"vcl{pr}", [f"vch{pr}"], 335, i + RK["vc"],
                   lambda e: e.tensor_tensor(Vb[1][0:NC, 2, :], VC, Vb[0][0:NC, 2, :].bitcast(F32),
                                             ALU.subtract))
            nm, rs = NM[:, s2, :], RS[:, s2, :]
            for t in range(2):
                op("tensor", f"S{i}.{t}", [f"q{i}.l", f"k{i}.l", pre(i - 1, "x{}.{}", i - 1, t),
                                          *begin(f"hp0.{2 * t}", f"hp0.{2 * t + 1}")], 420, i + RK["S"],
                   lambda e, t=t: split3(e, SA[t][:, 0:NP], [Qb[k][:, 128 * t:128 * t + 128] for k in range(2)],
                                         Kb, True, True))
                op("vector", f"m{i}.{t}", [f"S{i}.{t}", pre(i - 2, "x{}.{}", i - 2, t)], 411, i + RK["m"],
                   lambda e, t=t: e.tensor_reduce(nm[:, t:t + 1], SA[t][:, 0:NK], AX.X, ALU.max, negate=True))
                op("scalar", f"x{i}.{t}", [f"m{i}.{t}", pre(i - 2, "T{}.0", i - 2), pre(i - 2, "T{}.1", i - 2), pre(i - 2, "r{}", i - 2),
                                           INIT_OK if i < 2 else None], 515, i + RK["x"],
                   lambda e, t=t: e.activation(Pb[:, t, 0:NK], SA[t][:, 0:NK], ACT.Exp, bias=nm[:, t:t + 1],
                                               accum_out=rs[:, t:t + 1]))
            op("vector", f"r{i}", [f"x{i}.0", f"x{i}.1"], 85, i + RK["r"], lambda e: e.reciprocal(rs, rs))
            for t in range(2):
                op("gpsimd", f"p{i}.{t}", [f"r{i}"], 522, i + RK["r"],
                   lambda e, t=t: e.tensor_scalar(Pb[:, t, 0:NK], Pb[:, t, 0:NK], rs[:, t:t + 1], 0.0,
                                                  ALU.mult, ALU.add))

            Tb = PTS[s2]
            for u, (k0, k1, n, cost) in enumerate(((0, 2, 128, 440), (2, 3, NC, 220))):
                def tr(e, k0=k0, k1=k1, n=n):
                    for k in range(k0, k1):
                        for t in range(2):
                            r = e.transpose(PT[0:n, 256 * k + 128 * t:256 * k + 128 * t + 128],
                                            Pb[:, t, 128 * k:128 * k + n], ident)
                    return r
                c = slice(256 * k0, 256 * k1)
                op("tensor", f"T{i}.{u}", [f"p{i}.0", f"p{i}.1", pre(i - 1, "o{}.l" if u else "pt{}.0.l", i - 1),
                                          *begin(*(["y10", "lt0.1", "kv0.h1"] if u else ["ea0", "tb0", "zb0", "bb0", "vcl0", "vcl1"]))],
                   cost, i + RK[f"T{u}"], tr)
                op("scalar", f"pt{i}.{u}.h", [f"T{i}.{u}", pre(i - 2, "PV{}", i - 2)], ac(256 * (k1 - k0)) - 42, i + RK[f"pt{u}"],
                   lambda e, n=n, c=c: e.activation(Tb[0][0:n, c], PT[0:n, c], ACT.Copy))
                op("vector", f"pt{i}.{u}.l", [f"pt{i}.{u}.h"], tc(256 * (k1 - k0)), i + RK[f"pt{u}"],
                   lambda e, n=n, c=c: e.tensor_tensor(Tb[1][0:n, c], PT[0:n, c], Tb[0][0:n, c].bitcast(F32),
                                                       ALU.subtract))

            def pv(e):
                for k in range(3):
                    n = 128 if k < 2 else NC
                    c0 = 128 * (h % 2)
                    r = split3(e, PO, [Vb[j][0:n, k, c0:c0 + 128] for j in range(2)],
                               [Tb[j][0:n, 256 * k:256 * k + 256] for j in range(2)], k == 0, k == 2)
                return r
            op("tensor", f"PV{i}", [f"pt{i}.0.l", f"pt{i}.1.l", f"vl{pr}", f"vcl{pr}"], 980, i + RK["PV"], pv)
            bv = CO[:, C_BKV + 8 + h:C_BKV + 9 + h]
            op("scalar", f"o{i}.h", [f"PV{i}", pre(i - 2, "W{}", i - 2)], 358, i + RK["o"],
               lambda e: e.activation(Ob[0], PO, ACT.Identity, bias=bv))
            op("vector", f"o{i}.l", [f"o{i}.h"], 400, i + RK["o"],
               lambda e: e.scalar_tensor_tensor(Ob[1], PO, bv, Ob[0].bitcast(F32), ALU.add, ALU.subtract))

            def mw(e):
                for t in range(2):
                    r = split3(e, PW[:, 256 * t:256 * t + 256], [Ob[k][:, 128 * t:128 * t + 128] for k in range(2)],
                               [WO[k][:, h, :] for k in range(2)], h == 0 and t == 0, h == 7)
                return r
            op("tensor", f"W{i}", [f"o{i}.l", f"wo{half}.l", pre(b - 1, "y2{}", b - 1) if h == 0 else None,
                                    *begin(f"warm{len(WARM0) - 1}")],
               655, i + RK["W"], mw)


        def route(b):
            s, p = b % 2, b - 1
            X = X2E[s]
            rk = lambda f: 8 * b + RK["rt"] + RK["rtx"] * f
            free = [pre(b - 2, "st{}", b - 2)] + [pre(b - 2, "sc{}.{}", b - 2, k) for k in range(4)]
            if b < 2:
                free = ["wo1.l"]
            op("vector", f"y2{b}", [f"W{8 * b + 7}", f"x1b{b}", pre(p, "n4{}.a1", p), pre(p, "n4{}.a0", p),
                                    "xpw0.l", "xpw1.l", "ow.l"], 600, rk(0) - 1,
               lambda e: e.tensor_tensor(Y2.rearrange("p t n -> p (t n)"), PW,
                                         X1B[b % 3].rearrange("p t n -> p (t n)"), ALU.add))
            n4 = norm(f"n4{b}", "d", lambda t: Y2[:, t, :], lambda t: X[:, t, 0:256], [f"y2{b}"], rk(0),
                      free=free, again=[pre(p, "n4{}.a0", p), pre(p, "n4{}.a1", p)])
            dma("sync", f"st{b}", n4, f"st{s}", rk(0), lambda e: e.dma_start(
                acc[256 * b:256 * b + 256, :].rearrange("(t p) n -> p t n", p=128), X[:, :, 0:256]))
            op("vector", f"id{b}", [*n4, *free, "ld.consts"], 80, rk(0),
               lambda e: e.tensor_scalar(X[:, :, 256], KO[:, K_TOK:K_TOK + 2], 256.0 * b, None, ALU.add))

            def rt(e):
                for c in range(2):
                    for t in range(2):
                        r = e.transpose(D2[:, 256 * c + 128 * t:256 * c + 128 * t + 128],
                                        X[:, t, 128 * c:128 * c + 128], ident)
                return r
            op("tensor", f"rT{b}", [*n4, d2_turn(f"rT{b}")], 450, rk(0.1), rt)
            d2(f"rT{b}", [f"x2t{b}.h", f"x2t{b}.l"])
            D2v = D2.rearrange("p (c n) -> p c n", c=2)
            hi_lo(f"x2t{b}", D2v, XT2[0], XT2[1], 512, [f"rT{b}"], rk(0.1), free=[pre(p, "lg{}", p)])

            def lg(e):
                for c in range(2):
                    for k in range(2):
                        r = e.matmul(D2[0:40, 0:256], ES[:, c, :], XT2[k][:, c, :],
                                     start=c == 0 and k == 0, stop=c == 1 and k == 1)
                return r
            op("tensor", f"lg{b}", [f"x2t{b}.h", f"x2t{b}.l", "es.l", d2_turn(f"lg{b}")], 440, rk(0.2), lg)
            d2(f"lg{b}", [f"lgc{b}"])
            op("vector", f"lgc{b}", [f"lg{b}", pre(p, "lgT{}", p)], 335, rk(0.2),
               lambda e: e.tensor_copy(LGT[0:40, :], D2[0:40, 0:256]))

            def lt(e):
                for t in range(2):
                    r = e.transpose(D2[:, 40 * t:40 * t + 40], LGT[0:40, 128 * t:128 * t + 128],
                                    KO[0:40, K_ID:K_ID + 40])
                return r
            op("tensor", f"lgT{b}", [f"lgc{b}", d2_turn(f"lgT{b}")], 100, rk(0.3), lt)
            d2(f"lgT{b}", [f"l7{b}", f"l8{b}"])
            v = lambda name, waits, issue, f=0.4, cost=90: op("vector", f"{name}{b}", waits, cost, rk(f), issue)
            n = lambda name: f"{name}{b}"
            o = lambda name: pre(p, "{}{}", name, p)
            iota = KO[:, K_IOTA:K_IOTA + 8]
            D2l = D2[:, 0:80].rearrange("p (a b) -> p a b", a=2)
            v("l7", [n("lgT"), o("ix0."), o("ix1.")], lambda e: e.tensor_copy(LG, D2l[:, :, 0:8]))
            v("l8", [n("l7")], lambda e: e.tensor_tensor(LG, LG, D2l[:, :, 32:40], ALU.add))
            for t in range(2):
                v(f"mx{t}.", [n("l8"), o("d")], lambda e, t=t: e.max(M8[:, t, :], LG[:, t, :]))
                v(f"ix{t}.", [n(f"mx{t}."), o("if")], lambda e, t=t: e.max_index(I8[:, t, :], M8[:, t, :], LG[:, t, :]))
            v("if", [n("ix0."), n("ix1."), o("oh1.1.")], lambda e: e.tensor_copy(IF, I8[:, :, 0:2]))
            v("d", [n("mx0."), n("mx1."), o("e")],
              lambda e: e.tensor_tensor(DW[:, :, 0], M8[:, :, 1], M8[:, :, 0], ALU.subtract))
            op("scalar", n("e"), [n("d"), o("w2"), o("dn")], 95, rk(0.4),
               lambda e: e.activation(DW[:, :, 1], DW[:, :, 0], ACT.Exp))
            v("dn", [n("e"), o("w1")], lambda e: e.tensor_scalar(DW[:, :, 0], DW[:, :, 1], 1.0, None, ALU.add))
            v("w1", [n("dn"), o("w81.")], lambda e: e.reciprocal(DW[:, :, 2], DW[:, :, 0]))
            v("w2", [n("w1"), o("w81.")], lambda e: e.tensor_tensor(DW[:, :, 3], DW[:, :, 1], DW[:, :, 2], ALU.mult))
            v("gt", [n("e"), o("oh0.1."), o("oh1.1.")],
              lambda e: e.tensor_scalar(GT, DW[:, :, 1], 0.0, None, ALU.is_gt))
            for t in range(2):
                v(f"oh{t}.0.", [n("if"), o("pr0.")],
                  lambda e, t=t: e.tensor_scalar(OH[:, 0, t, :], iota, IF[:, t, 0:1], None, ALU.is_equal))
                v(f"oh{t}.1.", [n("if"), n("gt"), o("pr1.")],
                  lambda e, t=t: e.tensor_scalar(OH[:, 1, t, :], iota, IF[:, t, 1:2], GT[:, t:t + 1],
                                                 ALU.is_equal, ALU.mult))
            ohs = [n(f"oh{t}.{j}.") for t in range(2) for j in range(2)]
            v("ob", [*ohs, o("cum")], lambda e: e.tensor_tensor(OHB[:, :, :], OH[:, 0], OH[:, 1], ALU.add))
            for t in range(2):
                w8 = X[:, t, 257:265]
                v(f"wa{t}.", [n(f"oh{t}.0."), n("w1"), *free],
                  lambda e, t=t, w8=w8: e.tensor_scalar(w8, OH[:, 0, t, :], DW[:, t, 2:3], None, ALU.mult))
                v(f"w8{t}.", [n(f"wa{t}."), n(f"oh{t}.1."), n("w2")],
                  lambda e, t=t, w8=w8: e.scalar_tensor_tensor(w8, OH[:, 1, t, :], DW[:, t, 3:4], w8,
                                                               ALU.mult, ALU.add))

            def cum(e):
                m = lambda dst, w, t, a, z: e.matmul(D2[:, 8 * dst:8 * dst + 8], w[:, :], OHB[:, t, :], start=a,
                                                     stop=z, skip_group_check=True)
                m(0, TRI, 0, True, True)
                m(1, ONE, 0, False, False)
                m(1, TRI, 1, False, True)
                m(2, ONE, 0, False, False)
                return m(2, ONE, 1, False, True)
            op("tensor", n("cum"), [n("ob"), "tri", "one", d2_turn(f"cum{b}")], 130, rk(0.5), cum)
            d2(f"cum{b}", [n("pos"), n("run")] + ([n("g8x")] if b == NB - 1 else []))
            v("pos", [n("cum"), o("run"), "run.z", o("pr1."), o("pr0.")], lambda e: e.tensor_tensor(
                V8, D2[:, 0:16].rearrange("p (a b) -> p a b", a=2),
                RUN.unsqueeze(1).to_broadcast([128, 2, 8]), ALU.add), 0.5)
            v("run", [n("pos")], lambda e: e.tensor_tensor(RUN, RUN, D2[:, 16:24], ALU.add), 0.5)
            v("g8", [n("pos"), o("v8")], lambda e: e.scalar_tensor_tensor(
                G8, V8, 1.0 / FAR, KO[:, K_BASE:K_BASE + 16].rearrange("p (a b) -> p a b", a=2),
                ALU.mult, ALU.add), 0.5)
            if b == NB - 1:
                v("g8x", [n("g8"), n("cum")], lambda e: e.scalar_tensor_tensor(
                    G8[:, :, 0:EARLY], D2[:, 0:16].rearrange("p (a b) -> p a b", a=2)[:, :, 0:EARLY], 1.0 / FAR,
                    KO[:, K_LATE:K_LATE + 2 * EARLY].rearrange("p (a b) -> p a b", a=2), ALU.mult, ALU.add), 0.5)
            v("v8", [n("g8"), n("g8x") if b == NB - 1 else None], lambda e: e.scalar_tensor_tensor(V8, V8, float(CAP), G8, ALU.is_gt, ALU.add), 0.5)
            for j in range(2):
                v(f"pr{j}.", [n("v8"), *ohs, o("sl")],
                  lambda e, j=j: e.tensor_tensor(PR[:, j], OH[:, j], V8, ALU.mult), 0.5)
            v("sl", [n("pr0."), n("pr1."), o("sx")],
              lambda e: e.tensor_reduce(SL.rearrange("p a b -> p (a b)"), PR.rearrange("p a b c -> p (a b) c"),
                                        AX.X, ALU.add), 0.5)
            old = [pre(b - 2, "sc{}.{}", b - 2, k) for k in range(4)]
            v("sx", [n("sl"), *old], lambda e: e.tensor_scalar(
                IX[:, s, :], SL.rearrange("p a b -> p (a b)"), FAR, FAR, ALU.mult, ALU.add), 0.5)
            for k in range(4):
                dma("gpsimd", f"sc{b}.{k}", [n("sx"), *n4, n("id"), n("w80."), n("w81."), "pad.z", INIT_OK], f"sc{s}",
                    rk(0.6), lambda e, k=k: e.indirect_dma_start(
                        out=xs, out_offset=bass.IndirectOffsetOnAxis(ap=IX[:, s, k:k + 1], axis=0),
                        in_=X[:, k % 2, :], in_offset=None, bounds_check=xs.shape[0] - 1, oob_is_err=False), cost=1050,
                    kb=136)


        lastq = NI - 1
        l = NB - 1
        S1_DONE = [f"xl{l}.l", f"in{l}.1", f"z{l}.3.3", f"gs{l}.0.l", f"xp{l}", f"scan{l}", f"ys{l}.l", f"out{l}",
                   f"y1{l}", f"n1{l}.x0", f"n1{l}.x1", f"n1{l}.z0", f"n1{l}.z1", f"zT{l}", f"kv{l}.l", f"nc{l}.a0",
                   f"cT{l}", f"kc{l}.l"]
        QKV_DONE = [f"Q{lastq}", f"K{lastq}", f"V{lastq // 2}", f"Vc{lastq // 2}"]
        HEADS_DONE = [*QKV_DONE, f"PV{lastq}", f"PV{lastq - 1}", f"W{lastq}", f"W{lastq - 1}"]
        scattered = lambda *bs: [f"sc{b}.{k}" for b in bs for k in range(4)]
        passes = ([(e, CT, e * CAP) for e in range(E)] + [(e, 2, NT + 256 * e) for e in range(EARLY)])
        NPASS = len(passes)
        ups = lambda k: [f"U{k}.{m}" for m in range(4)]
        downs = lambda k: [f"Y{k}.{t}" for t in range(passes[k][1])]
        adds = lambda k: [f"sa{k}.{t}" for t in range(passes[k][1])] if k >= 0 else []
        u_free = {5: [f"q{lastq}.l", f"vl{lastq // 2}"], 6: [f"k{lastq}.l", f"vcl{lastq // 2}"], 4: [f"y2{l}"],
                  7: [f"run{l}", f"pos{l}", f"g8x{l}"]}
        y_free = {2: [f"o{lastq}.l"], 3: [f"o{lastq}.l"]}
        u_turn = [b for k in range(NPASS) for b in ((5, 6, 4, 5, 6, 4, 5, 6)[4 * k:4 * k + 4] if k < 2 else (5, 6, 4, 5) if k < EARLY else (6, 4, 7, 5))]
        fw_free, fi_free = {}, {}

        def expert(k):
            g, nt, row0 = passes[k]
            s, N, first = k % 2, 128 * nt, k < E
            fw = g if g < EARLY else 3 + g % 2
            X, Y, IH, W1, W2 = XSL[s], YO[s], FI[s], FW1[fw], FW2[fw]
            rk = lambda f: 8 * NB + 10 + 8 * min(k, E) + 3 * max(k - E, 0) + 8 * f
            p, pp = k - 1, k - 2
            if first:
                start = S1_DONE if fw == 0 else QKV_DONE if fw == 1 else HEADS_DONE
                for j, (raw, src, W) in enumerate(((RW1[s], w1[g], W1), (RW2[s], w2[g], W2))):
                    dma("sync", f"ld.f{k}.{j}", [*S1_DONE, pre(pp, "fw{}.{}.l", pp, j)], f"ld.f{s}{j}", rk(-2),
                        lambda e, raw=raw, src=src: e.dma_start(raw, src), kb=512)
                    hi_lo(f"fw{k}.{j}", raw, W[0], W[1], 1024, [f"ld.f{k}.{j}"], rk(-1.2),
                          free=fw_free.get((fw, j), start), lo_on="gpsimd")
                fw_free[fw, 0], fw_free[fw, 1] = ups(k), downs(k)
            f = k if first else g
            lists = scattered(NB - 3, NB - 2) if k < EARLY else scattered(NB - 2, NB - 1)
            dma("sync", f"ld.g{k}", [*lists, *S1_DONE,
                                     pre(pp, "fT{}", pp), pre(pp, "ie{}", pp), pre(pp, "we{}", pp)],
                f"ld.g{s}", rk(-1.5), lambda e: e.dma_start(
                    X[:, 0:nt, :], xs[row0:row0 + N, :].rearrange("(p t) n -> p t n", p=128)), kb=136 * nt)
            op("vector", f"ie{k}", [f"ld.g{k}", *adds(pp)], 90, rk(0),
               lambda e: e.tensor_copy(IE[:, s, 0:nt], X[:, 0:nt, 256]))
            op("vector", f"we{k}", [f"ld.g{k}"] + ([f"yo{pp}.{t}" for t in range(passes[pp][1])] if k > 1 else []),
               90, rk(0), lambda e: e.tensor_copy(WE[:, s, 0:nt], X[:, 0:nt, 257 + g]))

            def ft(e):
                for c in range(2):
                    for t in range(nt):
                        r = e.transpose(SA[c][:, 128 * t:128 * t + 128], X[:, t, 128 * c:128 * c + 128], ident)
                return r
            op("tensor", f"fT{k}", [f"ld.g{k}", pre(p, "fx{}.1.l", p), f"x{lastq}.0", f"x{lastq}.1"], 220 * nt,
               rk(RK["fT"]) if k else rk(0), ft)
            for c in range(2):
                free = QKV_DONE if k < 2 else ups(pp)
                op("scalar", f"fx{k}.{c}.h", [f"fT{k}", *free], ac(N), rk(0.1),
                   lambda e, c=c: e.activation(FX[s][0][:, c, 0:N], SA[c][:, 0:N], ACT.Copy))
                op("vector", f"fx{k}.{c}.l", [f"fx{k}.{c}.h"], tc(N), rk(0.1),
                   lambda e, c=c: e.tensor_tensor(FX[s][1][:, c, 0:N], SA[c][:, 0:N],
                                                  FX[s][0][:, c, 0:N].bitcast(F32), ALU.subtract))
            for m in range(4):
                ub = u_turn[4 * k + m]
                pb = bank(ub)[:, 0:N]

                def up(e, m=m, pb=pb):
                    for c in range(2):
                        r = split3(e, pb, [W1[j][:, c, 128 * m:128 * m + 128] for j in range(2)],
                                   [FX[s][j][:, c, 0:N] for j in range(2)], c == 0, c == 1)
                    return r
                op("tensor", f"U{k}.{m}", [f"fx{k}.0.l", f"fx{k}.1.l", f"fw{f}.0.l", *u_free[ub]], 330 * nt,
                   rk(0.2 + 0.1 * m), up)
                u_free[ub] = [f"i{k}.{m}.l"]
                free = downs(pp) if k > 1 else HEADS_DONE if s else QKV_DONE
                op("scalar", f"i{k}.{m}.h", [f"U{k}.{m}", *free], ac(N), rk(0.2 + 0.1 * m),
                   lambda e, m=m, pb=pb: e.activation(IH[0][:, m, 0:N], pb, ACT.Relu))
                op("vector", f"i{k}.{m}.l", [f"i{k}.{m}.h"], tc(N), rk(0.2 + 0.1 * m),
                   lambda e, m=m, pb=pb: e.scalar_tensor_tensor(IH[1][:, m, 0:N], pb, 0.0,
                                                                IH[0][:, m, 0:N].bitcast(F32), ALU.max, ALU.subtract))
            for t in range(nt):
                yb = 2 + t % 2
                pb = bank(yb)[:, 0:256]

                def down(e, ms, t=t, pb=pb):
                    for m in ms:
                        r = split3(e, pb, [IH[j][:, m, 128 * t:128 * t + 128] for j in range(2)],
                                   [W2[j][:, m, :] for j in range(2)], m == 0, m == 3)
                    return r
                if t == 0:
                    op("tensor", f"Ya{k}", [f"i{k}.{m}.l" for m in range(3)] + [f"fw{f}.1.l", *y_free[yb]], 990,
                       rk(0.6), lambda e, down=down: down(e, range(3)))
                    op("tensor", f"Y{k}.0", [f"i{k}.3.l"], 330, rk(0.6), lambda e, down=down: down(e, [3]))
                    P.after(f"Y{k}.0", f"Ya{k}")
                else:
                    op("tensor", f"Y{k}.{t}", [f"i{k}.{m}.l" for m in range(4)] + [f"fw{f}.1.l", *y_free[yb]], 1320,
                       rk(0.6 + 0.1 * t), lambda e, down=down: down(e, range(4)))
                y_free[yb] = [f"yo{k}.{t}"]
                op("scalar", f"yo{k}.{t}", [f"Y{k}.{t}", f"we{k}", *adds(pp), *S1_DONE],
                   358, rk(0.6 + 0.1 * t), lambda e, t=t, pb=pb: e.activation(
                       Y[:, t, :], pb, ACT.Copy, scale=WE[:, s, t:t + 1]))
                dma("gpsimd", f"sa{k}.{t}", [f"yo{k}.{t}", f"ie{k}", *adds(p), f"st{NB - 1}", f"st{NB - 2}", INIT_OK],
                    f"sa{s}", rk(0.8 + 0.1 * t), lambda e, t=t: e.indirect_dma_start(
                        out=acc, out_offset=bass.IndirectOffsetOnAxis(ap=IE[:, s, t:t + 1], axis=0),
                        in_=Y[:, t, :], in_offset=None, bounds_check=NT + PN - 1, oob_is_err=True,
                        compute_op=ALU.add), cost=1050, kb=128)


        def finish():
            most = [*adds(E - 2), *adds(E - 1)]
            room = [*HEADS_DONE, *scattered(NB - 2, NB - 1), f"st{NB - 1}", f"st{NB - 2}", f"x{lastq}.0", f"x{lastq}.1",
                    f"p{lastq}.0", f"p{lastq}.1", f"y2{NB - 1}", f"n4{NB - 1}.a0", f"n4{NB - 1}.a1"]
            st, mv, rs, nr = tail_stats
            rk = 8 * NB + 8 * NPASS + 40
            on = ("vector", "scalar", "gpsimd", "scalar")
            for n in range(NCH):
                rows = slice(256 * n, 256 * n + 256)
                added = most if n < NB - 1 else [*adds(NPASS - 2), *adds(NPASS - 1)]
                free = room if n < 8 else [f"fw{E - 2 + j}.{i}.l" for i in range(2) for j in range(2)]
                dma("sync", f"ld.a{n}", [*added, *free], f"ld.a{n}", rk + n,
                    lambda e, n=n, rows=rows: e.dma_start(AC[n], acc[rows, :].rearrange("(p t) n -> p t n", p=128)))
                for t in range(2):
                    k = 2 * n + t
                    op("vector", f"f.s{k}", [f"ld.a{n}"], 345, rk + n,
                       lambda e, n=n, t=t, k=k: e.bn_stats(st[:, k, :], AC[n][:, t, :]))
                    op("vector", f"f.m{k}", [f"f.s{k}"], 80, rk + n,
                       lambda e, k=k: e.bn_aggr(mv[:, k, :], st[:, k, :]))
                c = slice(2 * n, 2 * n + 2)
                op("vector", f"f.v{n}", [f"f.m{2 * n + t}" for t in range(2)], 80, rk + n,
                   lambda e, c=c: e.tensor_scalar(rs[:, c], mv[:, c, 1], EPS, None, ALU.add))
                op("gpsimd", f"f.r{n}", [f"f.v{n}", "mh"], 640, rk + n,
                   lambda e, c=c: e.tensor_tensor(rs[:, c], rs[:, c], MH[:, 0:2], ALU.pow))
                op("vector", f"f.n{n}", [f"f.r{n}"], 80, rk + n,
                   lambda e, c=c: e.scalar_tensor_tensor(nr[:, c], mv[:, c, 0], -1.0, rs[:, c], ALU.mult, ALU.mult))
                for t in range(2):
                    k = 2 * n + t
                    g = on[k % 4]
                    a = AC[n][:, t, :]
                    if g == "scalar":
                        f = lambda e, a=a, k=k: e.activation(a, a, ACT.Identity, bias=nr[:, k:k + 1],
                                                             scale=rs[:, k:k + 1])
                    else:
                        f = lambda e, a=a, k=k: e.tensor_scalar(a, a, rs[:, k:k + 1], nr[:, k:k + 1],
                                                                ALU.mult, ALU.add)
                    op(g, f"f.o{k}", [f"f.n{n}"], 490, rk + n, f)
                dma("sync", f"st.o{n}", [f"f.o{2 * n + t}" for t in range(2)], "st.o", rk + n,
                    lambda e, n=n, rows=rows: e.dma_start(out[rows, :].rearrange("(p t) n -> p t n", p=128), AC[n]))
            op("sync", "end", [f"st.o{n}" for n in range(NCH)], 10, rk + 50, lambda e: None)


        def keep_warm(name, waits, dst, n, rank):
            def body(e):
                for _ in range(n):
                    r = e.matmul(dst[:, 0:128], ONE[:, :], ONE[:, :], start=True, stop=True)
                return r
            op("tensor", name, ["one", *waits], 56 * n, rank, body)

        for n, w in enumerate(WARM0):
            keep_warm(f"warm{n}", [w, pre(n - 1, "warm{}", n - 1)], PW, 8, 1e5 + n)

        for b in range(NB):
            stage1(b)
            for h in range(H):
                head(b, h)
            route(b)
        for k in range(NPASS):
            expert(k)
        behind = {
            "gs0.2.l": ["wq0.l", "nc1.s0", "xl1.h"], "z0.3.3": ["ct0.0", "ct0.1"], "xl1.h": ["wk0.h"],
            "scan0": ["xl1.l", "ct1.0", "ct1.1"], "a0": ["wv0.h", "wo0.h"], "gs0.0.l": ["wk0.l"], "nc1.r": ["wk0.l"],
            "out0": ["in1.0"], "n10.rz": ["z1.0.0", "z1.1.0", "z1.2.0", "z1.3.0"], "kv0.l": ["z1.0.1", "z1.1.1"],
            "n10.r": ["wo0.l"],
        }
        for n, names in behind.items():
            for name in names:
                P.after(name, n)
        for j in range(2):
            P.after(f"fw2.{j}.l", f"n4{NB - 1}.r")
            P.after(f"fw2.{j}.h", f"n4{NB - 1}.a1")
            for k in (3, 4):
                P.after(f"fw{k}.{j}.l", f"sc{NB - 1}.3")
                P.after(f"fw{k}.{j}.h", f"e{NB - 1}")
        finish()
        for o in P.ops.values():
            flat = []
            for w in o["waits"]:
                flat += d2_end[w[1]] if isinstance(w, tuple) else [w]
            o["waits"] = flat
        P.sizes = (R.at, F.at)
        P.emit()
        return P



def layout(inputs):
    import numpy as np
    f = lambda n: np.asarray(inputs[n], dtype=np.float32)
    L = {}
    xx = f("x")
    nt = xx.shape[0] * xx.shape[1]
    cap = nt // E
    L["x"] = xx.reshape(nt, 256)
    L["xT"] = xx.reshape(nt, 256).T
    L["ctx_in"] = f("ctx_1024")
    cols = np.zeros((128, C_END), np.float32)
    part = lambda v: v.reshape(-1, 128).T
    cols[:, C_INB:C_INB + 4] = part(f("L0_attn_in_b"))
    cols[:, C_CB:C_CB + 4] = part(f("L0_attn_conv_b"))
    cols[:, C_CW:C_CW + 16] = f("L0_attn_conv_w").reshape(4, 128, 4).transpose(1, 0, 2).reshape(128, 16)
    cols[0:16, C_XPB] = f("L0_attn_xp_b")[0:16]
    cols[32:48, C_XPB] = f("L0_attn_xp_b")[16:32]
    cols[:, C_BQ:C_BQ + 8] = part(f("L0_xattn_bq"))
    cols[:, C_BKV:C_BKV + 16] = part(f("L0_xattn_bkv"))
    cols[:, C_GM:C_GM + 2] = part(f("L0_xattn_gamma_media"))
    cols[:, C_BM:C_BM + 2] = part(f("L0_xattn_beta_media"))
    cols[:, C_GL:C_GL + 2] = part(f("L0_xattn_gamma_lat"))
    cols[:, C_BL:C_BL + 2] = part(f("L0_xattn_beta_lat"))
    cols[:, C_E:C_E + 16] = f("L0_ffn_expert_embeddings").T.reshape(2, 128, 8).transpose(1, 0, 2).reshape(128, 16)
    L["cols"] = cols
    k = np.zeros((128, K_END), np.float32)
    k[:, K_ID:K_ID + 128] = np.eye(128)
    k[:, K_TRI:K_TRI + 128] = np.triu(np.ones((128, 128)))
    k[:, K_IOTA:K_IOTA + 16] = np.tile(np.arange(8), 2)
    k[:, K_BASE:K_BASE + 16] = np.tile((cap * np.arange(8) - 1 - FAR) / FAR, 2)
    k[:, K_TOK:K_TOK + 2] = np.arange(128)[:, None] + 128 * np.arange(2)
    k[:, K_DUMP:K_DUMP + 4] = nt + np.arange(128)[:, None] + 128 * np.arange(4)
    k[:, K_LATE:K_LATE + 2 * EARLY] = np.tile((nt + 256 * np.arange(EARLY) - 1 - FAR) / FAR, 2)
    L["consts"] = k
    c = lambda w: w.reshape(-1, 128, w.shape[-1]).transpose(1, 0, 2)
    L["in_w"] = c(f("L0_attn_in_w").T)
    L["xp_w"] = c(f("L0_attn_xp_w").T)
    L["out_w"] = np.concatenate([f("L0_attn_out_w").T, f("L0_attn_out_b")[None]], 0)
    L["Wq"] = c(f("L0_xattn_Wq"))
    L["Wkv"] = c(f("L0_xattn_Wkv"))
    L["Wo"] = c(f("L0_xattn_Wo"))
    L["bo"] = f("L0_xattn_bo")
    L["w1"] = f("L0_ffn_first_linear").transpose(0, 2, 1).reshape(E, 2, 128, 512).transpose(0, 2, 1, 3)
    L["w2"] = f("L0_ffn_second_linear").transpose(0, 2, 1).reshape(E, 4, 128, 256).transpose(0, 2, 1, 3)
    return {n: np.ascontiguousarray(a) for n, a in L.items()}


_INS = ["x", "xT", "ctx_in", "cols", "consts", "in_w", "xp_w", "out_w", "Wq", "Wkv", "Wo", "bo", "w1", "w2"]


def kernel(**inputs):
    import numpy as _np
    import concourse.bacc as _bacc
    from concourse import mybir as _mybir
    from concourse.bass_utils import run_bass_kernel_spmd as _run

    nc = _bacc.Bacc("TRN2", target_bir_lowering=False, num_devices=1)
    L = layout(inputs)
    arrays, args = {}, []
    for name in _INS:
        a = L[name]
        arrays[f"in_{name}_dram"] = a
        args.append(nc.dram_tensor(f"in_{name}_dram", a.shape, _mybir.dt.from_np(a.dtype), kind="ExternalInput").ap())
    nt = L["x"].shape[0]
    args.append(nc.dram_tensor("out_0_dram", [nt, 256], F32, kind="ExternalOutput").ap())
    decoder_layer(nc, *args)
    r = _run(nc, [arrays], core_ids=[0])
    return _np.asarray(r.results[0]["out_0_dram"]).reshape(nt // 256, 256, 256)
```
